# Optimizing a Trainium2 kernel written in Bass

```python
import numpy as np
import jax
import jax.numpy as jnp

def _softmax(x, axis=-1):
    return jax.nn.softmax(x, axis=axis)

def _gelu(x):
    return jax.nn.gelu(x, approximate=True)

def _silu(x):
    return jax.nn.silu(x)

def _sigmoid(x):
    return jax.nn.sigmoid(x)

def _layernorm(x, axis=-1, eps=1e-05):
    m = jnp.mean(x, axis=axis, keepdims=True)
    v = jnp.var(x, axis=axis, keepdims=True)
    return (x - m) / jnp.sqrt(v + eps)

def _scatter_add(tgt, idx, src, axis=0):
    return tgt.at[idx].add(src)

def _segment_sum(src, seg, n):
    return jax.ops.segment_sum(src, seg, n)
kernel_name = 'mk_gnn_resnorm_d4_gnn_r16_01fff4'

def setup_inputs(seed: int=0):
    np.random.seed(seed)
    _w = jnp.asarray

    def _rec_inputs():
        import jax
        import jax.numpy as jnp
        _gk = jax.random.key(seed)
        x = -0.0001074 + 0.9999 * jax.random.normal(jax.random.fold_in(_gk, 1), (6250, 128), jnp.float32)
        src = jax.random.randint(jax.random.fold_in(_gk, 2), (100000,), 0, 6250, jnp.int32)
        dst = jnp.minimum((6250 * jax.random.uniform(jax.random.fold_in(_gk, 3), (100000,)) ** 2.0).astype(jnp.int32), 99999)
        _o = jnp.argsort(dst, stable=True)
        src = src[_o]
        dst = dst[_o]
        edge_attr_3 = 0.000669165 + 0.999965 * jax.random.normal(jax.random.fold_in(_gk, 11), (100000, 3), jnp.float32)
        edge_weight = jax.random.uniform(jax.random.fold_in(_gk, 13), (100000,), jnp.float32, 0.0, 0.999998)
        return (x, src, dst, edge_attr_3, edge_weight)
    x, src, dst, edge_attr_3, edge_weight = _rec_inputs()

    def _L0_gnn_setup():
        import jax, jax.numpy as jnp
        import numpy as np
        NEG_SLOPE = 0.01

        def leaky(x):
            return jnp.where(x >= 0, x, NEG_SLOPE * x)
        key = jax.random.key(seed)
        ks = jax.random.split(key, 10)
        N, E, IN_DIM, OUT_DIM = (6250, 100000, 128, 128)
        indices = jax.random.randint(ks[0], (2, E), 0, N, dtype=jnp.int64 if jax.config.jax_enable_x64 else jnp.int32)
        features = jax.random.normal(ks[1], (N, IN_DIM), dtype=jnp.float32)
        s = 1.0 / np.sqrt(IN_DIM)
        W_att_w = jax.random.uniform(ks[2], (OUT_DIM, IN_DIM), minval=-s, maxval=s)
        W_att_b = jax.random.uniform(ks[3], (OUT_DIM,), minval=-s, maxval=s)
        W1_w = jax.random.uniform(ks[4], (OUT_DIM, IN_DIM), minval=-s, maxval=s)
        W1_b = jax.random.uniform(ks[5], (OUT_DIM,), minval=-s, maxval=s)
        W2_w = jax.random.uniform(ks[6], (OUT_DIM, OUT_DIM), minval=-s, maxval=s)
        W2_b = jax.random.uniform(ks[7], (OUT_DIM,), minval=-s, maxval=s)
        lim = float(np.sqrt(6.0 / (2 * OUT_DIM + 1)))
        a = jax.random.uniform(ks[8], (2 * OUT_DIM, 1), minval=-lim, maxval=lim)
        return {'indices': indices, 'features': features, 'num_nodes': N, 'W_att_w': W_att_w, 'W_att_b': W_att_b, 'W1_w': W1_w, 'W1_b': W1_b, 'W2_w': W2_w, 'W2_b': W2_b, 'a': a}
    _L0_gnn_all = _L0_gnn_setup()
    _L0_gnn_in = {k: v for k, v in _L0_gnn_all.items() if k in ('W_att_w', 'W_att_b', 'W1_w', 'W1_b', 'W2_w', 'W2_b', 'a')}
    del _L0_gnn_all

    def _L1_gnn_setup():
        import jax, jax.numpy as jnp
        import numpy as np
        N = 3125
        E = 50000
        IN_DIM = 128
        OUT_DIM = 128
        EDGE_DIM = 3
        H = 4
        HD = OUT_DIM // H
        SCALE = HD ** (-0.5)
        key = jax.random.key(seed)
        ks = jax.random.split(key, 10)
        x = jax.random.normal(ks[0], (N, IN_DIM), dtype=jnp.float32)
        edge_index = jax.random.randint(ks[1], (2, E), 0, N, dtype=jnp.int64)
        edge_attr = jax.random.normal(ks[2], (E, EDGE_DIM), dtype=jnp.float32)
        s = 1.0 / np.sqrt(IN_DIM)
        Wq = jax.random.normal(ks[3], (IN_DIM, H * HD), dtype=jnp.float32) * s
        Wk = jax.random.normal(ks[4], (IN_DIM, H * HD), dtype=jnp.float32) * s
        Wv = jax.random.normal(ks[5], (IN_DIM, H * HD), dtype=jnp.float32) * s
        We = jax.random.normal(ks[6], (EDGE_DIM, H), dtype=jnp.float32) * (1.0 / np.sqrt(EDGE_DIM))
        Wo = jax.random.normal(ks[7], (H * HD, OUT_DIM), dtype=jnp.float32) * (1.0 / np.sqrt(H * HD))
        bo = jnp.zeros((OUT_DIM,), dtype=jnp.float32)
        Wm = jax.random.normal(ks[8], (IN_DIM + OUT_DIM, OUT_DIM), dtype=jnp.float32) * (1.0 / np.sqrt(IN_DIM + OUT_DIM))
        bm = jnp.zeros((OUT_DIM,), dtype=jnp.float32)
        return {'x': x, 'edge_index': edge_index, 'edge_attr': edge_attr, 'Wq': Wq, 'Wk': Wk, 'Wv': Wv, 'We': We, 'Wo': Wo, 'bo': bo, 'Wm': Wm, 'bm': bm}
    _L1_gnn_all = _L1_gnn_setup()
    _L1_gnn_in = {k: v for k, v in _L1_gnn_all.items() if k in ('Wq', 'Wk', 'Wv', 'We', 'Wo', 'bo', 'Wm', 'bm')}
    del _L1_gnn_all

    def _L2_gnn_setup():
        import jax, jax.numpy as jnp
        import numpy as np
        N, E, D, EH, HID = (6250, 50000, 128, 64, 128)
        key = jax.random.key(seed)
        ks = jax.random.split(key, 12)
        s = 0.02
        h = jax.random.normal(ks[0], (N, D), dtype=jnp.float32)
        edge_index = jax.random.randint(ks[1], (2, E), 0, N, dtype=jnp.int32)
        We1 = jax.random.normal(ks[2], (2 * D, EH), dtype=jnp.float32) * s
        be1 = jnp.zeros((EH,), dtype=jnp.float32)
        We2 = jax.random.normal(ks[3], (EH, EH), dtype=jnp.float32) * s
        be2 = jnp.zeros((EH,), dtype=jnp.float32)
        Wn1 = jax.random.normal(ks[4], (EH + D, HID), dtype=jnp.float32) * s
        bn1 = jnp.zeros((HID,), dtype=jnp.float32)
        Wn2 = jax.random.normal(ks[5], (HID, D), dtype=jnp.float32) * s
        bn2 = jnp.zeros((D,), dtype=jnp.float32)
        return {'h': h, 'edge_index': edge_index, 'We1': We1, 'be1': be1, 'We2': We2, 'be2': be2, 'Wn1': Wn1, 'bn1': bn1, 'Wn2': Wn2, 'bn2': bn2}
    _L2_gnn_all = _L2_gnn_setup()
    _L2_gnn_in = {k: v for k, v in _L2_gnn_all.items() if k in ('We1', 'be1', 'We2', 'be2', 'Wn1', 'bn1', 'Wn2', 'bn2')}
    del _L2_gnn_all

    def _L3_gnn_setup():
        import jax, jax.numpy as jnp
        import numpy as np
        N = 3125
        E = 50000
        D = 128

        def _gcn_layer(x, row, col, ew, W, b, n):
            deg = jax.ops.segment_sum(ew, col, num_segments=n)
            dis = jnp.where(deg > 0, jax.lax.rsqrt(jnp.maximum(deg, 1e-12)), 0.0)
            norm = dis[row] * ew * dis[col]
            h = x @ W
            msg = h[row] * norm[:, None]
            out = jax.ops.segment_sum(msg, col, num_segments=n)
            return out + b
        key = jax.random.key(seed)
        k1, k2, k3, k4, k5 = jax.random.split(key, 5)
        x = jax.random.normal(k1, (N, D), dtype=jnp.float32)
        edge_index = jax.random.randint(k2, (2, E), 0, N, dtype=jnp.int64)
        edge_weight = jax.random.uniform(k3, (E,), dtype=jnp.float32)
        s = 1.0 / np.sqrt(D)
        W1 = jax.random.uniform(k4, (D, D), minval=-s, maxval=s, dtype=jnp.float32)
        b1 = jnp.zeros((D,), dtype=jnp.float32)
        W2 = jax.random.uniform(k5, (D, D), minval=-s, maxval=s, dtype=jnp.float32)
        b2 = jnp.zeros((D,), dtype=jnp.float32)
        return {'x': x, 'edge_index': edge_index, 'edge_weight': edge_weight, 'W1': W1, 'b1': b1, 'W2': W2, 'b2': b2}
    _L3_gnn_all = _L3_gnn_setup()
    _L3_gnn_in = {k: v for k, v in _L3_gnn_all.items() if k in ('W1', 'b1', 'W2', 'b2')}
    del _L3_gnn_all
    return {'x': x, 'src': src, 'dst': dst, 'edge_attr_3': edge_attr_3, 'edge_weight': edge_weight, 'L0_gnn_W_att_w': _L0_gnn_in['W_att_w'], 'L0_gnn_W_att_b': _L0_gnn_in['W_att_b'], 'L0_gnn_W1_w': _L0_gnn_in['W1_w'], 'L0_gnn_W1_b': _L0_gnn_in['W1_b'], 'L0_gnn_W2_w': _L0_gnn_in['W2_w'], 'L0_gnn_W2_b': _L0_gnn_in['W2_b'], 'L0_gnn_a': _L0_gnn_in['a'], 'L1_gnn_Wq': _L1_gnn_in['Wq'], 'L1_gnn_Wk': _L1_gnn_in['Wk'], 'L1_gnn_Wv': _L1_gnn_in['Wv'], 'L1_gnn_We': _L1_gnn_in['We'], 'L1_gnn_Wo': _L1_gnn_in['Wo'], 'L1_gnn_bo': _L1_gnn_in['bo'], 'L1_gnn_Wm': _L1_gnn_in['Wm'], 'L1_gnn_bm': _L1_gnn_in['bm'], 'L2_gnn_We1': _L2_gnn_in['We1'], 'L2_gnn_be1': _L2_gnn_in['be1'], 'L2_gnn_We2': _L2_gnn_in['We2'], 'L2_gnn_be2': _L2_gnn_in['be2'], 'L2_gnn_Wn1': _L2_gnn_in['Wn1'], 'L2_gnn_bn1': _L2_gnn_in['bn1'], 'L2_gnn_Wn2': _L2_gnn_in['Wn2'], 'L2_gnn_bn2': _L2_gnn_in['bn2'], 'L3_gnn_W1': _L3_gnn_in['W1'], 'L3_gnn_b1': _L3_gnn_in['b1'], 'L3_gnn_W2': _L3_gnn_in['W2'], 'L3_gnn_b2': _L3_gnn_in['b2']}

def reference(x, src, dst, edge_attr_3, edge_weight, L0_gnn_W_att_w, L0_gnn_W_att_b, L0_gnn_W1_w, L0_gnn_W1_b, L0_gnn_W2_w, L0_gnn_W2_b, L0_gnn_a, L1_gnn_Wq, L1_gnn_Wk, L1_gnn_Wv, L1_gnn_We, L1_gnn_Wo, L1_gnn_bo, L1_gnn_Wm, L1_gnn_bm, L2_gnn_We1, L2_gnn_be1, L2_gnn_We2, L2_gnn_be2, L2_gnn_Wn1, L2_gnn_bn1, L2_gnn_Wn2, L2_gnn_bn2, L3_gnn_W1, L3_gnn_b1, L3_gnn_W2, L3_gnn_b2):
    import jax
    import jax.numpy as jnp

    def _L0_gnn_ref(indices, features, num_nodes, W_att_w, W_att_b, W1_w, W1_b, W2_w, W2_b, a):
        import jax, jax.numpy as jnp
        import numpy as np
        NEG_SLOPE = 0.01

        def leaky(x):
            return jnp.where(x >= 0, x, NEG_SLOPE * x)
        src, dst = (indices[0], indices[1])
        out_dim = W_att_w.shape[0]
        h_trans = features @ W_att_w.T + W_att_b
        a_src, a_dst = (a[:out_dim], a[out_dim:])
        logits = leaky(h_trans[src] @ a_src + h_trans[dst] @ a_dst)
        exp_l = jnp.exp(logits)
        denom = jax.ops.segment_sum(exp_l, dst, num_segments=num_nodes)
        alpha = exp_l / (denom[dst] + 1e-09)
        h_msg = features @ W1_w.T + W1_b
        h_neigh = jax.ops.segment_sum(alpha * h_msg[src], dst, num_segments=num_nodes)
        h_self = features
        term1 = h_self + h_neigh
        term2 = h_self * h_neigh @ W2_w.T + W2_b
        return leaky(term1 + term2)

    def _L1_gnn_ref(x, edge_index, edge_attr, Wq, Wk, Wv, We, Wo, bo, Wm, bm):
        import jax, jax.numpy as jnp
        import numpy as np
        N = 3125
        E = 50000
        IN_DIM = 128
        OUT_DIM = 128
        EDGE_DIM = 3
        H = 4
        HD = OUT_DIM // H
        SCALE = HD ** (-0.5)
        n = x.shape[0]
        src = edge_index[0]
        dst = edge_index[1]
        Q = (x @ Wq).reshape(n, H, HD)
        K = (x @ Wk).reshape(n, H, HD)
        V = (x @ Wv).reshape(n, H, HD)
        edge_bias = edge_attr @ We
        attn = jnp.sum(Q[dst] * K[src], axis=-1) * SCALE + edge_bias
        attn = jnp.where(attn >= 0, attn, 0.2 * attn)
        attn_exp = jnp.exp(attn - jnp.max(attn))
        attn_sum = jax.ops.segment_sum(attn_exp, dst, num_segments=n)
        attn_norm = attn_exp / jnp.maximum(attn_sum[dst], 1e-12)
        weighted_V = V[src] * attn_norm[:, :, None]
        agg = jax.ops.segment_sum(weighted_V, dst, num_segments=n)
        agg = agg.reshape(n, H * HD) @ Wo + bo
        h = jnp.concatenate([x, agg], axis=1) @ Wm + bm
        return jax.nn.relu(h)

    def _L2_gnn_ref(h, edge_index, We1, be1, We2, be2, Wn1, bn1, Wn2, bn2):
        import jax, jax.numpy as jnp
        import numpy as np
        N, E, D, EH, HID = (6250, 50000, 128, 64, 128)
        row, col = (edge_index[0], edge_index[1])
        e = jnp.concatenate([h[row], h[col]], axis=1)
        e = jax.nn.silu(e @ We1 + be1)
        e = jax.nn.silu(e @ We2 + be2)
        agg = jax.ops.segment_sum(e, row, num_segments=h.shape[0])
        a = jnp.concatenate([h, agg], axis=1)
        out = jax.nn.silu(a @ Wn1 + bn1) @ Wn2 + bn2
        return h + out

    def _L3_gnn_ref(x, edge_index, edge_weight, W1, b1, W2, b2):
        import jax, jax.numpy as jnp
        import numpy as np
        N = 3125
        E = 50000
        D = 128

        def _gcn_layer(x, row, col, ew, W, b, n):
            deg = jax.ops.segment_sum(ew, col, num_segments=n)
            dis = jnp.where(deg > 0, jax.lax.rsqrt(jnp.maximum(deg, 1e-12)), 0.0)
            norm = dis[row] * ew * dis[col]
            h = x @ W
            msg = h[row] * norm[:, None]
            out = jax.ops.segment_sum(msg, col, num_segments=n)
            return out + b
        n = x.shape[0]
        loop = jnp.arange(n, dtype=edge_index.dtype)
        row = jnp.concatenate([edge_index[0], loop])
        col = jnp.concatenate([edge_index[1], loop])
        ew = jnp.concatenate([edge_weight, jnp.ones((n,), dtype=edge_weight.dtype)])
        h = _gcn_layer(x, row, col, ew, W1, b1, n)
        h = jax.nn.relu(h)
        out = _gcn_layer(h, row, col, ew, W2, b2, n)
        return out
    edge_index = jnp.stack([src, dst])
    x = _layernorm(x + _L0_gnn_ref(edge_index, x, 6250, L0_gnn_W_att_w, L0_gnn_W_att_b, L0_gnn_W1_w, L0_gnn_W1_b, L0_gnn_W2_w, L0_gnn_W2_b, L0_gnn_a), axis=-1)
    x = _layernorm(x + _L1_gnn_ref(x, edge_index, edge_attr_3, L1_gnn_Wq, L1_gnn_Wk, L1_gnn_Wv, L1_gnn_We, L1_gnn_Wo, L1_gnn_bo, L1_gnn_Wm, L1_gnn_bm), axis=-1)
    x = _layernorm(x + _L2_gnn_ref(x, edge_index, L2_gnn_We1, L2_gnn_be1, L2_gnn_We2, L2_gnn_be2, L2_gnn_Wn1, L2_gnn_bn1, L2_gnn_Wn2, L2_gnn_bn2), axis=-1)
    x = _layernorm(x + _L3_gnn_ref(x, edge_index, edge_weight, L3_gnn_W1, L3_gnn_b1, L3_gnn_W2, L3_gnn_b2), axis=-1)
    return x

_drawn_inputs = setup_inputs


def setup_inputs(seed=0):
    import zlib

    import numpy as np

    out = dict(_drawn_inputs(seed))
    spreads = {'L1_gnn_bo': (0.0, 0.1),
     'L1_gnn_bm': (0.0, 0.1),
     'L2_gnn_be1': (0.0, 0.8),
     'L2_gnn_be2': (0.0, 0.8),
     'L2_gnn_bn1': (0.0, 0.8),
     'L2_gnn_bn2': (0.0, 0.441),
     'L3_gnn_b1': (0.0, 0.1),
     'L3_gnn_b2': (0.0, 0.1)}
    factors = {'edge_weight': 9.486,
     'L0_gnn_W_att_b': 64.0,
     'L2_gnn_We1': 8.0,
     'L2_gnn_We2': 8.0,
     'L2_gnn_Wn1': 3.556,
     'L2_gnn_Wn2': 3.226,
     'L0_gnn_W_att_w': 3.043,
     'L0_gnn_W2_b': 2.761,
     'L0_gnn_a': 2.733}
    for name, (base, spread) in spreads.items():
        noise = np.random.default_rng([zlib.crc32(name.encode()), seed]).standard_normal(out[name].shape)
        drawn = base * np.exp(spread * noise) if base else spread * noise
        out[name] = jnp.asarray(drawn.astype(out[name].dtype))
    for name, factor in factors.items():
        out[name] = (out[name] * factor).astype(out[name].dtype)
    return out
```

```python
import concourse.bass as bass
from concourse import mybir
from contextlib import ExitStack

F32 = mybir.dt.float32
BF16 = mybir.dt.bfloat16
I32 = mybir.dt.int32
U32 = mybir.dt.uint32
ALU = mybir.AluOpType
ACT = mybir.ActivationFunctionType
AX = mybir.AxisListType

P = 128
D = 128
N, E = 6250, 100000
ET = -(-E // P)
BT = 4
NT = -(-N // (P * BT)) * BT
NB = NT // BT
NP = NT * P
G = 4
RING = 4
USED = -(-N // P)
STEPS = -(-(ET + USED - 1) // (G * RING)) * G * RING
GROUPS = STEPS // G
ITERS = GROUPS // RING
SB = -(-STEPS // P)
COLS = SB * P
AW = 132
H, HD = 4, 32
EH = 64
PAD_DST = 1 << 20
FAR = 8192
SCALE = float(HD) ** -0.5
EPS = 1e-5
BIG = 1e30


class Chain:

    def __init__(self, eng, sem, base=0):
        self.eng, self.sem, self.base, self.n = eng, sem, base, 0

    def __call__(self, instruction):
        self.n += 1
        return instruction.then_inc(self.sem, 1)

    def wait(self):
        self.eng.wait_ge(self.sem, self.base + self.n)


def edge_rounds(eng, body):
    for g in range(RING):
        body(0, g, g, RING)
    with eng.Fori(1, ITERS - 1) as i:
        for g in range(RING):
            body(i, g, RING, RING)
    for g in range(RING):
        body(ITERS - 1, g, RING, RING - 1 - g)


def later(i, g, by):
    return i + (g + by) // RING, (g + by) % RING


def build(nc, x, edge_i, edge_f, W_att_w, W_att_b, W1_w, W1_b, W2_w, W2_b, a_vec,
          Wq, Wk, Wv, We, Wo, bo, Wm, bm, We1, be1, We2, be2, Wn1, bn1, Wn2, bn2,
          G1, g1b, G2, g2b, out):
    ctx = ExitStack()
    with ctx:
        def sb(name, shape, dt=F32):
            return ctx.enter_context(nc.sbuf_tensor(name, shape, dt))

        early, early_sems = ExitStack(), []

        def sem(name, early_only=True):
            if early_only and early_sems is not None:
                early_sems.append(early.enter_context(nc.semaphore(name)))
                return early_sems[-1]
            return ctx.enter_context(nc.semaphore(name))

        def dram(name, shape):
            return nc.dram_tensor(name, shape, F32, kind="Internal").ap()

        t0 = dram("table_attention", [NP, AW])
        t1 = dram("table_key_value", [NP, 2 * D])
        t2 = dram("table_edge_mlp", [NP, EH])
        t3 = dram("table_gcn1", [NP, D])
        t4 = dram("table_gcn2", [NP, D])
        mlp_sum = [dram(f"mlp_sum{u}", [NP + P, EH]) for u in range(G)]
        step_node_dram = nc.dram_tensor("step_node_dram", [COLS], I32, kind="Internal").ap()

        xs = sb("x_nodes", [P, NT, D])
        acc = sb("acc", [P, NT, AW])
        tab = sb("tab", [P, NT, AW])
        look = sb("look", [P, NT, 3 * D], BF16)
        dst_score = look[:, 0:NT, :].rearrange("p t c -> p (t c)").bitcast(F32)[:, 0:NP]
        dis = sb("dis", [P, NT])
        neg_max = sb("neg_max", [P, NT + G - 1])
        src_i = sb("src_i", [P, COLS], I32)
        rel = sb("rel", [P, COLS])
        ew = sb("ew", [P, COLS])
        key = sb("key", [P, COLS])
        step_node = sb("step_node", [1, COLS], I32)
        ring = sb("ring", [P, RING * G, 2 * D])
        idx_now = sb("idx_now", [P, RING * G], I32)
        rel_now = sb("rel_now", [P, RING * G])
        ew_now = sb("ew_now", [P, RING * G])
        key_now = sb("key_now", [P, RING * G])
        bias_now = sb("bias_now", [P, RING, G * H])
        hot = sb("hot", [P, RING, G, P], BF16)
        hotf = sb("hotf", [P, RING, G, P])
        hotT = sb("hotT", [P, RING, G * P], BF16)
        wide = sb("wide", [P, RING, G, AW])
        lg = sb("lg", [P, RING, 2, G * H])
        small = sb("small", [P, RING, 8 * G])
        junk = sb("junk", [P, 2, G * D])
        put_i = sb("put_i", [P, RING, G], I32)
        iota_i = sb("iota_i", [P, P], I32)
        iota = sb("iota", [P, P])
        iota_b = sb("iota_b", [P, P], BF16)
        ident = sb("ident", [P, P])
        ident_b = sb("ident_b", [P, P], BF16)
        tri = sb("tri", [P, P])
        part_i = sb("part_i", [P, SB], I32)
        part = sb("part", [P, SB])
        far = sb("far", [P, 2])
        ones = sb("ones", [P, P])
        eps = sb("eps", [P, 1])
        w_in = sb("w_in", [P, 3, D])
        a2 = sb("a2", [P, 2])
        ab = sb("ab", [P, 1])
        w0 = sb("w0", [P, AW])
        wad = sb("wad", [P, 4])
        b0 = sb("b0", [P, AW])
        w2T = sb("w2T", [P, D])
        b2 = sb("b2", [P, D])
        wkv = sb("wkv", [P, 2 * D])
        wq = sb("wq", [P, D])
        web = sb("web", [P, 3 * H])
        wo = sb("wo", [P, D])
        boc = sb("boc", [P, 1])
        wm = sb("wm", [P, 2, D])
        bmb = sb("bmb", [P, D])
        we1 = sb("we1", [P, 2, EH])
        be1b = sb("be1b", [P, EH])
        we2 = sb("we2", [EH + 1, EH])
        wn1 = sb("wn1", [P, 2, D])
        bn1c = sb("bn1c", [P, 1])
        wn2 = sb("wn2", [P, D])
        bn2b = sb("bn2b", [P, D])
        wg1 = sb("wg1", [P, D])
        wg2 = sb("wg2", [P, D])
        bg1 = sb("bg1", [P, D])
        bg2 = sb("bg2", [P, D])
        ringf = ring[:, :, :].rearrange("p a b -> p (a b)")
        tA, tB, tC, tX, tN, tY = (ringf[:, n * BT * D:(n + 1) * BT * D].rearrange("p (t d) -> p t d", t=BT) for n in range(6))
        tT0 = ringf[:, 6 * BT * D:6 * BT * D + BT * AW].rearrange("p (t c) -> p t c", t=BT)
        tT2 = ringf[:, 6 * BT * D:6 * BT * D + BT * EH].rearrange("p (t c) -> p t c", t=BT)
        tS = ringf[:, 6 * BT * D:6 * BT * D + G * BT * EH].rearrange("p (u t f) -> p u t f", u=G, t=BT)
        tKV = ringf[:, 6 * BT * D:8 * BT * D].rearrange("p (t d) -> p t d", t=BT)
        rT = hotf[:, 0:3, :, :].rearrange("p a b c -> p a (b c)")
        stat = sb("stat", [P, BT, 8])
        mv = sb("mv", [P, BT, 2])
        rs = sb("rs", [P, NT, 2 * H])
        top = sb("top", [1, 4])
        kv_row = ew[0:1, 0:ET]
        last_i = key[0:1, 0:ET].bitcast(I32)
        tabf = tab[:, :, :].rearrange("p t c -> p (t c)")
        got_f = tabf[:, 0:SB * 4 * P].rearrange("p (b c) -> p b c", b=SB)
        lookf = look[:, :, :].rearrange("p t c -> p (t c)").bitcast(F32)
        got_if = lookf[:, COLS:COLS + SB * 2 * P].rearrange("p (b c) -> p b c", b=SB)
        got_i = tabf[:, SB * 4 * P:SB * 6 * P].bitcast(I32).rearrange("p (b c) -> p b c", b=SB)
        bias = tabf[:, 0:COLS * H].rearrange("p (s h) -> p s h", h=H)
        accf = acc[:, :, :].rearrange("p t c -> p (t c)")
        keys = accf[:, 0:ET]
        one_row = accf[:, ET:2 * ET]
        attr = [accf[:, 2 * ET + c * COLS:2 * ET + (c + 1) * COLS] for c in range(3)]
        src_f = accf[:, 2 * ET + 3 * COLS:2 * ET + 4 * COLS]
        ok_row = lookf[:, 0:COLS]

        bank = [ctx.enter_context(nc.psum_tensor(f"bank{n}", [P, 512], F32)) for n in range(8)]

        rounds = sem("gather_rounds", False)
        gathered = [sem(f"gathered{g}", False) for g in range(RING)]
        scattered = [sem(f"scattered{u}", False) for u in range(G)]
        gcount = [0]

        v, s_, t_, q_ = nc.vector, nc.scalar, nc.tensor, nc.gpsimd

        loaded_dst, loaded_w, loaded_x = sem("loaded_dst"), sem("loaded_w"), sem("loaded_x")
        iota_made, const_made = sem("iota_made"), sem("const_made")
        prep_v = sem("prep_vector")
        node_out, steps_got, keys_done, tiles_done = sem("node_out"), sem("steps_got"), sem("keys_done"), sem("tiles_done")
        rows_ready, rows_T, rows_kept = sem("rows_ready"), sem("rows_T"), sem("rows_kept")
        w_T, zero_made, node_in = sem("w_T"), sem("zero_made"), sem("node_in")
        tile_row_done, keys_T = sem("tile_row_done"), sem("keys_T")

        NW = [0]
        with nc.Block() as block:
            @block.sync
            def _(sp):
                with nc.allow_non_contiguous_dma(reason="last dst of each tile, columns of biases"):
                    sp.dma_start(last_i[:, :], edge_i[:, 2 * P - 1:2 * P].rearrange("t one -> one t")).then_inc(loaded_dst, 16)

                    def w(dst, src):
                        NW[0] += 16
                        sp.dma_start(dst, src).then_inc(loaded_w, 16)

                    def row(dst, vec):
                        w(dst, vec.partition_broadcast(P))

                    w(w_in[:, 0, :], W_att_w)
                    w(w_in[:, 1, :], W1_w)
                    w(w_in[:, 2, :], W2_w)
                    w(a2[:, :], a_vec.rearrange("(c o) one -> o (c one)", c=2))
                    w(ab[:, :], W_att_b.rearrange("(o one) -> o one", one=1))
                    row(b0[:, 0:D], W1_b)
                    row(b2[:, :], W2_b)
                    w(wkv[:, 0:D], Wk)
                    w(wkv[:, D:2 * D], Wv)
                    w(wq[:, :], Wq)
                    row(web[:, :], We.rearrange("c h -> (c h)"))
                    w(wo[:, :], Wo)
                    w(boc[:, :], bo.rearrange("(o one) -> o one", one=1))
                    w(wm[:, :, :], Wm.rearrange("(c p) o -> p c o", p=P))
                    row(bmb[:, :], bm)
                    w(we1[:, :, :], We1.rearrange("(c p) o -> p c o", p=P))
                    row(be1b[:, :], be1)
                    w(we2[0:EH, :], We2)
                    w(we2[EH:EH + 1, :], be2.rearrange("(one o) -> one o", one=1))
                    w(wn1[:, 0, :], Wn1[0:D, :])
                    w(wn1[0:EH, 1, :], Wn1[D:D + EH, :])
                    w(bn1c[:, :], bn1.rearrange("(o one) -> o one", one=1))
                    w(wn2[:, :], Wn2)
                    row(bn2b[:, :], bn2)
                    w(wg1[:, :], G1)
                    w(wg2[:, :], G2)
                    row(bg1[:, :], g1b)
                    row(bg2[:, :], g2b)
                    sp.dma_start(xs[:, :, :], x.rearrange("(t p) d -> p t d", p=P)).then_inc(loaded_x, 16)
                    sp.wait_ge(tiles_done, 1)
                    sp.dma_start(step_node_dram.rearrange("(b p) -> p b", p=P), part_i[:, :]).then_inc(node_out, 16)
                    sp.wait_ge(node_out, 16)
                    sp.dma_start(step_node[:, :], step_node_dram.rearrange("(one s) -> one s", one=1)).then_inc(node_in, 16)
                sp.wait_ge(loaded_x, 16)
                sp.wait_ge(loaded_w, NW[0])
                sp.wait_ge(node_in, 16)

            @block.gpsimd
            def _(pool):
                q_.iota(iota_i[:, :], pattern=[[1, P]], base=0, channel_multiplier=0).then_inc(iota_made, 1)
                q_.iota(part_i[:, :], pattern=[[P, SB]], base=0, channel_multiplier=1).then_inc(iota_made, 1)
                q_.iota(src_i[0:1, 0:ET], pattern=[[1, ET]], base=0, channel_multiplier=0).then_inc(iota_made, 1)
                q_.memset(ident[:, :], 0.0).then_inc(iota_made, 1)
                pool.wait_ge(iota_made, 4)
                q_.affine_select(out=ident[:, :], in_=ident[:, :], compare_op=ALU.not_equal, fill=1.0,
                                 base=0, pattern=[[-1, P]], channel_multiplier=1).then_inc(const_made, 1)
                q_.memset(ring[:, :, :], 0.0).then_inc(zero_made, 1)
                pool.wait_ge(zero_made, 1)
                zeros = ring[:, :, :].rearrange("p a b -> p (a b)")[:, 0:(NT + 1) * EH].rearrange("p (t f) -> p t f", f=EH)
                for u in range(G):
                    pool.dma_start(mlp_sum[u].rearrange("(t p) f -> p t f", p=P), zeros).then_inc(scattered[u], 16)
                pool.wait_ge(keys_done, 1)
                for b in range(SB):
                    at = bass.IndirectOffsetOnAxis(ap=put_i[:, :, :].rearrange("p a b -> p (a b)")[:, b:b + 1].bitcast(U32), axis=0)
                    q_.indirect_dma_start(got_i[:, b, :], None, edge_i, at).then_inc(steps_got, 16)
                    q_.indirect_dma_start(got_f[:, b, :], None, edge_f, at).then_inc(steps_got, 16)
                for u in range(G):
                    pool.wait_ge(scattered[u], 16)

            @block.vector
            def _(dve):
                ch = Chain(dve, prep_v)
                dve.wait_ge(iota_made, 3)
                ch(v.tensor_copy(iota[:, :], iota_i[:, :]))
                ch(v.tensor_copy(part[:, :], part_i[:, :]))
                ch(v.memset(ones[:, :], 1.0))
                ch(v.memset(eps[:, :], EPS))
                ch(v.memset(one_row[:, :], 1.0))
                ch(v.tensor_copy(kv_row[:, :], src_i[0:1, 0:ET]))
                dve.wait_ge(loaded_dst, 16)
                ch(v.tensor_scalar(out=last_i[:, :], in0=last_i[:, :], scalar1=7, scalar2=None, op0=ALU.logical_shift_right))
                ch.wait()
                ch(v.tensor_copy(junk[0:1, :, :].rearrange("p a b -> p (a b)")[:, 0:ET], last_i[:, :]))
                ch(v.tensor_copy(iota_b[:, :], iota[:, :]))
                ch.wait()
                ch(v.tensor_scalar(out=tri[:, :], in0=iota[:, :], scalar1=part[:, 0:1], scalar2=None, op0=ALU.is_lt))
                ch(v.tensor_scalar(out=far[:, 0:1], in0=part[:, 0:1], scalar1=float(FAR), scalar2=None, op0=ALU.add))
                ch(v.tensor_scalar(out=far[:, 1:2], in0=part[:, 0:1], scalar1=float(NP), scalar2=None, op0=ALU.add))
                v.tensor_add(kv_row[:, :], kv_row[:, :], junk[0:1, :, :].rearrange("p a b -> p (a b)")[:, 0:ET]).then_inc(tile_row_done, 1)
                dve.wait_ge(const_made, 1)
                ch(v.tensor_copy(ident_b[:, :], ident[:, :]))
                dve.wait_ge(keys_T, 1)
                ch(v.tensor_copy(keys[:, 0:512], bank[0][:, 0:512]))
                ch(v.tensor_copy(keys[:, 512:ET], bank[1][:, 0:ET - 512]))
                ch.wait()
                for b in range(SB):
                    ch(v.scalar_tensor_tensor(out=tabf[:, b * ET:(b + 1) * ET], in0=keys[:, :], scalar=part[:, b:b + 1],
                                              in1=one_row[:, :], op0=ALU.is_lt, op1=ALU.mult,
                                              accum_out=small[:, 0, b:b + 1]))
                ch.wait()
                ch(v.tensor_scalar(out=small[:, 1, 0:SB], in0=small[:, 0, 0:SB], scalar1=float(ET - 1), scalar2=None, op0=ALU.min))
                ch.wait()
                v.tensor_copy(put_i[:, :, :].rearrange("p a b -> p (a b)")[:, 0:SB], small[:, 1, 0:SB]).then_inc(keys_done, 1)
                ch(v.tensor_sub(small[:, 2, 0:SB], part[:, :], small[:, 1, 0:SB]))
                ch.wait()
                ch(v.tensor_scalar(out=small[:, 0, 0:SB], in0=small[:, 2, 0:SB], scalar1=float(NT - 1), scalar2=None, op0=ALU.min))
                ch.wait()
                v.tensor_copy(part_i[:, :], small[:, 0, 0:SB]).then_inc(tiles_done, 1)
                ch(v.tensor_scalar(out=small[:, 3, 0:SB], in0=small[:, 2, 0:SB], scalar1=float(P), scalar2=None, op0=ALU.mult))
                dve.wait_ge(steps_got, 32 * SB)
                ch(v.tensor_copy(got_if, got_i))
                ch.wait()
                for b in range(SB):
                    last = v.tensor_scalar(out=got_if[:, b, P:2 * P], in0=got_if[:, b, P:2 * P],
                                           scalar1=small[:, 3, b:b + 1], scalar2=None, op0=ALU.subtract)
                last.then_inc(rows_ready, 1)
                for b in range(SB):
                    at = slice(b * P, (b + 1) * P)
                    dve.wait_ge(rows_T, b + 1)
                    c0, c1 = bank[2 * (b % 2)], bank[2 * (b % 2) + 1]
                    ch(v.tensor_copy(src_f[:, at], c0[:, 0:P]))
                    ch(v.tensor_copy(rel[:, at], c0[:, P:2 * P]))
                    ch(v.tensor_copy(ew[:, at], c0[:, 2 * P:3 * P]))
                    ch(v.tensor_copy(attr[0][:, at], c0[:, 3 * P:4 * P]))
                    ch(v.tensor_copy(attr[1][:, at], c1[:, 0:P]))
                    v.tensor_copy(attr[2][:, at], c1[:, P:2 * P]).then_inc(rows_kept, 1)
                dve.wait_ge(rows_kept, SB)
                ch.wait()
                ch(v.tensor_copy(src_i[:, :], src_f))
                ch(v.tensor_scalar(out=ok_row, in0=rel[:, :], scalar1=0.0, scalar2=None, op0=ALU.is_ge))
                ch.wait()
                ch(v.scalar_tensor_tensor(out=ok_row, in0=rel[:, :], scalar=float(P), in1=ok_row, op0=ALU.is_lt, op1=ALU.mult))
                ch.wait()
                ch(v.scalar_tensor_tensor(out=key[:, :], in0=src_f, scalar=far[:, 0:1], in1=ok_row, op0=ALU.subtract, op1=ALU.mult))
                ch.wait()
                ch(v.tensor_scalar(out=key[:, :], in0=key[:, :], scalar1=far[:, 0:1], scalar2=None, op0=ALU.add))
                ch(v.tensor_scalar(out=ok_row, in0=ok_row, scalar1=-1.0, scalar2=BIG, op0=ALU.add, op1=ALU.mult))
                dve.wait_ge(loaded_w, NW[0])
                for h in range(H):
                    ch.wait()
                    ch(v.scalar_tensor_tensor(out=bias[:, :, h], in0=attr[0], scalar=web[:, h:h + 1], in1=ok_row, op0=ALU.mult, op1=ALU.add))
                for c in (1, 2):
                    for h in range(H):
                        ch.wait()
                        ch(v.scalar_tensor_tensor(out=bias[:, :, h], in0=attr[c], scalar=web[:, c * H + h:c * H + h + 1],
                                                  in1=bias[:, :, h], op0=ALU.mult, op1=ALU.add))
                ch(v.memset(neg_max[:, :], BIG))
                ch(v.memset(top[:, :], -BIG))
                ch.wait()
                ch(v.memset(acc[:, :, :], 0.0))
                ch(v.memset(b0[:, D:D + 1], 1.0))
                ch(v.memset(b0[:, D + 2:AW], 0.0))
                ch(v.memset(w0[:, D:AW], 0.0))
                ch.wait()
                dve.wait_ge(w_T, 1)
                ch(v.tensor_copy(w0[:, 0:D], bank[4][:, 0:D]))
                ch(v.tensor_copy(w2T[:, :], bank[4][:, D:2 * D]))
                ch(v.tensor_copy(w0[:, D + 1:D + 2], bank[5][:, 0:1]))
                ch(v.tensor_copy(wad[:, 0:1], bank[5][:, 1:2]))
                ch(v.tensor_copy(b0[:, D + 1:D + 2], bank[5][:, 2:3]))
                ch(v.tensor_copy(wad[:, 1:2], bank[5][:, 3:4]))
                ch.wait()

            @block.tensor
            def _(pe):
                pe.wait_ge(tile_row_done, 1)
                t_.matmul(bank[0][:, 0:512], ones[0:1, :], kv_row[:, 0:512], start=True, stop=True)
                t_.matmul(bank[1][:, 0:ET - 512], ones[0:1, :], kv_row[:, 512:ET], start=True, stop=True).then_inc(keys_T, 1)
                pe.wait_ge(const_made, 1)
                pe.wait_ge(loaded_w, NW[0])
                t_.transpose(bank[4][:, 0:D], w_in[:, 1, :], ident[:, :])
                t_.transpose(bank[4][:, D:2 * D], w_in[:, 2, :], ident[:, :])
                t_.matmul(bank[5][:, 0:2], w_in[:, 0, :], a2[:, :], start=True, stop=True)
                t_.matmul(bank[5][:, 2:4], ab[:, 0:1].to_broadcast([P, P]), a2[:, :], start=True, stop=True).then_inc(w_T, 1)
                pe.wait_ge(rows_ready, 1)
                for b in range(SB):
                    if b >= 2:
                        pe.wait_ge(rows_kept, b - 1)
                    c0, c1 = bank[2 * (b % 2)], bank[2 * (b % 2) + 1]
                    t_.transpose(c0[:, 0:P], got_if[:, b, 0:P], ident[:, :])
                    t_.transpose(c0[:, P:2 * P], got_if[:, b, P:2 * P], ident[:, :])
                    t_.transpose(c0[:, 2 * P:3 * P], got_f[:, b, 0:P], ident[:, :])
                    t_.transpose(c0[:, 3 * P:4 * P], got_f[:, b, P:2 * P], ident[:, :])
                    t_.transpose(c1[:, 0:P], got_f[:, b, 2 * P:3 * P], ident[:, :])
                    t_.transpose(c1[:, P:2 * P], got_f[:, b, 3 * P:4 * P], ident[:, :]).then_inc(rows_T, 1)

        def tiles(b):
            return bass.ds(b * BT, BT)

        def flat(a):
            return a.rearrange("p a b -> p (a b)")

        def arrived(eng, i, g):
            eng.wait_ge(gathered[g], 16 * G * (gcount[0] + i + 1))

        def place(k, g, placed, *columns):
            for now, every in columns + ((idx_now, src_i),):
                last = s_.copy(now[:, g * G:(g + 1) * G], every[:, bass.ds(k * G, G)])
            last.then_inc(placed, 1)

        def gather(pool, k, g, table, width, placed, table_out):
            pool.wait_ge(table_out, 16 * NB)
            pool.wait_ge(placed, k + 1)
            pool.sem_inc(rounds, 1)
            for u in range(G):
                slot = g * G + u
                q_.indirect_dma_start(ring[:, slot, 0:width], None, table, bass.IndirectOffsetOnAxis(
                    ap=idx_now[:, slot:slot + 1].bitcast(U32), axis=0)).then_inc(gathered[g], 16)

        def node_regs(eng, name):
            return [[eng.alloc_register(f"{name}{j}{u}") for u in range(G)] for j in range(2)]

        def load_nodes(eng, regs, k, g):
            eng.reg_load(regs[g % 2], step_node[0:1, bass.ds(k * G, G)])

        def nodes_of(eng, regs, g):
            return [eng.snap(r, min_val=0, max_val=NT - 1) for r in regs[g % 2]]

        def hots(g):
            return dict(in0=iota[:, :].unsqueeze(1).to_broadcast([P, G, P]),
                        in1=rel_now[:, g * G:(g + 1) * G].unsqueeze(2).to_broadcast([P, G, P]), op=ALU.is_equal)

        def layer_norm(ch, b, y, outs, var, std):
            ch.wait()
            for u in range(BT):
                ch(v.bn_stats(out=stat[:, u, 0:6], in_=y[:, u, :]))
            ch.wait()
            ch.eng.sem_inc(rounds, 1)
            for u in range(BT):
                last = v.bn_aggr(out=mv[:, u, :], in_=stat[:, u, 0:6])
            last.then_inc(var, 1)
            ch.eng.wait_ge(std, b + 1)
            ch(v.reciprocal(stat[:, :, 6], stat[:, :, 6]))
            ch.wait()
            return [v.tensor_scalar(out=outs[u], in0=y[:, u, :], scalar1=mv[:, u, 0:1], scalar2=stat[:, u, 6:7],
                                    op0=ALU.subtract, op1=ALU.mult) for u in range(BT)]

        def root(act, b, var, std):
            act.wait_ge(var, b + 1)
            s_.activation(stat[:, :, 6], mv[:, :, 1], ACT.Sqrt, bias=eps[:, 0:1]).then_inc(std, 1)

        def split3(ch, src, dst):
            ch.wait()
            for c in range(3):
                ch(v.tensor_copy(dst(c), src))
                ch.wait()
                if c < 2:
                    ch(v.tensor_sub(src, src, dst(c)))
                    ch.wait()

        x_staged, x_T, xT_kept, t0_mm, t0_kept, score_mm, t0_out, t0_free = (
            sem(f"n0_{n}") for n in ("x_staged", "x_T", "xT_kept", "t0_mm", "t0_kept", "score_mm", "t0_out", "t0_free"))
        with nc.Block() as block:
            @block.gpsimd
            def _(pool):
                pool.sem_inc(x_T, 1)
                with pool.Fori(0, NB) as b:
                    pool.wait_ge(x_T, b + 1)
                    pool.sem_inc(rounds, 1)
                    q_.tensor_copy(tX[:, :, :], xs[:, tiles(b), :]).then_inc(x_staged, 1)

            @block.tensor
            def _(pe):
                with pe.Fori(0, NB) as b:
                    pe.wait_ge(x_staged, b + 1)
                    for u in range(BT):
                        last = t_.transpose(bank[0][:, u * P:(u + 1) * P], tX[:, u, :], ident[:, :])
                    last.then_inc(x_T, 1)
                    pe.wait_ge(xT_kept, b + 1)
                    pe.wait_ge(t0_kept, b + 1)
                    for u in range(BT):
                        last = t_.matmul(bank[1 + u // 2][:, (u % 2) * AW:(u % 2 + 1) * AW],
                                         rT[:, 0, u * P:(u + 1) * P], w0[:, :], start=True, stop=True)
                    last.then_inc(t0_mm, 1)
                    t_.matmul(bank[3][:, :], wad[:, 0:1].to_broadcast([P, P]), rT[:, 0, :], start=True, stop=True).then_inc(score_mm, 1)

            @block.scalar
            def _(act):
                with act.Fori(0, NB) as b:
                    act.wait_ge(x_T, b + 2)
                    s_.copy(rT[:, 0, :], bank[0][:, :]).then_inc(xT_kept, 1)
                    act.wait_ge(score_mm, b + 1)
                    s_.activation(dst_score[:, bass.ds(b * BT * P, BT * P)], bank[3][:, :], ACT.Identity, bias=wad[:, 1:2])

            @block.vector
            def _(dve):
                dve.sem_inc(t0_kept, 1)
                with dve.Fori(0, NB) as b:
                    dve.wait_ge(t0_mm, b + 1)
                    dve.wait_ge(t0_free, b + 1)
                    for j in range(2):
                        last = v.tensor_add(tT0[:, 2 * j:2 * j + 2, :],
                                            bank[1 + j][:, 0:2 * AW].rearrange("p (t c) -> p t c", t=2),
                                            b0[:, :].unsqueeze(1).to_broadcast([P, 2, AW]))
                    last.then_inc(t0_kept, 1)

            @block.sync
            def _(sp):
                sp.sem_inc(t0_free, 1)
                with sp.Fori(0, NB) as b:
                    sp.wait_ge(t0_kept, b + 2)
                    sp.dma_start(t0.rearrange("(t p) c -> p t c", p=P)[:, tiles(b), :], tT0[:, :, :]).then_inc(t0_out, 16)
                    sp.wait_ge(t0_out, 16 * b + 16)
                    sp.sem_inc(t0_free, 1)

        l0_placed, l0_logit, l0_wide, l0_sum, l0_acc, l0_v, l0_p = (
            sem(f"l0_{n}") for n in ("placed", "logit", "wide", "sum", "acc", "vector", "prob"))
        with nc.Block() as block:
            @block.gpsimd
            def _(pool):
                with pool.Fori(0, ITERS) as i:
                    for g in range(RING):
                        gather(pool, i * RING + g, g, t0, AW, l0_placed, t0_out)

            @block.scalar
            def _(act):
                for k in range(RING):
                    place(k, k, l0_placed, (rel_now, rel), (ew_now, ew))
                with act.Fori(0, ITERS) as i:
                    for g in range(RING):
                        k = i * RING + g
                        act.wait_ge(l0_logit, k + 1)
                        s_.activation(small[:, g, 0:G], lg[:, g, 1, 0:G], ACT.Exp).then_inc(l0_p, 1)
                        s_.copy(wide[:, g, :, D + 1], ew_now[:, g * G:(g + 1) * G])
                        act.wait_ge(l0_p, k + 1)
                        for u in range(G):
                            last = s_.activation(wide[:, g, u, 0:D + 1], ring[:, g * G + u, 0:D + 1], ACT.Identity,
                                                 scale=small[:, g, u:u + 1])
                        last.then_inc(l0_wide, 1)
                        act.wait_ge(l0_wide, k + 1)
                        place(k + RING, g, l0_placed, (rel_now, rel), (ew_now, ew))

            @block.tensor
            def _(pe):
                with pe.Fori(0, ITERS) as i:
                    for g in range(RING):
                        k = i * RING + g
                        pe.wait_ge(l0_wide, k + 1)
                        pe.wait_ge(l0_acc, k * G + G)
                        for u in range(G):
                            last = t_.matmul(bank[2 * (g % 2) + u // 2][:, (u % 2) * AW:(u % 2) * AW + D + 2],
                                             hotf[:, g, u, :], wide[:, g, u, 0:D + 2], start=True, stop=True)
                        last.then_inc(l0_sum, 1)

            @block.vector
            def _(dve):
                regs = node_regs(dve, "l0_node")

                def front(i, g):
                    k = i * RING + g
                    ch = Chain(dve, l0_v, 2 * k)
                    load_nodes(dve, regs, k, g)
                    nodes = nodes_of(dve, regs, g)
                    dve.wait_ge(l0_placed, k + 1)
                    v.tensor_tensor(out=hotf[:, g, :, :], **hots(g))
                    for u in range(G):
                        last = v.scalar_tensor_tensor(out=junk[:, 0, u * P:(u + 1) * P], in0=iota[:, :],
                                                      scalar=rel_now[:, g * G + u:g * G + u + 1],
                                                      in1=dst_score[:, bass.ds(nodes[u] * P, P)],
                                                      op0=ALU.is_equal, op1=ALU.mult, accum_out=small[:, g, G + u:G + u + 1])
                    ch(last)
                    arrived(dve, i, g)
                    ch.wait()
                    ch(v.tensor_add(lg[:, g, 0, 0:G], ring[:, g * G:(g + 1) * G, D + 1], small[:, g, G:2 * G]))
                    ch.wait()
                    v.scalar_tensor_tensor(out=lg[:, g, 1, 0:G], in0=lg[:, g, 0, 0:G], scalar=0.01, in1=lg[:, g, 0, 0:G],
                                           op0=ALU.mult, op1=ALU.max).then_inc(l0_logit, 1)

                def back(i, g):
                    k = i * RING + g
                    nodes = nodes_of(dve, regs, g)
                    dve.wait_ge(l0_sum, k + 1)
                    for u in range(G):
                        here = flat(acc[:, bass.ds(nodes[u], 1), 0:D + 2])
                        dve.wait_ge(l0_acc, k * G + 2 * G + u)
                        v.tensor_add(here, here, bank[2 * (g % 2) + u // 2][:, (u % 2) * AW:(u % 2) * AW + D + 2]).then_inc(l0_acc, 1)

                def both(i, g, past, left):
                    if left:
                        front(*later(i, g, 1))
                    back(i, g)

                dve.sem_inc(l0_acc, 2 * G)
                front(0, 0)
                edge_rounds(dve, both)
        gcount[0] += ITERS


        (n1_prod, n1_prodT, n1_prodT_kept, n1_mm, n1_xn, n1_xnT, n1_xnT_kept, n1_kv_mm, n1_q_mm, n1_kv_kept,
         t1_out, t1_free, n1_copied, n1_v, n1_deg, n1_dis, n1_var, n1_std) = (sem(f"n1_{n}") for n in (
             "prod", "prodT", "prodT_kept", "mm", "xn", "xnT", "xnT_kept", "kv_mm", "q_mm", "kv_kept",
             "t1_out", "t1_free", "copied", "vector", "deg", "dis", "var", "std"))
        N1 = 19
        with nc.Block() as block:
            @block.vector
            def _(dve):
                def batch(b):
                    ch = Chain(dve, n1_v, N1 * b + 4)
                    x_b = xs[:, tiles(b), :]
                    ch(v.tensor_scalar(out=stat[:, :, 7], in0=acc[:, tiles(b), D], scalar1=1e-9, scalar2=None, op0=ALU.add))
                    ch.wait()
                    ch(v.reciprocal(stat[:, :, 7], stat[:, :, 7]))
                    ch.wait()
                    ch(v.tensor_tensor(out=tA, in0=acc[:, tiles(b), 0:D], in1=stat[:, :, 7:8].to_broadcast([P, BT, D]), op=ALU.mult))
                    ch.wait()
                    v.tensor_tensor(out=tB, in0=tA, in1=x_b, op=ALU.mult).then_inc(n1_prod, 1)
                    ch(v.tensor_tensor(out=tC, in0=tA, in1=x_b, op=ALU.add))
                    ch.wait()
                    ch(v.tensor_tensor(out=tC, in0=tC, in1=b2[:, :].unsqueeze(1).to_broadcast([P, BT, D]), op=ALU.add))
                    ch.wait()
                    dve.wait_ge(n1_mm, b + 1)
                    ch(v.tensor_tensor(out=flat(tA), in0=bank[1][:, :], in1=flat(tC), op=ALU.add))
                    ch.wait()
                    ch(v.scalar_tensor_tensor(out=flat(tA), in0=flat(tA), scalar=0.01, in1=flat(tA), op0=ALU.mult, op1=ALU.max))
                    ch.wait()
                    ch(v.tensor_tensor(out=tY, in0=tA, in1=x_b, op=ALU.add))
                    dve.wait_ge(n1_copied, b + 1)
                    layer_norm(ch, b, tY, [tN[:, u, :] for u in range(BT)], n1_var, n1_std)[-1].then_inc(n1_xn, 1)
                    dve.wait_ge(n1_q_mm, b + 1)
                    ch(v.tensor_scalar(out=flat(tA), in0=bank[5][:, :], scalar1=SCALE, scalar2=None, op0=ALU.mult))
                    split3(ch, tA, lambda c: look[:, tiles(b), c * D:(c + 1) * D])
                    assert ch.n == N1

                ch = Chain(dve, n1_v)
                deg = neg_max[:, 0:NT]
                ch(v.tensor_scalar(out=deg, in0=acc[:, :, D + 1], scalar1=1.0, scalar2=None, op0=ALU.add))
                ch.wait()
                v.tensor_scalar(out=dis[:, :], in0=deg, scalar1=1e-12, scalar2=None, op0=ALU.max).then_inc(n1_deg, 1)
                dve.wait_ge(n1_dis, 1)
                ch(v.reciprocal(dis[:, :], dis[:, :]))
                ch.wait()
                ch(v.scalar_tensor_tensor(out=dis[:, :], in0=deg, scalar=0.0, in1=dis[:, :], op0=ALU.is_gt, op1=ALU.mult))
                ch.wait()
                ch(v.memset(neg_max[:, :], BIG))
                with dve.Fori(0, NB) as b:
                    batch(b)

            @block.tensor
            def _(pe):
                with pe.Fori(0, NB) as b:
                    pe.wait_ge(n1_prod, b + 1)
                    for u in range(BT):
                        last = t_.transpose(bank[0][:, u * P:(u + 1) * P], tB[:, u, :], ident[:, :])
                    last.then_inc(n1_prodT, 1)
                    pe.wait_ge(n1_prodT_kept, b + 1)
                    for u in range(BT):
                        last = t_.matmul(bank[1][:, u * P:(u + 1) * P], rT[:, 0, u * P:(u + 1) * P], w2T[:, :], start=True, stop=True)
                    last.then_inc(n1_mm, 1)
                    pe.wait_ge(n1_xn, b + 1)
                    for u in range(BT):
                        last = t_.transpose(bank[2][:, u * P:(u + 1) * P], tN[:, u, :], ident[:, :])
                    last.then_inc(n1_xnT, 1)
                    pe.wait_ge(n1_xnT_kept, b + 1)
                    for u in range(BT):
                        last = t_.matmul(bank[5][:, u * P:(u + 1) * P], rT[:, 1, u * P:(u + 1) * P], wq[:, :], start=True, stop=True)
                    last.then_inc(n1_q_mm, 1)
                    pe.wait_ge(n1_kv_kept, b + 1)
                    for u in range(BT):
                        last = t_.matmul(bank[3 + u // 2][:, (u % 2) * 2 * D:(u % 2 + 1) * 2 * D],
                                         rT[:, 1, u * P:(u + 1) * P], wkv[:, :], start=True, stop=True)
                    last.then_inc(n1_kv_mm, 1)

            @block.scalar
            def _(act):
                act.sem_inc(n1_kv_kept, 1)
                act.wait_ge(n1_deg, 1)
                s_.activation(dis[:, :], dis[:, :], ACT.Sqrt).then_inc(n1_dis, 1)
                with act.Fori(0, NB) as b:
                    act.wait_ge(n1_prodT, b + 1)
                    s_.copy(rT[:, 0, :], bank[0][:, :]).then_inc(n1_prodT_kept, 1)
                    root(act, b, n1_var, n1_std)
                    act.wait_ge(n1_xnT, b + 1)
                    s_.copy(rT[:, 1, :], bank[2][:, :]).then_inc(n1_xnT_kept, 1)
                    act.wait_ge(n1_kv_mm, b + 1)
                    act.wait_ge(t1_free, b + 1)
                    s_.copy(flat(tKV[:, 0:2, :]), bank[3][:, :])
                    s_.copy(flat(tKV[:, 2:4, :]), bank[4][:, :]).then_inc(n1_kv_kept, 1)

            @block.gpsimd
            def _(pool):
                pool.sem_inc(n1_copied, 1)
                with pool.Fori(0, NB) as b:
                    pool.wait_ge(n1_xn, b + 1)
                    pool.sem_inc(rounds, 1)
                    q_.tensor_copy(xs[:, tiles(b), :], tN).then_inc(n1_copied, 1)
                pool.wait_ge(n1_v, N1 * NB + 4)
                q_.memset(acc[:, :, :], 0.0)

            @block.sync
            def _(sp):
                sp.sem_inc(t1_free, 1)
                with sp.Fori(0, NB) as b:
                    sp.wait_ge(n1_kv_kept, b + 2)
                    sp.dma_start(t1.rearrange("(t p) c -> p t c", p=P)[:, tiles(b), :], tKV).then_inc(t1_out, 16)
                    sp.wait_ge(t1_out, 16 * b + 16)
                    sp.sem_inc(t1_free, 1)

        (l1_placed, l1_away, l1_hot, l1_hotT, l1_hot_kept, l1_q, l1_gm, l1_gmT, l1_top, l1_topB, l1_neg, l1_p, l1_wide, l1_sum,
         l1_v) = (sem(f"l1_{n}") for n in (
             "placed", "away", "hot", "hotT", "hot_kept", "query", "group_max", "group_max_T", "top", "top_spread", "neg_top", "prob",
             "wide", "sum", "vector"))
        l1_acc = [sem(f"l1_acc{u}") for u in range(G)]
        TR, QB, MB, SUM = bank[0], (bank[1], bank[2]), bank[3], 4
        with nc.Block() as block:
            @block.gpsimd
            def _(pool):
                with pool.Fori(0, ITERS) as i:
                    for g in range(RING):
                        gather(pool, i * RING + g, g, t1, 2 * D, l1_placed, t1_out)

            @block.scalar
            def _(act):
                away = junk[:, 1, :]

                def place1(k, g):
                    s_.copy(rel_now[:, g * G:(g + 1) * G], rel[:, bass.ds(k * G, G)])
                    s_.copy(bias_now[:, g, :], tabf[:, bass.ds(k * G * H, G * H)])
                    place(k, g, l1_placed)

                def far_away(i, g, past):
                    k = i * RING + g
                    act.wait_ge(l1_placed, k + 1)
                    if past:
                        act.wait_ge(l1_hot, k)
                    for u in range(G):
                        last = s_.activation(away[:, u * P:(u + 1) * P], iota[:, :], ACT.Abs, scale=-1.0,
                                             bias=rel_now[:, g * G + u:g * G + u + 1])
                    last.then_inc(l1_away, 1)

                def one_hot(i, g, past):
                    k = i * RING + g
                    if past >= RING:
                        act.wait_ge(l1_sum, k - RING + 1)
                    act.wait_ge(l1_away, k + 1)
                    s_.activation(flat(hotf[:, g, :, :]), away, ACT.Relu, scale=-1.0, bias=1.0)
                    s_.activation(flat(hot[:, g, :, :]), away, ACT.Relu, scale=-1.0, bias=1.0).then_inc(l1_hot, 1)

                def keep_hot(i, g):
                    act.wait_ge(l1_hotT, i * RING + g + 1)
                    s_.copy(hotT[:, g, :], TR[:, :].bitcast(BF16)[:, 0:G * P]).then_inc(l1_hot_kept, 1)

                def weights(i, g):
                    act.wait_ge(l1_neg, i * RING + g + 1)
                    s_.activation(wide[:, g, :, D:AW], lg[:, g, 1, :].rearrange("p (u h) -> p u h", u=G), ACT.Exp,
                                  bias=small[:, g, 1:2])
                    s_.activation(small[:, g, 2:3], small[:, (g - 1) % RING, 1:2], ACT.Exp, scale=-1.0,
                                  bias=small[:, g, 1:2]).then_inc(l1_p, 1)

                def step(i, g, past, left):
                    k = i * RING + g
                    if left > 1:
                        far_away(*later(i, g, 2), past + 2)
                    if past:
                        weights(*later(i, g, -1))
                    if left > 1:
                        one_hot(*later(i, g, 2), past + 2)
                        keep_hot(*later(i, g, 2))
                    if past:
                        act.wait_ge(l1_wide, k)
                        place1(k + RING - 1, (g + RING - 1) % RING)

                for k in range(RING):
                    place1(k, k)
                for g in range(2):
                    far_away(0, g, g)
                    one_hot(0, g, g)
                    keep_hot(0, g)
                edge_rounds(act, step)
                weights(ITERS - 1, RING - 1)

            @block.tensor
            def _(pe):
                regs = node_regs(pe, "l1_q")

                def turn(i, g):
                    pe.wait_ge(l1_hot, i * RING + g + 1)
                    for u in range(G):
                        last = t_.transpose(TR[:, :].bitcast(BF16)[:, u * P:(u + 1) * P], hot[:, g, u, :], ident_b[:, :])
                    last.then_inc(l1_hotT, 1)

                def query(i, g):
                    load_nodes(pe, regs, i * RING + g, g)
                    nodes = nodes_of(pe, regs, g)
                    pe.wait_ge(l1_hot_kept, i * RING + g + 1)
                    for u in range(G):
                        for c in range(3):
                            last = t_.matmul(QB[g % 2][:, u * P:(u + 1) * P], hotT[:, g, u * P:(u + 1) * P],
                                             flat(look[:, bass.ds(nodes[u], 1), c * D:(c + 1) * D]), start=(c == 0), stop=(c == 2))
                    last.then_inc(l1_q, 1)

                def summed(i, g):
                    k = i * RING + g
                    pe.wait_ge(l1_wide, k + 1)
                    pe.wait_ge(l1_acc[G - 1], k + 1)
                    for u in range(G):
                        last = t_.matmul(bank[SUM + 2 * (g % 2) + u // 2][:, (u % 2) * AW:(u % 2 + 1) * AW],
                                         hotf[:, g, u, :], wide[:, g, u, :], start=True, stop=True)
                    last.then_inc(l1_sum, 1)

                def step(i, g, past, left):
                    k = i * RING + g
                    if past >= 2:
                        summed(*later(i, g, -2))
                    if left:
                        query(*later(i, g, 1))
                    pe.wait_ge(l1_gm, k + 1)
                    t_.transpose(MB[0:1, 0:P], small[:, g, 0:1], ident[:, :]).then_inc(l1_gmT, 1)
                    if left > 1:
                        turn(*later(i, g, 2))
                    pe.wait_ge(l1_top, k + 1)
                    t_.matmul(MB[:, P:P + 1], ones[0:1, :], top[:, 0:1], start=True, stop=True).then_inc(l1_topB, 1)

                turn(0, 0)
                query(0, 0)
                turn(0, 1)
                edge_rounds(pe, step)
                summed(ITERS - 1, RING - 2)
                summed(ITERS - 1, RING - 1)

            @block.vector
            def _(dve):
                regs = node_regs(dve, "l1_node")
                L1 = 5

                def add(i, g, u, nodes):
                    k = i * RING + g
                    here = flat(acc[:, bass.ds(nodes[u], 1), :])
                    new = bank[SUM + 2 * (g % 2) + u // 2][:, (u % 2) * AW:(u % 2 + 1) * AW]
                    if u:
                        dve.wait_ge(l1_acc[u - 1], k + 1)
                        v.tensor_add(here, here, new).then_inc(l1_acc[u], 1)
                    else:
                        dve.wait_ge(l1_sum, k + 1)
                        dve.wait_ge(l1_acc[G - 1], k + 2)
                        v.tensor_copy(neg_max[:, bass.ds(nodes[0], G)], small[:, g, 1:2].to_broadcast([P, G]))
                        v.scalar_tensor_tensor(out=here, in0=here, scalar=small[:, g, 2:3], in1=new,
                                               op0=ALU.mult, op1=ALU.add).then_inc(l1_acc[0], 1)

                def widen(i, g):
                    dve.wait_ge(l1_p, i * RING + g + 1)
                    v.tensor_tensor(out=wide[:, g, :, 0:D].rearrange("p u (h d) -> p u h d", h=H),
                                    in0=ring[:, g * G:(g + 1) * G, D:2 * D].rearrange("p u (h d) -> p u h d", h=H),
                                    in1=wide[:, g, :, D:AW].unsqueeze(3).to_broadcast([P, G, H, HD]), op=ALU.mult).then_inc(l1_wide, 1)

                def negate(i, g):
                    dve.wait_ge(l1_topB, i * RING + g + 1)
                    v.tensor_scalar(out=small[:, g, 1:2], in0=MB[:, P:P + 1], scalar1=-1.0, scalar2=None, op0=ALU.mult).then_inc(l1_neg, 1)

                def back(i, g):
                    nodes = nodes_of(dve, regs, g)
                    return lambda u: add(i, g, u, nodes)

                def step(i, g, past, left):
                    k = i * RING + g
                    ch = Chain(dve, l1_v, L1 * k + 1)
                    add_step = back(*later(i, g, -3)) if past >= 3 else lambda u: None
                    arrived(dve, i, g)
                    dve.wait_ge(l1_q, k + 1)
                    prod = junk[:, 0, :]
                    ch(v.tensor_tensor(out=prod.rearrange("p (u d) -> p u d", u=G), in0=QB[g % 2][:, :].rearrange("p (u d) -> p u d", u=G),
                                       in1=ring[:, g * G:(g + 1) * G, 0:D], op=ALU.mult))
                    if past:
                        negate(*later(i, g, -1))
                    add_step(0)
                    ch.wait()
                    ch(v.tensor_reduce(out=lg[:, g, 0, :], in_=prod.rearrange("p (a d) -> p a d", d=HD), axis=AX.X, op=ALU.add))
                    add_step(1)
                    ch.wait()
                    ch(v.tensor_add(lg[:, g, 0, :], lg[:, g, 0, :], bias_now[:, g, :]))
                    ch.wait()
                    ch(v.scalar_tensor_tensor(out=lg[:, g, 1, :], in0=lg[:, g, 0, :], scalar=0.2, in1=lg[:, g, 0, :],
                                              op0=ALU.mult, op1=ALU.max))
                    ch.wait()
                    v.reduce_max(small[:, g, 0:1], lg[:, g, 1, :], axis=AX.X).then_inc(l1_gm, 1)
                    if past:
                        widen(*later(i, g, -1))
                    add_step(2)
                    add_step(3)
                    if past >= 2:
                        load_nodes(dve, regs, k - 2, g - 2)
                    dve.wait_ge(l1_gmT, k + 1)
                    ch(v.reduce_max(top[:, 1:2], MB[0:1, 0:P], axis=AX.X))
                    ch.wait()
                    v.tensor_max(top[:, 0:1], top[:, 0:1], top[:, 1:2]).then_inc(l1_top, 1)
                    assert ch.n == L1

                dve.sem_inc(l1_acc[G - 1], 2)
                v.memset(small[:, RING - 1, 1:2], BIG).then_inc(l1_v, 1)
                edge_rounds(dve, step)
                negate(ITERS - 1, RING - 1)
                widen(ITERS - 1, RING - 1)
                for g in range(1, RING):
                    load_nodes(dve, regs, (ITERS - 1) * RING + g, g)
                    add_step = back(ITERS - 1, g)
                    for u in range(G):
                        add_step(u)
        gcount[0] += ITERS

        with nc.Block() as block:
            @block.sync
            def _(sp):
                for used in early_sems:
                    sp.sem_clear(used)
        early.close()
        early_sems = None

        (n2_staged, n2_agg, n2_aggT, n2_aggT_kept, n2_o_mm, n2_o_kept, n2_xT, n2_xT_kept, n2_mm, n2_var, n2_std, n2_xn, n2_xnT,
         n2_xnT_kept, n2_e_mm, n2_e_kept, t2_out, t2_free, n2_copied, n2_v, n2_neg, n2_factor) = (sem(f"n2_{n}") for n in (
             "staged", "agg", "aggT", "aggT_kept", "o_mm", "o_kept", "xT", "xT_kept", "mm", "var", "std", "xn", "xnT", "xnT_kept",
             "e_mm", "e_kept", "t2_out", "t2_free", "copied", "vector", "neg_top", "factor"))
        N2 = 13
        with nc.Block() as block:
            @block.vector
            def _(dve):
                def batch(b):
                    ch = Chain(dve, n2_v, N2 * b + 4)
                    v.tensor_tensor(out=tB.rearrange("p t (h d) -> p t h d", h=H),
                                    in0=acc[:, tiles(b), 0:D].rearrange("p t (h d) -> p t h d", h=H),
                                    in1=rs[:, tiles(b), 0:H].unsqueeze(3).to_broadcast([P, BT, H, HD]), op=ALU.mult).then_inc(n2_agg, 1)
                    dve.wait_ge(n2_mm, b + 1)
                    ch(v.tensor_tensor(out=tA, in0=bank[3][:, :].rearrange("p (t d) -> p t d", t=BT),
                                       in1=bmb[:, :].unsqueeze(1).to_broadcast([P, BT, D]), op=ALU.add))
                    ch.wait()
                    ch(v.scalar_tensor_tensor(out=flat(tY), in0=flat(tA), scalar=0.0, in1=flat(tX), op0=ALU.max, op1=ALU.add))
                    dve.wait_ge(n2_copied, b + 1)
                    layer_norm(ch, b, tY, [tN[:, u, :] for u in range(BT)], n2_var, n2_std)[-1].then_inc(n2_xn, 1)
                    dve.wait_ge(n2_e_mm, b + 1)
                    halves = bank[5][:, :].rearrange("p (t c) -> p t c", t=BT)
                    dve.wait_ge(t2_free, b + 1)
                    v.tensor_tensor(out=tT2, in0=halves[:, :, 0:EH], in1=be1b[:, :].unsqueeze(1).to_broadcast([P, BT, EH]),
                                    op=ALU.add).then_inc(n2_e_kept, 1)
                    ch(v.tensor_copy(tA[:, :, 0:EH], halves[:, :, EH:2 * EH]))
                    split3(ch, tA[:, :, 0:EH], lambda c: look[:, tiles(b), c * EH:(c + 1) * EH])
                    assert ch.n == N2, ch.n

                ch = Chain(dve, n2_v)
                spread = rs[:, :, H:H + 1].to_broadcast([P, NT, H])
                dve.wait_ge(n2_factor, 1)
                ch(v.tensor_tensor(out=rs[:, :, 0:H], in0=acc[:, :, D:AW], in1=spread, op=ALU.mult))
                ch.wait()
                ch(v.tensor_scalar(out=rs[:, :, 0:H], in0=rs[:, :, 0:H], scalar1=1e-12, scalar2=None, op0=ALU.max))
                ch.wait()
                ch(v.reciprocal(rs[:, :, 0:H], rs[:, :, 0:H]))
                ch.wait()
                ch(v.tensor_tensor(out=rs[:, :, 0:H], in0=rs[:, :, 0:H], in1=spread, op=ALU.mult))
                ch.wait()
                with dve.Fori(0, NB) as b:
                    batch(b)

            @block.tensor
            def _(pe):
                with pe.Fori(0, NB) as b:
                    pe.wait_ge(n2_staged, b + 1)
                    for u in range(BT):
                        last = t_.transpose(bank[2][:, u * P:(u + 1) * P], tX[:, u, :], ident[:, :])
                    last.then_inc(n2_xT, 1)
                    pe.wait_ge(n2_agg, b + 1)
                    for u in range(BT):
                        last = t_.transpose(bank[0][:, u * P:(u + 1) * P], tB[:, u, :], ident[:, :])
                    last.then_inc(n2_aggT, 1)
                    pe.wait_ge(n2_aggT_kept, b + 1)
                    t_.matmul(bank[1][:, :], wo[:, :], rT[:, 0, :], start=True, stop=True).then_inc(n2_o_mm, 1)
                    pe.wait_ge(n2_xT_kept, b + 1)
                    pe.wait_ge(n2_o_kept, b + 1)
                    for u in range(BT):
                        at = slice(u * P, (u + 1) * P)
                        t_.matmul(bank[3][:, at], rT[:, 1, at], wm[:, 0, :], start=True, stop=False)
                        last = t_.matmul(bank[3][:, at], rT[:, 2, at], wm[:, 1, :], start=False, stop=True)
                    last.then_inc(n2_mm, 1)
                    pe.wait_ge(n2_xn, b + 1)
                    for u in range(BT):
                        last = t_.transpose(bank[4][:, u * P:(u + 1) * P], tN[:, u, :], ident[:, :])
                    last.then_inc(n2_xnT, 1)
                    pe.wait_ge(n2_xnT_kept, b + 1)
                    for u in range(BT):
                        for c in range(2):
                            last = t_.matmul(bank[5][:, u * P + c * EH:u * P + (c + 1) * EH], rT[:, 0, u * P:(u + 1) * P], we1[:, c, :],
                                             start=True, stop=True)
                    last.then_inc(n2_e_mm, 1)

            @block.scalar
            def _(act):
                s_.activation(rs[:, :, H], neg_max[:, 0:NT], ACT.Exp, scale=-1.0, bias=small[:, RING - 1, 1:2]).then_inc(n2_factor, 1)
                with act.Fori(0, NB) as b:
                    act.wait_ge(n2_xT, b + 1)
                    s_.copy(rT[:, 1, :], bank[2][:, :]).then_inc(n2_xT_kept, 1)
                    act.wait_ge(n2_aggT, b + 1)
                    s_.copy(rT[:, 0, :], bank[0][:, :]).then_inc(n2_aggT_kept, 1)
                    act.wait_ge(n2_o_mm, b + 1)
                    s_.activation(rT[:, 2, :], bank[1][:, :], ACT.Identity, bias=boc[:, 0:1]).then_inc(n2_o_kept, 1)
                    root(act, b, n2_var, n2_std)
                    act.wait_ge(n2_xnT, b + 1)
                    s_.copy(rT[:, 0, :], bank[4][:, :]).then_inc(n2_xnT_kept, 1)

            @block.gpsimd
            def _(pool):
                pool.sem_inc(n2_copied, 1)
                with pool.Fori(0, NB) as b:
                    pool.wait_ge(n2_copied, b + 1)
                    pool.sem_inc(rounds, 1)
                    q_.tensor_copy(tX, xs[:, tiles(b), :]).then_inc(n2_staged, 1)
                    pool.wait_ge(n2_xn, b + 1)
                    pool.sem_inc(rounds, 1)
                    q_.tensor_copy(xs[:, tiles(b), :], tN).then_inc(n2_copied, 1)
                pool.wait_ge(n2_v, N2 * NB + 4)
                q_.memset(acc[:, :, :], 0.0)

            @block.sync
            def _(sp):
                sp.sem_inc(t2_free, 1)
                with sp.Fori(0, NB) as b:
                    sp.wait_ge(n2_e_kept, b + 1)
                    sp.dma_start(t2.rearrange("(t p) c -> p t c", p=P)[:, tiles(b), :], tT2).then_inc(t2_out, 16)
                    sp.wait_ge(t2_out, 16 * b + 16)
                    sp.sem_inc(t2_free, 1)

        (l2_placed, l2_hot, l2_hotT, l2_hot_kept, l2_half, l2_pre, l2_s1, l2_s1T, l2_s1T_kept, l2_e, l2_s2, l2_dup, l2_cut, l2_keyB,
         l2_same, l2_v, l2_init) = (sem(f"l2_{n}") for n in (
             "placed", "hot", "hotT", "hot_kept", "half", "pre", "silu1", "silu1T", "silu1T_kept", "e", "silu2", "dup", "cut", "keyB",
             "same", "vector", "init"))
        TR, KB, HB, ST, EB, DB = bank[0:6]
        same_tri = tabf[:, 0:G * P]
        s1T = tabf[0:EH + 1, G * P:2 * G * P]
        W4 = G * EH
        with nc.Block() as block:
            def cut(g):
                return wide[:, g, :, :].rearrange("p u c -> p (u c)")[:, 0:W4]

            def silu2(g):
                return wide[:, g, :, :].rearrange("p u c -> p (u c)")[:, W4:2 * W4]

            @block.gpsimd
            def _(pool):
                def step(i, g, past, left):
                    k = i * RING + g
                    for u in range(G):
                        pool.wait_ge(scattered[u], 16 * k + 16)
                    pool.wait_ge(l2_cut, k + 1)
                    pool.sem_inc(rounds, 1)
                    for u in range(G):
                        q_.indirect_dma_start(mlp_sum[u], bass.IndirectOffsetOnAxis(ap=put_i[:, g, u:u + 1].bitcast(U32), axis=0),
                                              cut(g)[:, u * EH:(u + 1) * EH], None, compute_op=ALU.add).then_inc(scattered[u], 16)
                    if left >= RING - 1:
                        gather(pool, k + RING - 1, (g + RING - 1) % RING, t2, EH, l2_placed, t2_out)

                for k in range(RING - 1):
                    gather(pool, k, k, t2, EH, l2_placed, t2_out)
                edge_rounds(pool, step)
                for u in range(G):
                    pool.wait_ge(scattered[u], 16 * GROUPS + 16)

            @block.scalar
            def _(act):
                columns = ((rel_now, rel), (key_now, key))

                def keep_hot(i, g):
                    act.wait_ge(l2_hotT, i * RING + g + 1)
                    s_.copy(hotT[:, g, :], TR[:, :].bitcast(BF16)[:, 0:G * P]).then_inc(l2_hot_kept, 1)

                def second(i, g):
                    act.wait_ge(l2_e, i * RING + g + 1)
                    s_.activation(silu2(g), EB[:, 0:W4], ACT.Silu).then_inc(l2_s2, 1)

                def step(i, g, past, left):
                    k = i * RING + g
                    act.wait_ge(l2_pre, k + 1)
                    s_.activation(junk[:, g % 2, 0:W4], junk[:, g % 2, W4:2 * W4], ACT.Silu).then_inc(l2_s1, 1)
                    if left:
                        keep_hot(*later(i, g, 1))
                    if past:
                        second(*later(i, g, -1))
                    act.wait_ge(l2_s1T, k + 1)
                    s_.copy(s1T[0:EH, :], ST[0:EH, :]).then_inc(l2_s1T_kept, 1)
                    place(k + RING, g, l2_placed, *columns)

                for k in range(RING):
                    place(k, k, l2_placed, *columns)
                keep_hot(0, 0)
                edge_rounds(act, step)
                second(ITERS - 1, RING - 1)

            @block.tensor
            def _(pe):
                regs = node_regs(pe, "l2_half")

                def turn(i, g):
                    pe.wait_ge(l2_hot, i * RING + g + 1)
                    for u in range(G):
                        t_.matmul(KB[:, u * P:(u + 1) * P], key_now[:, g * G + u:g * G + u + 1].to_broadcast([P, P]), ident[:, :],
                                  start=True, stop=True)
                    for u in range(G):
                        last = t_.transpose(TR[:, :].bitcast(BF16)[:, u * P:(u + 1) * P], hot[:, g, u, :], ident_b[:, :])
                    last.then_inc(l2_hotT, 1)

                def half(i, g):
                    load_nodes(pe, regs, i * RING + g, g)
                    nodes = nodes_of(pe, regs, g)
                    pe.wait_ge(l2_hot_kept, i * RING + g + 1)
                    for u in range(G):
                        for c in range(3):
                            last = t_.matmul(HB[:, u * EH:(u + 1) * EH], hotT[:, g, u * P:(u + 1) * P],
                                             flat(look[:, bass.ds(nodes[u], 1), c * EH:(c + 1) * EH]), start=(c == 0), stop=(c == 2))
                    last.then_inc(l2_half, 1)

                def same_sums(i, g):
                    pe.wait_ge(l2_s2, i * RING + g + 1)
                    pe.wait_ge(l2_same, i * RING + g + 1)
                    for u in range(G):
                        last = t_.matmul(DB[:, u * EH:(u + 1) * EH], hotf[:, g, u, :], silu2(g)[:, u * EH:(u + 1) * EH], start=True, stop=True)
                    last.then_inc(l2_dup, 1)

                def step(i, g, past, left):
                    k = i * RING + g
                    if left:
                        turn(*later(i, g, 1))
                    pe.wait_ge(l2_s1, k + 1)
                    pe.sem_inc(rounds, 1)
                    for u in range(G):
                        last = t_.transpose(ST[0:EH, u * P:(u + 1) * P], junk[:, g % 2, u * EH:(u + 1) * EH], ident[:, :])
                    last.then_inc(l2_s1T, 1)
                    if left:
                        half(*later(i, g, 1))
                    if past:
                        same_sums(*later(i, g, -1))
                    pe.wait_ge(l2_s1T_kept, k + 1)
                    for u in range(G):
                        last = t_.matmul(EB[:, u * EH:(u + 1) * EH], s1T[:, u * P:(u + 1) * P], we2[:, :], start=True, stop=True)
                    last.then_inc(l2_e, 1)

                turn(0, 0)
                half(0, 0)
                edge_rounds(pe, step)
                pe.wait_ge(l2_cut, GROUPS - 1)
                same_sums(ITERS - 1, RING - 1)

            @block.vector
            def _(dve):
                L2 = 7

                def one_hot(i, g):
                    dve.wait_ge(l2_placed, i * RING + g + 1)
                    v.tensor_tensor(out=hot[:, g, :, :], **hots(g)).then_inc(l2_hot, 1)

                def duplicates(i, g):
                    k = i * RING + g
                    ch = Chain(dve, l2_v, L2 * k)
                    keys_g = key_now[:, g * G:(g + 1) * G]
                    dve.wait_ge(l2_hotT, k + 1)
                    v.tensor_tensor(out=hotf[:, g, :, :], in0=KB[:, :].rearrange("p (u e) -> p u e", u=G),
                                    in1=keys_g.unsqueeze(2).to_broadcast([P, G, P]), op=ALU.is_equal).then_inc(l2_same, 1)
                    dve.wait_ge(l2_same, k + 1)
                    ch(v.tensor_tensor(out=same_tri.rearrange("p (u e) -> p u e", u=G), in0=hotf[:, g, :, :],
                                       in1=tri[:, :].unsqueeze(1).to_broadcast([P, G, P]), op=ALU.mult))
                    ch.wait()
                    s = [small[:, g, j * G:(j + 1) * G] for j in range(5)]
                    ch(v.tensor_reduce(out=s[0], in_=same_tri.rearrange("p (u e) -> p u e", u=G), axis=AX.X, op=ALU.add))
                    ch(v.tensor_scalar(out=s[2], in0=keys_g, scalar1=far[:, 1:2], scalar2=None, op0=ALU.subtract))
                    ch.wait()
                    ch(v.tensor_scalar(out=s[1], in0=s[0], scalar1=0.5, scalar2=None, op0=ALU.is_lt))
                    ch.wait()
                    ch(v.scalar_tensor_tensor(out=s[3], in0=keys_g, scalar=float(FAR), in1=s[1], op0=ALU.is_lt, op1=ALU.mult))
                    ch.wait()
                    ch(v.tensor_tensor(out=s[4], in0=s[2], in1=s[3], op=ALU.mult))
                    ch.wait()
                    ch(v.tensor_scalar(out=put_i[:, g, :], in0=s[4], scalar1=far[:, 1:2], scalar2=None, op0=ALU.add))
                    assert ch.n == L2, ch.n

                def keep_cut(i, g):
                    dve.wait_ge(l2_dup, i * RING + g + 1)
                    v.tensor_copy(cut(g), DB[:, 0:W4]).then_inc(l2_cut, 1)

                def step(i, g, past, left):
                    k = i * RING + g
                    if past >= RING - 1:
                        for u in range(G):
                            dve.wait_ge(scattered[u], 16 * k - 16)
                    arrived(dve, i, g)
                    dve.wait_ge(l2_half, k + 1)
                    v.tensor_tensor(out=junk[:, g % 2, W4:2 * W4].rearrange("p (u f) -> p u f", u=G),
                                    in0=HB[:, 0:W4].rearrange("p (u f) -> p u f", u=G), in1=ring[:, g * G:(g + 1) * G, 0:EH],
                                    op=ALU.add).then_inc(l2_pre, 1)
                    if left:
                        one_hot(*later(i, g, 1))
                        duplicates(*later(i, g, 1))
                    if past:
                        keep_cut(*later(i, g, -1))

                v.memset(tabf[EH:EH + 1, G * P:2 * G * P], 1.0).then_inc(l2_init, 1)
                one_hot(0, 0)
                duplicates(0, 0)
                edge_rounds(dve, step)
                keep_cut(ITERS - 1, RING - 1)
        gcount[0] += ITERS

        (n3_staged, n3_in, n3_used, n3_sum, n3_xT, n3_sumT, n3_xT_kept, n3_sumT_kept, n3_h_mm, n3_h_kept, n3_mm, n3_var, n3_std, n3_xn,
         n3_xnT, n3_xnT_kept, n3_t_mm, n3_t_kept, t3_out, n3_copied, n3_v) = (sem(f"n3_{n}") for n in (
             "staged", "in", "used", "sum", "xT", "sumT", "xT_kept", "sumT_kept", "h_mm", "h_kept", "mm", "var", "std", "xn", "xnT",
             "xnT_kept", "t_mm", "t_kept", "t3_out", "copied", "vector"))
        N3 = 9
        with nc.Block() as block:
            @block.sync
            def _(sp):
                def load(b):
                    for u in range(G):
                        sp.dma_start(tS[:, u, :, :], mlp_sum[u][0:NP, :].rearrange("(t p) f -> p t f", p=P)[:, tiles(b), :]).then_inc(n3_in, 16)

                sp.sem_inc(n3_used, 1)
                with sp.Fori(0, NB) as b:
                    sp.wait_ge(n3_used, b + 1)
                    load(b)
                    sp.wait_ge(n3_t_kept, b + 1)
                    sp.dma_start(t3.rearrange("(t p) c -> p t c", p=P)[:, tiles(b), :], tab[:, tiles(b), 0:D]).then_inc(t3_out, 16)
                sp.wait_ge(t3_out, 16 * NB)

            @block.vector
            def _(dve):
                with dve.Fori(0, NB) as b:
                    ch = Chain(dve, n3_v, N3 * b)
                    dve.wait_ge(n3_in, 16 * G * b + 16 * G)
                    ch(v.tensor_add(tB[:, :, 0:EH], tS[:, 0, :, :], tS[:, 1, :, :]))
                    ch(v.tensor_add(tC[:, :, 0:EH], tS[:, 2, :, :], tS[:, 3, :, :]))
                    ch.wait()
                    v.tensor_add(tB[:, :, 0:EH], tB[:, :, 0:EH], tC[:, :, 0:EH]).then_inc(n3_sum, 1)
                    dve.wait_ge(n3_mm, b + 1)
                    ch(v.tensor_tensor(out=tA, in0=bank[3][:, :].rearrange("p (t d) -> p t d", t=BT),
                                       in1=bn2b[:, :].unsqueeze(1).to_broadcast([P, BT, D]), op=ALU.add))
                    ch.wait()
                    ch(v.scalar_tensor_tensor(out=flat(tY), in0=flat(tX), scalar=2.0, in1=flat(tA), op0=ALU.mult, op1=ALU.add))
                    dve.wait_ge(n3_copied, b + 1)
                    layer_norm(ch, b, tY, [tN[:, u, :] for u in range(BT)], n3_var, n3_std)[-1].then_inc(n3_xn, 1)
                    dve.wait_ge(n3_t_mm, b + 1)
                    v.tensor_tensor(out=tab[:, tiles(b), 0:D], in0=bank[5][:, :].rearrange("p (t d) -> p t d", t=BT),
                                    in1=dis[:, tiles(b)].unsqueeze(2).to_broadcast([P, BT, D]), op=ALU.mult).then_inc(n3_t_kept, 1)
                    assert ch.n == N3

            @block.tensor
            def _(pe):
                with pe.Fori(0, NB) as b:
                    pe.wait_ge(n3_staged, b + 1)
                    for u in range(BT):
                        last = t_.transpose(bank[1][:, u * P:(u + 1) * P], tX[:, u, :], ident[:, :])
                    last.then_inc(n3_xT, 1)
                    pe.wait_ge(n3_sum, b + 1)
                    pe.sem_inc(rounds, 1)
                    for u in range(BT):
                        last = t_.transpose(bank[0][0:EH, u * P:(u + 1) * P], tB[:, u, 0:EH], ident[:, :])
                    last.then_inc(n3_sumT, 1)
                    pe.wait_ge(n3_xT_kept, b + 1)
                    t_.matmul(bank[2][:, :], wn1[:, 0, :], rT[:, 1, :], start=True, stop=False)
                    pe.wait_ge(n3_sumT_kept, b + 1)
                    t_.matmul(bank[2][:, :], wn1[0:EH, 1, :], rT[0:EH, 0, :], start=False, stop=True).then_inc(n3_h_mm, 1)
                    pe.wait_ge(n3_h_kept, b + 1)
                    for u in range(BT):
                        last = t_.matmul(bank[3][:, u * P:(u + 1) * P], rT[:, 2, u * P:(u + 1) * P], wn2[:, :], start=True, stop=True)
                    last.then_inc(n3_mm, 1)
                    pe.wait_ge(n3_xn, b + 1)
                    for u in range(BT):
                        last = t_.transpose(bank[4][:, u * P:(u + 1) * P], tN[:, u, :], ident[:, :])
                    last.then_inc(n3_xnT, 1)
                    pe.wait_ge(n3_xnT_kept, b + 1)
                    for u in range(BT):
                        last = t_.matmul(bank[5][:, u * P:(u + 1) * P], rT[:, 1, u * P:(u + 1) * P], wg1[:, :], start=True, stop=True)
                    last.then_inc(n3_t_mm, 1)

            @block.scalar
            def _(act):
                with act.Fori(0, NB) as b:
                    act.wait_ge(n3_xT, b + 1)
                    s_.copy(rT[:, 1, :], bank[1][:, :]).then_inc(n3_xT_kept, 1)
                    act.wait_ge(n3_sumT, b + 1)
                    s_.copy(rT[0:EH, 0, :], bank[0][0:EH, :]).then_inc(n3_sumT_kept, 1)
                    act.wait_ge(n3_h_mm, b + 1)
                    s_.activation(rT[:, 2, :], bank[2][:, :], ACT.Silu, bias=bn1c[:, 0:1]).then_inc(n3_h_kept, 1)
                    root(act, b, n3_var, n3_std)
                    act.wait_ge(n3_xnT, b + 1)
                    s_.copy(rT[:, 1, :], bank[4][:, :]).then_inc(n3_xnT_kept, 1)

            @block.gpsimd
            def _(pool):
                pool.sem_inc(n3_copied, 1)
                with pool.Fori(0, NB) as b:
                    pool.wait_ge(n3_copied, b + 1)
                    pool.sem_inc(rounds, 1)
                    q_.tensor_copy(tX, xs[:, tiles(b), :]).then_inc(n3_staged, 1)
                    pool.wait_ge(n3_sum, b + 1)
                    pool.sem_inc(n3_used, 1)
                    pool.wait_ge(n3_xn, b + 1)
                    pool.sem_inc(rounds, 1)
                    q_.tensor_copy(xs[:, tiles(b), :], tN).then_inc(n3_copied, 1)

        def convolution(name, table, table_out):
            placed, hot_made, summed, added = (sem(f"{name}_{n}") for n in ("placed", "hot", "sum", "acc"))
            with nc.Block() as block:
                @block.gpsimd
                def _(pool):
                    with pool.Fori(0, ITERS) as i:
                        for g in range(RING):
                            gather(pool, i * RING + g, g, table, D, placed, table_out)

                @block.scalar
                def _(act):
                    for k in range(RING):
                        place(k, k, placed, (rel_now, rel), (ew_now, ew))
                    with act.Fori(0, ITERS) as i:
                        for g in range(RING):
                            k = i * RING + g
                            act.wait_ge(summed, k + 1)
                            place(k + RING, g, placed, (rel_now, rel), (ew_now, ew))

                @block.tensor
                def _(pe):
                    with pe.Fori(0, ITERS) as i:
                        for g in range(RING):
                            k = i * RING + g
                            pe.wait_ge(hot_made, k + 1)
                            pe.wait_ge(added, k * G + G)
                            arrived(pe, i, g)
                            for u in range(G):
                                last = t_.matmul(bank[g][:, u * P:(u + 1) * P], hotf[:, g, u, :], ring[:, g * G + u, 0:D],
                                                 start=True, stop=True)
                            last.then_inc(summed, 1)

                @block.vector
                def _(dve):
                    regs = node_regs(dve, f"{name}_node")

                    def front(i, g):
                        dve.wait_ge(placed, i * RING + g + 1)
                        for u in range(G):
                            at = slice(g * G + u, g * G + u + 1)
                            last = v.tensor_scalar(out=hotf[:, g, u, :], in0=iota[:, :], scalar1=rel_now[:, at], scalar2=ew_now[:, at],
                                                   op0=ALU.is_equal, op1=ALU.mult)
                        last.then_inc(hot_made, 1)

                    def back(i, g):
                        k = i * RING + g
                        load_nodes(dve, regs, k, g)
                        nodes = nodes_of(dve, regs, g)
                        dve.wait_ge(summed, k + 1)
                        for u in range(G):
                            here = flat(acc[:, bass.ds(nodes[u], 1), 0:D])
                            dve.wait_ge(added, k * G + RING * G + u)
                            v.tensor_add(here, here, bank[g][:, u * P:(u + 1) * P]).then_inc(added, 1)

                    def both(i, g, past, left):
                        if left:
                            front(*later(i, g, 1))
                        back(i, g)

                    dve.sem_inc(added, RING * G)
                    front(0, 0)
                    edge_rounds(dve, both)
            gcount[0] += ITERS

        convolution("c1", t3, t3_out)

        n4_r, n4_rT, n4_rT_kept, n4_mm, n4_kept, t4_out, n4_v = (
            sem(f"n4_{n}") for n in ("relu", "reluT", "reluT_kept", "mm", "kept", "t4_out", "vector"))
        N4 = 3
        with nc.Block() as block:
            @block.vector
            def _(dve):
                with dve.Fori(0, NB) as b:
                    ch = Chain(dve, n4_v, N4 * b)
                    spread = dis[:, tiles(b)].unsqueeze(2).to_broadcast([P, BT, D])
                    ch(v.tensor_add(tA, acc[:, tiles(b), 0:D], tab[:, tiles(b), 0:D]))
                    ch.wait()
                    ch(v.tensor_tensor(out=tA, in0=tA, in1=spread, op=ALU.mult))
                    ch.wait()
                    ch(v.tensor_tensor(out=tA, in0=tA, in1=bg1[:, :].unsqueeze(1).to_broadcast([P, BT, D]), op=ALU.add))
                    ch.wait()
                    v.tensor_scalar(out=tB, in0=tA, scalar1=0.0, scalar2=None, op0=ALU.max).then_inc(n4_r, 1)
                    dve.wait_ge(n4_mm, b + 1)
                    v.tensor_tensor(out=tab[:, tiles(b), 0:D], in0=bank[1][:, :].rearrange("p (t d) -> p t d", t=BT),
                                    in1=spread, op=ALU.mult).then_inc(n4_kept, 1)

            @block.tensor
            def _(pe):
                with pe.Fori(0, NB) as b:
                    pe.wait_ge(n4_r, b + 1)
                    for u in range(BT):
                        last = t_.transpose(bank[0][:, u * P:(u + 1) * P], tB[:, u, :], ident[:, :])
                    last.then_inc(n4_rT, 1)
                    pe.wait_ge(n4_rT_kept, b + 1)
                    for u in range(BT):
                        last = t_.matmul(bank[1][:, u * P:(u + 1) * P], rT[:, 0, u * P:(u + 1) * P], wg2[:, :], start=True, stop=True)
                    last.then_inc(n4_mm, 1)

            @block.scalar
            def _(act):
                with act.Fori(0, NB) as b:
                    act.wait_ge(n4_rT, b + 1)
                    s_.copy(rT[:, 0, :], bank[0][:, :]).then_inc(n4_rT_kept, 1)

            @block.gpsimd
            def _(pool):
                pool.wait_ge(n4_r, NB)
                q_.memset(acc[:, :, :], 0.0)

            @block.sync
            def _(sp):
                with sp.Fori(0, NB) as b:
                    sp.wait_ge(n4_kept, b + 1)
                    sp.dma_start(t4.rearrange("(t p) c -> p t c", p=P)[:, tiles(b), :], tab[:, tiles(b), 0:D]).then_inc(t4_out, 16)
                sp.wait_ge(t4_out, 16 * NB)

        convolution("c2", t4, t4_out)

        n5_var, n5_std, n5_done, n5_out, n5_v = (sem(f"n5_{n}") for n in ("var", "std", "done", "out", "vector"))
        N5 = 9
        with nc.Block() as block:
            @block.vector
            def _(dve):
                with dve.Fori(0, NB) as b:
                    ch = Chain(dve, n5_v, N5 * b)
                    ch(v.tensor_add(tA, acc[:, tiles(b), 0:D], tab[:, tiles(b), 0:D]))
                    ch.wait()
                    ch(v.tensor_tensor(out=tA, in0=tA, in1=dis[:, tiles(b)].unsqueeze(2).to_broadcast([P, BT, D]), op=ALU.mult))
                    ch.wait()
                    ch(v.tensor_tensor(out=tA, in0=tA, in1=bg2[:, :].unsqueeze(1).to_broadcast([P, BT, D]), op=ALU.add))
                    ch.wait()
                    ch(v.tensor_add(tY, tA, xs[:, tiles(b), :]))
                    layer_norm(ch, b, tY, [flat(tab[:, bass.ds(b * BT + u, 1), 0:D]) for u in range(BT)], n5_var, n5_std)[-1].then_inc(n5_done, 1)
                    dve.wait_ge(n5_done, b + 1)
                    assert ch.n == N5

            @block.scalar
            def _(act):
                with act.Fori(0, NB) as b:
                    root(act, b, n5_var, n5_std)

            @block.sync
            def _(sp):
                with sp.Fori(0, NB) as b:
                    sp.wait_ge(n5_done, b + 1)
                    sp.dma_start(out.rearrange("(t p) c -> p t c", p=P)[:, tiles(b), :], tab[:, tiles(b), 0:D]).then_inc(n5_out, 16)
                sp.wait_ge(n5_out, 16 * NB)


_WEIGHTS = ["L0_gnn_W_att_w", "L0_gnn_W_att_b", "L0_gnn_W1_w", "L0_gnn_W1_b", "L0_gnn_W2_w", "L0_gnn_W2_b", "L0_gnn_a",
            "L1_gnn_Wq", "L1_gnn_Wk", "L1_gnn_Wv", "L1_gnn_We", "L1_gnn_Wo", "L1_gnn_bo", "L1_gnn_Wm", "L1_gnn_bm",
            "L2_gnn_We1", "L2_gnn_be1", "L2_gnn_We2", "L2_gnn_be2", "L2_gnn_Wn1", "L2_gnn_bn1", "L2_gnn_Wn2", "L2_gnn_bn2",
            "L3_gnn_W1", "L3_gnn_b1", "L3_gnn_W2", "L3_gnn_b2"]


def kernel(**inputs):
    import numpy as _np
    import concourse.bacc as _bacc
    from concourse import mybir as _mybir
    from concourse.bass_utils import run_bass_kernel_spmd as _run

    a = {k: _np.asarray(v) for k, v in inputs.items()}

    def tiled(v, fill):
        padded = _np.full(ET * P, fill, v.dtype)
        padded[:E] = v
        return padded.reshape(ET, P)

    arrays = {"x": _np.concatenate([a["x"], _np.zeros((NP - N, D), a["x"].dtype)]),
              "edge_i": _np.concatenate([tiled(a["src"], 0), tiled(a["dst"], PAD_DST)], axis=1),
              "edge_f": _np.concatenate([tiled(a["edge_weight"], 0)] + [tiled(a["edge_attr_3"][:, c], 0) for c in range(3)], axis=1)}
    arrays.update({w: a[w] for w in _WEIGHTS})
    arrays = {f"in_{k}": _np.ascontiguousarray(v) for k, v in arrays.items()}
    nc = _bacc.Bacc("TRN2", target_bir_lowering=False, num_devices=1)
    args = [nc.dram_tensor(k, v.shape, _mybir.dt.from_np(v.dtype), kind="ExternalInput").ap() for k, v in arrays.items()]
    out = nc.dram_tensor("out_nodes", (NP, D), F32, kind="ExternalOutput").ap()
    build(nc, *args, out)
    r = _run(nc, [arrays], core_ids=[0])
    return r.results[0]["out_nodes"][:N]
```

```python
import concourse.bass as bass
from concourse import mybir
from contextlib import ExitStack

F32 = mybir.dt.float32
BF16 = mybir.dt.bfloat16
I32 = mybir.dt.int32
U32 = mybir.dt.uint32
ALU = mybir.AluOpType
ACT = mybir.ActivationFunctionType
AX = mybir.AxisListType

P = 128
D = 128
N, E = 6250, 100000
ET = -(-E // P)
BT = 4
NT = -(-N // (P * BT)) * BT
NB = NT // BT
NP = NT * P
G = 4
RING = 4
USED = -(-N // P)
STEPS = -(-(ET + USED - 1) // (G * RING)) * G * RING
GROUPS = STEPS // G
ITERS = GROUPS // RING
SB = -(-STEPS // P)
COLS = SB * P
AW = 132
H, HD = 4, 32
EH = 64
PAD_DST = 1 << 20
FAR = 8192
SCALE = float(HD) ** -0.5
EPS = 1e-5
BIG = 1e30


class Chain:

    def __init__(self, eng, sem, base=0):
        self.eng, self.sem, self.base, self.n = eng, sem, base, 0

    def __call__(self, instruction):
        self.n += 1
        return instruction.then_inc(self.sem, 1)

    def wait(self):
        self.eng.wait_ge(self.sem, self.base + self.n)


def edge_rounds(eng, body):
    for g in range(RING):
        body(0, g, g, RING)
    with eng.Fori(1, ITERS - 1) as i:
        for g in range(RING):
            body(i, g, RING, RING)
    for g in range(RING):
        body(ITERS - 1, g, RING, RING - 1 - g)


def later(i, g, by):
    return i + (g + by) // RING, (g + by) % RING


def build(nc, x, edge_i, edge_f, W_att_w, W_att_b, W1_w, W1_b, W2_w, W2_b, a_vec,
          Wq, Wk, Wv, We, Wo, bo, Wm, bm, We1, be1, We2, be2, Wn1, bn1, Wn2, bn2,
          G1, g1b, G2, g2b, out):
    ctx = ExitStack()
    with ctx:
        def sb(name, shape, dt=F32):
            return ctx.enter_context(nc.sbuf_tensor(name, shape, dt))

        early, early_sems = ExitStack(), []

        def sem(name, early_only=True):
            if early_only and early_sems is not None:
                early_sems.append(early.enter_context(nc.semaphore(name)))
                return early_sems[-1]
            return ctx.enter_context(nc.semaphore(name))

        def dram(name, shape):
            return nc.dram_tensor(name, shape, F32, kind="Internal").ap()

        t0 = dram("table_attention", [NP, AW])
        t1 = dram("table_key_value", [NP, 2 * D])
        t2 = dram("table_edge_mlp", [NP, EH])
        t3 = dram("table_gcn1", [NP, D])
        t4 = dram("table_gcn2", [NP, D])
        mlp_sum = [dram(f"mlp_sum{u}", [NP + P, EH]) for u in range(G)]
        step_node_dram = nc.dram_tensor("step_node_dram", [COLS], I32, kind="Internal").ap()

        xs = sb("x_nodes", [P, NT, D])
        acc = sb("acc", [P, NT, AW])
        tab = sb("tab", [P, NT, AW])
        look = sb("look", [P, NT, 3 * D], BF16)
        dst_score = look[:, 0:NT, :].rearrange("p t c -> p (t c)").bitcast(F32)[:, 0:NP]
        dis = sb("dis", [P, NT])
        neg_max = sb("neg_max", [P, NT + G - 1])
        src_i = sb("src_i", [P, COLS], I32)
        rel = sb("rel", [P, COLS])
        ew = sb("ew", [P, COLS])
        key = sb("key", [P, COLS])
        step_node = sb("step_node", [1, COLS], I32)
        ring = sb("ring", [P, RING * G, 2 * D])
        idx_now = sb("idx_now", [P, RING * G], I32)
        rel_now = sb("rel_now", [P, RING * G])
        ew_now = sb("ew_now", [P, RING * G])
        key_now = sb("key_now", [P, RING * G])
        bias_now = sb("bias_now", [P, RING, G * H])
        hot = sb("hot", [P, RING, G, P], BF16)
        hotf = sb("hotf", [P, RING, G, P])
        hotT = sb("hotT", [P, RING, G * P], BF16)
        wide = sb("wide", [P, RING, G, AW])
        lg = sb("lg", [P, RING, 2, G * H])
        small = sb("small", [P, RING, 8 * G])
        junk = sb("junk", [P, 2, G * D])
        put_i = sb("put_i", [P, RING, G], I32)
        iota_i = sb("iota_i", [P, P], I32)
        iota = sb("iota", [P, P])
        iota_b = sb("iota_b", [P, P], BF16)
        ident = sb("ident", [P, P])
        ident_b = sb("ident_b", [P, P], BF16)
        tri = sb("tri", [P, P])
        part_i = sb("part_i", [P, SB], I32)
        part = sb("part", [P, SB])
        far = sb("far", [P, 2])
        ones = sb("ones", [P, P])
        eps = sb("eps", [P, 1])
        w_in = sb("w_in", [P, 3, D])
        a2 = sb("a2", [P, 2])
        ab = sb("ab", [P, 1])
        w0 = sb("w0", [P, AW])
        wad = sb("wad", [P, 4])
        b0 = sb("b0", [P, AW])
        w2T = sb("w2T", [P, D])
        b2 = sb("b2", [P, D])
        wkv = sb("wkv", [P, 2 * D])
        wq = sb("wq", [P, D])
        web = sb("web", [P, 3 * H])
        wo = sb("wo", [P, D])
        boc = sb("boc", [P, 1])
        wm = sb("wm", [P, 2, D])
        bmb = sb("bmb", [P, D])
        we1 = sb("we1", [P, 2, EH])
        be1b = sb("be1b", [P, EH])
        we2 = sb("we2", [EH + 1, EH])
        wn1 = sb("wn1", [P, 2, D])
        bn1c = sb("bn1c", [P, 1])
        wn2 = sb("wn2", [P, D])
        bn2b = sb("bn2b", [P, D])
        wg1 = sb("wg1", [P, D])
        wg2 = sb("wg2", [P, D])
        bg1c = sb("bg1c", [P, 1])
        bg2 = sb("bg2", [P, D])
        ringf = ring[:, :, :].rearrange("p a b -> p (a b)")
        tA, tB, tC, tX, tN, tY = (ringf[:, n * BT * D:(n + 1) * BT * D].rearrange("p (t d) -> p t d", t=BT) for n in range(6))
        tT0 = ringf[:, 6 * BT * D:6 * BT * D + BT * AW].rearrange("p (t c) -> p t c", t=BT)
        tT2 = ringf[:, 6 * BT * D:6 * BT * D + BT * EH].rearrange("p (t c) -> p t c", t=BT)
        tS = ringf[:, 6 * BT * D:6 * BT * D + G * BT * EH].rearrange("p (u t f) -> p u t f", u=G, t=BT)
        tKV = ringf[:, 6 * BT * D:8 * BT * D].rearrange("p (t d) -> p t d", t=BT)
        rT = hotf[:, :, :, :].rearrange("p a b c -> p a (b c)")
        stat = sb("stat", [P, BT, 8])
        mv = sb("mv", [P, BT, 2])
        rs = sb("rs", [P, NT, 2 * H])
        top = sb("top", [1, 4])
        kv_row = ew[0:1, 0:ET]
        last_i = key[0:1, 0:ET].bitcast(I32)
        tabf = tab[:, :, :].rearrange("p t c -> p (t c)")
        got_f = tabf[:, 0:SB * 4 * P].rearrange("p (b c) -> p b c", b=SB)
        lookf = look[:, :, :].rearrange("p t c -> p (t c)").bitcast(F32)
        got_if = lookf[:, COLS:COLS + SB * 2 * P].rearrange("p (b c) -> p b c", b=SB)
        got_i = tabf[:, SB * 4 * P:SB * 6 * P].bitcast(I32).rearrange("p (b c) -> p b c", b=SB)
        bias = tabf[:, 0:COLS * H].rearrange("p (s h) -> p s h", h=H)
        accf = acc[:, :, :].rearrange("p t c -> p (t c)")
        keys = accf[:, 0:ET]
        one_row = accf[:, ET:2 * ET]
        attr = [accf[:, 2 * ET + c * COLS:2 * ET + (c + 1) * COLS] for c in range(3)]
        src_f = accf[:, 2 * ET + 3 * COLS:2 * ET + 4 * COLS]
        ok_row = lookf[:, 0:COLS]

        bank = [ctx.enter_context(nc.psum_tensor(f"bank{n}", [P, 512], F32)) for n in range(8)]

        rounds = sem("gather_rounds", False)
        gathered = [sem(f"gathered{g}", False) for g in range(RING)]
        scattered = [sem(f"scattered{u}", False) for u in range(G)]
        gcount = [0]

        v, s_, t_, q_ = nc.vector, nc.scalar, nc.tensor, nc.gpsimd

        loaded_dst, loaded_w, loaded_x = sem("loaded_dst"), sem("loaded_w"), sem("loaded_x")
        iota_made, const_made = sem("iota_made"), sem("const_made")
        prep_v = sem("prep_vector")
        node_out, steps_got, keys_done, tiles_done = sem("node_out"), sem("steps_got"), sem("keys_done"), sem("tiles_done")
        rows_ready, rows_T, rows_kept = sem("rows_ready"), sem("rows_T"), sem("rows_kept")
        w_T, zero_made, node_in = sem("w_T"), sem("zero_made"), sem("node_in")
        tile_row_done, keys_T = sem("tile_row_done"), sem("keys_T")

        NW = [0]
        with nc.Block() as block:
            @block.sync
            def _(sp):
                with nc.allow_non_contiguous_dma(reason="last dst of each tile, columns of biases"):
                    sp.dma_start(last_i[:, :], edge_i[:, 2 * P - 1:2 * P].rearrange("t one -> one t")).then_inc(loaded_dst, 16)

                    def w(dst, src):
                        NW[0] += 16
                        sp.dma_start(dst, src).then_inc(loaded_w, 16)

                    def row(dst, vec):
                        w(dst, vec.partition_broadcast(P))

                    w(w_in[:, 0, :], W_att_w)
                    w(w_in[:, 1, :], W1_w)
                    w(w_in[:, 2, :], W2_w)
                    w(a2[:, :], a_vec.rearrange("(c o) one -> o (c one)", c=2))
                    w(ab[:, :], W_att_b.rearrange("(o one) -> o one", one=1))
                    row(b0[:, 0:D], W1_b)
                    row(b2[:, :], W2_b)
                    w(wkv[:, 0:D], Wk)
                    w(wkv[:, D:2 * D], Wv)
                    w(wq[:, :], Wq)
                    row(web[:, :], We.rearrange("c h -> (c h)"))
                    w(wo[:, :], Wo)
                    w(boc[:, :], bo.rearrange("(o one) -> o one", one=1))
                    w(wm[:, :, :], Wm.rearrange("(c p) o -> p c o", p=P))
                    row(bmb[:, :], bm)
                    w(we1[:, :, :], We1.rearrange("(c p) o -> p c o", p=P))
                    row(be1b[:, :], be1)
                    w(we2[0:EH, :], We2)
                    w(we2[EH:EH + 1, :], be2.rearrange("(one o) -> one o", one=1))
                    w(wn1[:, 0, :], Wn1[0:D, :])
                    w(wn1[0:EH, 1, :], Wn1[D:D + EH, :])
                    w(bn1c[:, :], bn1.rearrange("(o one) -> o one", one=1))
                    w(wn2[:, :], Wn2)
                    row(bn2b[:, :], bn2)
                    w(wg1[:, :], G1)
                    w(wg2[:, :], G2)
                    w(bg1c[:, :], g1b.rearrange("(o one) -> o one", one=1))
                    row(bg2[:, :], g2b)
                    sp.dma_start(xs[:, :, :], x.rearrange("(t p) d -> p t d", p=P)).then_inc(loaded_x, 16)
                    sp.wait_ge(tiles_done, 1)
                    sp.dma_start(step_node_dram.rearrange("(b p) -> p b", p=P), part_i[:, :]).then_inc(node_out, 16)
                    sp.wait_ge(node_out, 16)
                    sp.dma_start(step_node[:, :], step_node_dram.rearrange("(one s) -> one s", one=1)).then_inc(node_in, 16)
                sp.wait_ge(loaded_x, 16)
                sp.wait_ge(loaded_w, NW[0])
                sp.wait_ge(node_in, 16)

            @block.gpsimd
            def _(pool):
                q_.iota(iota_i[:, :], pattern=[[1, P]], base=0, channel_multiplier=0).then_inc(iota_made, 1)
                q_.iota(part_i[:, :], pattern=[[P, SB]], base=0, channel_multiplier=1).then_inc(iota_made, 1)
                q_.iota(src_i[0:1, 0:ET], pattern=[[1, ET]], base=0, channel_multiplier=0).then_inc(iota_made, 1)
                q_.memset(ident[:, :], 0.0).then_inc(iota_made, 1)
                pool.wait_ge(iota_made, 4)
                q_.affine_select(out=ident[:, :], in_=ident[:, :], compare_op=ALU.not_equal, fill=1.0,
                                 base=0, pattern=[[-1, P]], channel_multiplier=1).then_inc(const_made, 1)
                q_.memset(ring[:, :, :], 0.0).then_inc(zero_made, 1)
                pool.wait_ge(zero_made, 1)
                zeros = ring[:, :, :].rearrange("p a b -> p (a b)")[:, 0:(NT + 1) * EH].rearrange("p (t f) -> p t f", f=EH)
                for u in range(G):
                    pool.dma_start(mlp_sum[u].rearrange("(t p) f -> p t f", p=P), zeros).then_inc(scattered[u], 16)
                pool.wait_ge(keys_done, 1)
                for b in range(SB):
                    at = bass.IndirectOffsetOnAxis(ap=put_i[:, :, :].rearrange("p a b -> p (a b)")[:, b:b + 1].bitcast(U32), axis=0)
                    q_.indirect_dma_start(got_i[:, b, :], None, edge_i, at).then_inc(steps_got, 16)
                    q_.indirect_dma_start(got_f[:, b, :], None, edge_f, at).then_inc(steps_got, 16)
                for u in range(G):
                    pool.wait_ge(scattered[u], 16)

            @block.vector
            def _(dve):
                ch = Chain(dve, prep_v)
                dve.wait_ge(iota_made, 3)
                ch(v.tensor_copy(iota[:, :], iota_i[:, :]))
                ch(v.tensor_copy(part[:, :], part_i[:, :]))
                ch(v.memset(ones[:, :], 1.0))
                ch(v.memset(eps[:, :], EPS))
                ch(v.memset(one_row[:, :], 1.0))
                ch(v.tensor_copy(kv_row[:, :], src_i[0:1, 0:ET]))
                dve.wait_ge(loaded_dst, 16)
                ch(v.tensor_scalar(out=last_i[:, :], in0=last_i[:, :], scalar1=7, scalar2=None, op0=ALU.logical_shift_right))
                ch.wait()
                ch(v.tensor_copy(junk[0:1, :, :].rearrange("p a b -> p (a b)")[:, 0:ET], last_i[:, :]))
                ch(v.tensor_copy(iota_b[:, :], iota[:, :]))
                ch.wait()
                ch(v.tensor_scalar(out=tri[:, :], in0=iota[:, :], scalar1=part[:, 0:1], scalar2=None, op0=ALU.is_lt))
                ch(v.tensor_scalar(out=far[:, 0:1], in0=part[:, 0:1], scalar1=float(FAR), scalar2=None, op0=ALU.add))
                ch(v.tensor_scalar(out=far[:, 1:2], in0=part[:, 0:1], scalar1=float(NP), scalar2=None, op0=ALU.add))
                v.tensor_add(kv_row[:, :], kv_row[:, :], junk[0:1, :, :].rearrange("p a b -> p (a b)")[:, 0:ET]).then_inc(tile_row_done, 1)
                dve.wait_ge(const_made, 1)
                ch(v.tensor_copy(ident_b[:, :], ident[:, :]))
                dve.wait_ge(keys_T, 1)
                ch(v.tensor_copy(keys[:, 0:512], bank[0][:, 0:512]))
                ch(v.tensor_copy(keys[:, 512:ET], bank[1][:, 0:ET - 512]))
                ch.wait()
                for b in range(SB):
                    ch(v.scalar_tensor_tensor(out=tabf[:, b * ET:(b + 1) * ET], in0=keys[:, :], scalar=part[:, b:b + 1],
                                              in1=one_row[:, :], op0=ALU.is_lt, op1=ALU.mult,
                                              accum_out=small[:, 0, b:b + 1]))
                ch.wait()
                ch(v.tensor_scalar(out=small[:, 1, 0:SB], in0=small[:, 0, 0:SB], scalar1=float(ET - 1), scalar2=None, op0=ALU.min))
                ch.wait()
                v.tensor_copy(put_i[:, :, :].rearrange("p a b -> p (a b)")[:, 0:SB], small[:, 1, 0:SB]).then_inc(keys_done, 1)
                ch(v.tensor_sub(small[:, 2, 0:SB], part[:, :], small[:, 1, 0:SB]))
                ch.wait()
                ch(v.tensor_scalar(out=small[:, 0, 0:SB], in0=small[:, 2, 0:SB], scalar1=float(NT - 1), scalar2=None, op0=ALU.min))
                ch.wait()
                v.tensor_copy(part_i[:, :], small[:, 0, 0:SB]).then_inc(tiles_done, 1)
                ch(v.tensor_scalar(out=small[:, 3, 0:SB], in0=small[:, 2, 0:SB], scalar1=float(P), scalar2=None, op0=ALU.mult))
                dve.wait_ge(steps_got, 32 * SB)
                ch(v.tensor_copy(got_if, got_i))
                ch.wait()
                for b in range(SB):
                    last = v.tensor_scalar(out=got_if[:, b, P:2 * P], in0=got_if[:, b, P:2 * P],
                                           scalar1=small[:, 3, b:b + 1], scalar2=None, op0=ALU.subtract)
                last.then_inc(rows_ready, 1)
                for b in range(SB):
                    at = slice(b * P, (b + 1) * P)
                    dve.wait_ge(rows_T, b + 1)
                    c0, c1 = bank[2 * (b % 2)], bank[2 * (b % 2) + 1]
                    ch(v.tensor_copy(src_f[:, at], c0[:, 0:P]))
                    ch(v.tensor_copy(rel[:, at], c0[:, P:2 * P]))
                    ch(v.tensor_copy(ew[:, at], c0[:, 2 * P:3 * P]))
                    ch(v.tensor_copy(attr[0][:, at], c0[:, 3 * P:4 * P]))
                    ch(v.tensor_copy(attr[1][:, at], c1[:, 0:P]))
                    v.tensor_copy(attr[2][:, at], c1[:, P:2 * P]).then_inc(rows_kept, 1)
                dve.wait_ge(rows_kept, SB)
                ch.wait()
                ch(v.tensor_copy(src_i[:, :], src_f))
                ch(v.tensor_scalar(out=ok_row, in0=rel[:, :], scalar1=0.0, scalar2=None, op0=ALU.is_ge))
                ch.wait()
                ch(v.scalar_tensor_tensor(out=ok_row, in0=rel[:, :], scalar=float(P), in1=ok_row, op0=ALU.is_lt, op1=ALU.mult))
                ch.wait()
                ch(v.scalar_tensor_tensor(out=key[:, :], in0=src_f, scalar=far[:, 0:1], in1=ok_row, op0=ALU.subtract, op1=ALU.mult))
                ch.wait()
                ch(v.tensor_scalar(out=key[:, :], in0=key[:, :], scalar1=far[:, 0:1], scalar2=None, op0=ALU.add))
                ch(v.tensor_scalar(out=ok_row, in0=ok_row, scalar1=-1.0, scalar2=BIG, op0=ALU.add, op1=ALU.mult))
                dve.wait_ge(loaded_w, NW[0])
                for h in range(H):
                    ch.wait()
                    ch(v.scalar_tensor_tensor(out=bias[:, :, h], in0=attr[0], scalar=web[:, h:h + 1], in1=ok_row, op0=ALU.mult, op1=ALU.add))
                for c in (1, 2):
                    for h in range(H):
                        ch.wait()
                        ch(v.scalar_tensor_tensor(out=bias[:, :, h], in0=attr[c], scalar=web[:, c * H + h:c * H + h + 1],
                                                  in1=bias[:, :, h], op0=ALU.mult, op1=ALU.add))
                ch(v.memset(neg_max[:, :], BIG))
                ch(v.memset(top[:, :], -BIG))
                ch.wait()
                ch(v.memset(acc[:, :, :], 0.0))
                ch(v.memset(b0[:, D:D + 1], 1.0))
                ch(v.memset(b0[:, D + 2:AW], 0.0))
                ch(v.memset(w0[:, D:AW], 0.0))
                ch.wait()
                dve.wait_ge(w_T, 1)
                ch(v.tensor_copy(w0[:, 0:D], bank[4][:, 0:D]))
                ch(v.tensor_copy(w2T[:, :], bank[4][:, D:2 * D]))
                ch(v.tensor_copy(w0[:, D + 1:D + 2], bank[5][:, 0:1]))
                ch(v.tensor_copy(wad[:, 0:1], bank[5][:, 1:2]))
                ch(v.tensor_copy(b0[:, D + 1:D + 2], bank[5][:, 2:3]))
                ch(v.tensor_copy(wad[:, 1:2], bank[5][:, 3:4]))
                ch.wait()

            @block.tensor
            def _(pe):
                pe.wait_ge(tile_row_done, 1)
                t_.matmul(bank[0][:, 0:512], ones[0:1, :], kv_row[:, 0:512], start=True, stop=True)
                t_.matmul(bank[1][:, 0:ET - 512], ones[0:1, :], kv_row[:, 512:ET], start=True, stop=True).then_inc(keys_T, 1)
                pe.wait_ge(const_made, 1)
                pe.wait_ge(loaded_w, NW[0])
                t_.transpose(bank[4][:, 0:D], w_in[:, 1, :], ident[:, :])
                t_.transpose(bank[4][:, D:2 * D], w_in[:, 2, :], ident[:, :])
                t_.matmul(bank[5][:, 0:2], w_in[:, 0, :], a2[:, :], start=True, stop=True)
                t_.matmul(bank[5][:, 2:4], ab[:, 0:1].to_broadcast([P, P]), a2[:, :], start=True, stop=True).then_inc(w_T, 1)
                pe.wait_ge(rows_ready, 1)
                for b in range(SB):
                    if b >= 2:
                        pe.wait_ge(rows_kept, b - 1)
                    c0, c1 = bank[2 * (b % 2)], bank[2 * (b % 2) + 1]
                    t_.transpose(c0[:, 0:P], got_if[:, b, 0:P], ident[:, :])
                    t_.transpose(c0[:, P:2 * P], got_if[:, b, P:2 * P], ident[:, :])
                    t_.transpose(c0[:, 2 * P:3 * P], got_f[:, b, 0:P], ident[:, :])
                    t_.transpose(c0[:, 3 * P:4 * P], got_f[:, b, P:2 * P], ident[:, :])
                    t_.transpose(c1[:, 0:P], got_f[:, b, 2 * P:3 * P], ident[:, :])
                    t_.transpose(c1[:, P:2 * P], got_f[:, b, 3 * P:4 * P], ident[:, :]).then_inc(rows_T, 1)

        def tiles(b):
            return bass.ds(b * BT, BT)

        def flat(a):
            return a.rearrange("p a b -> p (a b)")

        def arrived(eng, i, g):
            eng.wait_ge(gathered[g], 16 * G * (gcount[0] + i + 1))

        def place(k, g, placed, *columns):
            for now, every in columns + ((idx_now, src_i),):
                last = s_.copy(now[:, g * G:(g + 1) * G], every[:, bass.ds(k * G, G)])
            last.then_inc(placed, 1)

        def gather(pool, k, g, table, width, placed, table_out):
            pool.wait_ge(table_out, 16 * NB)
            pool.wait_ge(placed, k + 1)
            pool.sem_inc(rounds, 1)
            for u in range(G):
                slot = g * G + u
                q_.indirect_dma_start(ring[:, slot, 0:width], None, table, bass.IndirectOffsetOnAxis(
                    ap=idx_now[:, slot:slot + 1].bitcast(U32), axis=0)).then_inc(gathered[g], 16)

        def node_regs(eng, name):
            return [[eng.alloc_register(f"{name}{j}{u}") for u in range(G)] for j in range(2)]

        def load_nodes(eng, regs, k, g):
            eng.reg_load(regs[g % 2], step_node[0:1, bass.ds(k * G, G)])

        def nodes_of(eng, regs, g):
            return [eng.snap(r, min_val=0, max_val=NT - 1) for r in regs[g % 2]]

        def hots(g):
            return dict(in0=iota[:, :].unsqueeze(1).to_broadcast([P, G, P]),
                        in1=rel_now[:, g * G:(g + 1) * G].unsqueeze(2).to_broadcast([P, G, P]), op=ALU.is_equal)

        def batch_rounds(eng, batch):
            batch(0, True, False)
            with eng.Fori(1, NB - 1) as b:
                batch(b, False, False)
            batch(NB - 1, False, True)

        NORM = BT + 1

        def norm_stats(ch, y, var):
            ch.wait()
            for u in range(BT):
                ch(v.bn_stats(out=stat[:, u, 0:6], in_=y[:, u, :]))
            ch.wait()
            ch.eng.sem_inc(rounds, 1)
            for u in range(BT):
                last = v.bn_aggr(out=mv[:, u, :], in_=stat[:, u, 0:6])
            last.then_inc(var, 1)

        def normalize(ch, b, y, outs, std):
            ch.eng.wait_ge(std, b + 1)
            ch(v.reciprocal(stat[:, :, 6], stat[:, :, 6]))
            ch.wait()
            for u in range(BT):
                last = v.tensor_scalar(out=outs[u], in0=y[:, u, :], scalar1=mv[:, u, 0:1], scalar2=stat[:, u, 6:7],
                                       op0=ALU.subtract, op1=ALU.mult)
            return last

        def layer_norm(ch, b, y, outs, var, std):
            norm_stats(ch, y, var)
            return normalize(ch, b, y, outs, std)

        def root(act, b, var, std):
            act.wait_ge(var, b + 1)
            s_.activation(stat[:, :, 6], mv[:, :, 1], ACT.Sqrt, bias=eps[:, 0:1]).then_inc(std, 1)

        x_staged, x_T, xT_kept, t0_mm, t0_kept, score_mm, t0_out, t0_free = (
            sem(f"n0_{n}") for n in ("x_staged", "x_T", "xT_kept", "t0_mm", "t0_kept", "score_mm", "t0_out", "t0_free"))
        with nc.Block() as block:
            @block.gpsimd
            def _(pool):
                pool.sem_inc(x_T, 1)
                with pool.Fori(0, NB) as b:
                    pool.wait_ge(x_T, b + 1)
                    pool.sem_inc(rounds, 1)
                    q_.tensor_copy(tX[:, :, :], xs[:, tiles(b), :]).then_inc(x_staged, 1)

            @block.tensor
            def _(pe):
                with pe.Fori(0, NB) as b:
                    pe.wait_ge(x_staged, b + 1)
                    for u in range(BT):
                        last = t_.transpose(bank[0][:, u * P:(u + 1) * P], tX[:, u, :], ident[:, :])
                    last.then_inc(x_T, 1)
                    pe.wait_ge(xT_kept, b + 1)
                    pe.wait_ge(t0_kept, b + 1)
                    for u in range(BT):
                        last = t_.matmul(bank[1 + u // 2][:, (u % 2) * AW:(u % 2 + 1) * AW],
                                         rT[:, 0, u * P:(u + 1) * P], w0[:, :], start=True, stop=True)
                    last.then_inc(t0_mm, 1)
                    t_.matmul(bank[3][:, :], wad[:, 0:1].to_broadcast([P, P]), rT[:, 0, :], start=True, stop=True).then_inc(score_mm, 1)

            @block.scalar
            def _(act):
                with act.Fori(0, NB) as b:
                    act.wait_ge(x_T, b + 2)
                    s_.copy(rT[:, 0, :], bank[0][:, :]).then_inc(xT_kept, 1)
                    act.wait_ge(score_mm, b + 1)
                    s_.activation(dst_score[:, bass.ds(b * BT * P, BT * P)], bank[3][:, :], ACT.Identity, bias=wad[:, 1:2])

            @block.vector
            def _(dve):
                dve.sem_inc(t0_kept, 1)
                with dve.Fori(0, NB) as b:
                    dve.wait_ge(t0_mm, b + 1)
                    dve.wait_ge(t0_free, b + 1)
                    for j in range(2):
                        last = v.tensor_add(tT0[:, 2 * j:2 * j + 2, :],
                                            bank[1 + j][:, 0:2 * AW].rearrange("p (t c) -> p t c", t=2),
                                            b0[:, :].unsqueeze(1).to_broadcast([P, 2, AW]))
                    last.then_inc(t0_kept, 1)

            @block.sync
            def _(sp):
                sp.sem_inc(t0_free, 1)
                with sp.Fori(0, NB) as b:
                    sp.wait_ge(t0_kept, b + 2)
                    sp.dma_start(t0.rearrange("(t p) c -> p t c", p=P)[:, tiles(b), :], tT0[:, :, :]).then_inc(t0_out, 16)
                    sp.wait_ge(t0_out, 16 * b + 16)
                    sp.sem_inc(t0_free, 1)

        l0_placed, l0_logit, l0_wide, l0_sum, l0_acc, l0_v, l0_p = (
            sem(f"l0_{n}") for n in ("placed", "logit", "wide", "sum", "acc", "vector", "prob"))
        with nc.Block() as block:
            @block.gpsimd
            def _(pool):
                with pool.Fori(0, ITERS) as i:
                    for g in range(RING):
                        gather(pool, i * RING + g, g, t0, AW, l0_placed, t0_out)

            @block.scalar
            def _(act):
                for k in range(RING):
                    place(k, k, l0_placed, (rel_now, rel), (ew_now, ew))
                with act.Fori(0, ITERS) as i:
                    for g in range(RING):
                        k = i * RING + g
                        act.wait_ge(l0_logit, k + 1)
                        s_.activation(small[:, g, 0:G], lg[:, g, 1, 0:G], ACT.Exp).then_inc(l0_p, 1)
                        s_.copy(wide[:, g, :, D + 1], ew_now[:, g * G:(g + 1) * G])
                        act.wait_ge(l0_p, k + 1)
                        for u in range(G):
                            last = s_.activation(wide[:, g, u, 0:D + 1], ring[:, g * G + u, 0:D + 1], ACT.Identity,
                                                 scale=small[:, g, u:u + 1])
                        last.then_inc(l0_wide, 1)
                        act.wait_ge(l0_wide, k + 1)
                        place(k + RING, g, l0_placed, (rel_now, rel), (ew_now, ew))

            @block.tensor
            def _(pe):
                with pe.Fori(0, ITERS) as i:
                    for g in range(RING):
                        k = i * RING + g
                        pe.wait_ge(l0_wide, k + 1)
                        pe.wait_ge(l0_acc, k * G + G)
                        for u in range(G):
                            last = t_.matmul(bank[2 * (g % 2) + u // 2][:, (u % 2) * AW:(u % 2) * AW + D + 2],
                                             hotf[:, g, u, :], wide[:, g, u, 0:D + 2], start=True, stop=True)
                        last.then_inc(l0_sum, 1)

            @block.vector
            def _(dve):
                regs = node_regs(dve, "l0_node")

                def front(i, g):
                    k = i * RING + g
                    ch = Chain(dve, l0_v, 2 * k)
                    load_nodes(dve, regs, k, g)
                    nodes = nodes_of(dve, regs, g)
                    dve.wait_ge(l0_placed, k + 1)
                    v.tensor_tensor(out=hotf[:, g, :, :], **hots(g))
                    for u in range(G):
                        last = v.scalar_tensor_tensor(out=junk[:, 0, u * P:(u + 1) * P], in0=iota[:, :],
                                                      scalar=rel_now[:, g * G + u:g * G + u + 1],
                                                      in1=dst_score[:, bass.ds(nodes[u] * P, P)],
                                                      op0=ALU.is_equal, op1=ALU.mult, accum_out=small[:, g, G + u:G + u + 1])
                    ch(last)
                    arrived(dve, i, g)
                    ch.wait()
                    ch(v.tensor_add(lg[:, g, 0, 0:G], ring[:, g * G:(g + 1) * G, D + 1], small[:, g, G:2 * G]))
                    ch.wait()
                    v.scalar_tensor_tensor(out=lg[:, g, 1, 0:G], in0=lg[:, g, 0, 0:G], scalar=0.01, in1=lg[:, g, 0, 0:G],
                                           op0=ALU.mult, op1=ALU.max).then_inc(l0_logit, 1)

                def back(i, g):
                    k = i * RING + g
                    nodes = nodes_of(dve, regs, g)
                    dve.wait_ge(l0_sum, k + 1)
                    for u in range(G):
                        here = flat(acc[:, bass.ds(nodes[u], 1), 0:D + 2])
                        dve.wait_ge(l0_acc, k * G + 2 * G + u)
                        v.tensor_add(here, here, bank[2 * (g % 2) + u // 2][:, (u % 2) * AW:(u % 2) * AW + D + 2]).then_inc(l0_acc, 1)

                def both(i, g, past, left):
                    if left:
                        front(*later(i, g, 1))
                    back(i, g)

                dve.sem_inc(l0_acc, 2 * G)
                front(0, 0)
                edge_rounds(dve, both)
        gcount[0] += ITERS


        (n1_hn, n1_c, n1_prod, n1_prodT, n1_prodT_kept, n1_mm, n1_xn, n1_xnT, n1_xnT_kept, n1_kv_mm, n1_q_mm, n1_kv_kept, n1_q0,
         n1_cx, n1_q_rest, n1_q1, t1_out, t1_free, n1_copied, n1_v, n1_deg, n1_dis, n1_var, n1_std) = (sem(f"n1_{n}") for n in (
             "hn", "c", "prod", "prodT", "prodT_kept", "mm", "xn", "xnT", "xnT_kept", "kv_mm", "q_mm", "kv_kept", "q0",
             "c_x", "q_rest", "q1", "t1_out", "t1_free", "copied", "vector", "deg", "dis", "var", "std"))
        N1 = 3 + NORM
        with nc.Block() as block:
            @block.vector
            def _(dve):
                def front(b):
                    x_b = xs[:, tiles(b), :]
                    v.tensor_tensor(out=tA, in0=acc[:, tiles(b), 0:D], in1=rs[:, tiles(b), 0:1].to_broadcast([P, BT, D]),
                                    op=ALU.mult).then_inc(n1_hn, 1)
                    dve.wait_ge(n1_hn, b + 1)
                    v.tensor_tensor(out=tB, in0=tA, in1=x_b, op=ALU.mult).then_inc(n1_prod, 1)

                def rest(b):
                    dve.wait_ge(n1_q0, b + 1)
                    v.scalar_tensor_tensor(out=tX, in0=bank[5][:, :].rearrange("p (t d) -> p t d", t=BT), scalar=SCALE,
                                           in1=look[:, tiles(b), 0:D], op0=ALU.mult, op1=ALU.subtract).then_inc(n1_q_rest, 1)

                def last_part(b):
                    dve.wait_ge(n1_q1, b + 1)
                    v.tensor_sub(look[:, tiles(b), 2 * D:3 * D], tX, look[:, tiles(b), D:2 * D])

                def batch(b, first, last):
                    ch = Chain(dve, n1_v, N1 * b + 6)
                    if not first:
                        dve.wait_ge(n1_xn, b)
                    dve.wait_ge(n1_mm, b + 1)
                    dve.wait_ge(n1_c, b + 1)
                    ch(v.tensor_tensor(out=flat(tY), in0=bank[1][:, :], in1=flat(tC), op=ALU.add))
                    ch.wait()
                    ch(v.scalar_tensor_tensor(out=flat(tY), in0=flat(tY), scalar=0.01, in1=flat(tY), op0=ALU.mult, op1=ALU.max))
                    ch.wait()
                    ch(v.tensor_tensor(out=tY, in0=tY, in1=xs[:, tiles(b), :], op=ALU.add))
                    norm_stats(ch, tY, n1_var)
                    if not first:
                        rest(b - 1)
                    if not last:
                        front(b + 1)
                    if not first:
                        last_part(b - 1)
                    dve.wait_ge(n1_copied, b + 1)
                    normalize(ch, b, tY, [tN[:, u, :] for u in range(BT)], n1_std).then_inc(n1_xn, 1)
                    assert ch.n == N1

                ch = Chain(dve, n1_v)
                deg = neg_max[:, 0:NT]
                ch(v.tensor_scalar(out=deg, in0=acc[:, :, D + 1], scalar1=1.0, scalar2=None, op0=ALU.add))
                ch(v.tensor_scalar(out=rs[:, :, 0], in0=acc[:, :, D], scalar1=1e-9, scalar2=None, op0=ALU.add))
                ch.wait()
                v.tensor_scalar(out=dis[:, :], in0=deg, scalar1=1e-12, scalar2=None, op0=ALU.max).then_inc(n1_deg, 1)
                ch(v.reciprocal(rs[:, :, 0], rs[:, :, 0]))
                ch.wait()
                front(0)
                dve.wait_ge(n1_dis, 1)
                ch(v.reciprocal(dis[:, :], dis[:, :]))
                ch.wait()
                ch(v.scalar_tensor_tensor(out=dis[:, :], in0=deg, scalar=0.0, in1=dis[:, :], op0=ALU.is_gt, op1=ALU.mult))
                ch.wait()
                ch(v.memset(neg_max[:, :], BIG))
                assert ch.n == 6
                batch_rounds(dve, batch)
                rest(NB - 1)
                last_part(NB - 1)

            @block.tensor
            def _(pe):
                def front(b):
                    pe.wait_ge(n1_prod, b + 1)
                    for u in range(BT):
                        last = t_.transpose(bank[0][:, u * P:(u + 1) * P], tB[:, u, :], ident[:, :])
                    last.then_inc(n1_prodT, 1)
                    pe.wait_ge(n1_prodT_kept, b + 1)
                    for u in range(BT):
                        last = t_.matmul(bank[1][:, u * P:(u + 1) * P], rT[:, 0, u * P:(u + 1) * P], w2T[:, :], start=True, stop=True)
                    last.then_inc(n1_mm, 1)

                def batch(b, first, last):
                    if not last:
                        front(b + 1)
                    pe.wait_ge(n1_xn, b + 1)
                    for u in range(BT):
                        done = t_.transpose(bank[2][:, u * P:(u + 1) * P], tN[:, u, :], ident[:, :])
                    done.then_inc(n1_xnT, 1)
                    pe.wait_ge(n1_xnT_kept, b + 1)
                    for u in range(BT):
                        done = t_.matmul(bank[5][:, u * P:(u + 1) * P], rT[:, 1, u * P:(u + 1) * P], wq[:, :], start=True, stop=True)
                    done.then_inc(n1_q_mm, 1)
                    pe.wait_ge(n1_kv_kept, b + 1)
                    for u in range(BT):
                        done = t_.matmul(bank[3 + u // 2][:, (u % 2) * 2 * D:(u % 2 + 1) * 2 * D],
                                         rT[:, 1, u * P:(u + 1) * P], wkv[:, :], start=True, stop=True)
                    done.then_inc(n1_kv_mm, 1)

                front(0)
                batch_rounds(pe, batch)

            @block.scalar
            def _(act):
                def front(b):
                    act.wait_ge(n1_prodT, b + 1)
                    s_.copy(rT[:, 0, :], bank[0][:, :]).then_inc(n1_prodT_kept, 1)

                def second_part(b):
                    act.wait_ge(n1_q_rest, b + 1)
                    s_.copy(look[:, tiles(b), D:2 * D], tX).then_inc(n1_q1, 1)

                def batch(b, first, last):
                    root(act, b, n1_var, n1_std)
                    if not first:
                        second_part(b - 1)
                    if not last:
                        front(b + 1)
                    act.wait_ge(n1_xnT, b + 1)
                    s_.copy(rT[:, 1, :], bank[2][:, :]).then_inc(n1_xnT_kept, 1)
                    act.wait_ge(n1_q_mm, b + 1)
                    s_.activation(look[:, tiles(b), 0:D], bank[5][:, :].rearrange("p (t d) -> p t d", t=BT), ACT.Copy,
                                  scale=SCALE).then_inc(n1_q0, 1)
                    act.wait_ge(n1_kv_mm, b + 1)
                    act.wait_ge(t1_free, b + 1)
                    s_.copy(flat(tKV[:, 0:2, :]), bank[3][:, :])
                    s_.copy(flat(tKV[:, 2:4, :]), bank[4][:, :]).then_inc(n1_kv_kept, 1)

                act.sem_inc(n1_kv_kept, 1)
                act.wait_ge(n1_deg, 1)
                s_.activation(dis[:, :], dis[:, :], ACT.Sqrt).then_inc(n1_dis, 1)
                front(0)
                batch_rounds(act, batch)
                second_part(NB - 1)

            @block.gpsimd
            def _(pool):
                def front(b):
                    pool.wait_ge(n1_hn, b + 1)
                    pool.sem_inc(rounds, 1)
                    q_.tensor_tensor(out=tC, in0=tA, in1=xs[:, tiles(b), :], op=ALU.add).then_inc(n1_cx, 1)
                    pool.wait_ge(n1_cx, b + 1)
                    q_.tensor_tensor(out=tC, in0=tC, in1=b2[:, :].unsqueeze(1).to_broadcast([P, BT, D]), op=ALU.add).then_inc(n1_c, 1)

                def batch(b, first, last):
                    if not last:
                        front(b + 1)
                    pool.wait_ge(n1_xn, b + 1)
                    pool.sem_inc(rounds, 1)
                    q_.tensor_copy(xs[:, tiles(b), :], tN).then_inc(n1_copied, 1)

                pool.sem_inc(n1_copied, 1)
                front(0)
                batch_rounds(pool, batch)
                q_.memset(acc[:, :, :], 0.0)

            @block.sync
            def _(sp):
                sp.sem_inc(t1_free, 1)
                with sp.Fori(0, NB) as b:
                    sp.wait_ge(n1_kv_kept, b + 2)
                    sp.dma_start(t1.rearrange("(t p) c -> p t c", p=P)[:, tiles(b), :], tKV).then_inc(t1_out, 16)
                    sp.wait_ge(t1_out, 16 * b + 16)
                    sp.sem_inc(t1_free, 1)

        (l1_placed, l1_away, l1_hot, l1_hotT, l1_hot_kept, l1_q, l1_gm, l1_gmT, l1_top, l1_topB, l1_neg, l1_p, l1_wide, l1_sum,
         l1_v) = (sem(f"l1_{n}") for n in (
             "placed", "away", "hot", "hotT", "hot_kept", "query", "group_max", "group_max_T", "top", "top_spread", "neg_top", "prob",
             "wide", "sum", "vector"))
        l1_acc = [sem(f"l1_acc{u}") for u in range(G)]
        TR, QB, MB, SUM = bank[0], (bank[1], bank[2]), bank[3], 4
        with nc.Block() as block:
            @block.gpsimd
            def _(pool):
                with pool.Fori(0, ITERS) as i:
                    for g in range(RING):
                        gather(pool, i * RING + g, g, t1, 2 * D, l1_placed, t1_out)

            @block.scalar
            def _(act):
                away = junk[:, 1, :]

                def place1(k, g):
                    s_.copy(rel_now[:, g * G:(g + 1) * G], rel[:, bass.ds(k * G, G)])
                    s_.copy(bias_now[:, g, :], tabf[:, bass.ds(k * G * H, G * H)])
                    place(k, g, l1_placed)

                def far_away(i, g, past):
                    k = i * RING + g
                    act.wait_ge(l1_placed, k + 1)
                    if past:
                        act.wait_ge(l1_hot, k)
                    for u in range(G):
                        last = s_.activation(away[:, u * P:(u + 1) * P], iota[:, :], ACT.Abs, scale=-1.0,
                                             bias=rel_now[:, g * G + u:g * G + u + 1])
                    last.then_inc(l1_away, 1)

                def one_hot(i, g, past):
                    k = i * RING + g
                    if past >= RING:
                        act.wait_ge(l1_sum, k - RING + 1)
                    act.wait_ge(l1_away, k + 1)
                    s_.activation(flat(hotf[:, g, :, :]), away, ACT.Relu, scale=-1.0, bias=1.0)
                    s_.activation(flat(hot[:, g, :, :]), away, ACT.Relu, scale=-1.0, bias=1.0).then_inc(l1_hot, 1)

                def keep_hot(i, g):
                    act.wait_ge(l1_hotT, i * RING + g + 1)
                    s_.copy(hotT[:, g, :], TR[:, :].bitcast(BF16)[:, 0:G * P]).then_inc(l1_hot_kept, 1)

                def weights(i, g):
                    act.wait_ge(l1_neg, i * RING + g + 1)
                    s_.activation(wide[:, g, :, D:AW], lg[:, g, 1, :].rearrange("p (u h) -> p u h", u=G), ACT.Exp,
                                  bias=small[:, g, 1:2])
                    s_.activation(small[:, g, 2:3], small[:, (g - 1) % RING, 1:2], ACT.Exp, scale=-1.0,
                                  bias=small[:, g, 1:2]).then_inc(l1_p, 1)

                def step(i, g, past, left):
                    k = i * RING + g
                    if left > 1:
                        far_away(*later(i, g, 2), past + 2)
                    if past:
                        weights(*later(i, g, -1))
                    if left > 1:
                        one_hot(*later(i, g, 2), past + 2)
                        keep_hot(*later(i, g, 2))
                    if past:
                        act.wait_ge(l1_wide, k)
                        place1(k + RING - 1, (g + RING - 1) % RING)

                for k in range(RING):
                    place1(k, k)
                for g in range(2):
                    far_away(0, g, g)
                    one_hot(0, g, g)
                    keep_hot(0, g)
                edge_rounds(act, step)
                weights(ITERS - 1, RING - 1)

            @block.tensor
            def _(pe):
                regs = node_regs(pe, "l1_q")

                def turn(i, g):
                    pe.wait_ge(l1_hot, i * RING + g + 1)
                    for u in range(G):
                        last = t_.transpose(TR[:, :].bitcast(BF16)[:, u * P:(u + 1) * P], hot[:, g, u, :], ident_b[:, :])
                    last.then_inc(l1_hotT, 1)

                def query(i, g):
                    load_nodes(pe, regs, i * RING + g, g)
                    nodes = nodes_of(pe, regs, g)
                    pe.wait_ge(l1_hot_kept, i * RING + g + 1)
                    for u in range(G):
                        for c in range(3):
                            last = t_.matmul(QB[g % 2][:, u * P:(u + 1) * P], hotT[:, g, u * P:(u + 1) * P],
                                             flat(look[:, bass.ds(nodes[u], 1), c * D:(c + 1) * D]), start=(c == 0), stop=(c == 2))
                    last.then_inc(l1_q, 1)

                def summed(i, g):
                    k = i * RING + g
                    pe.wait_ge(l1_wide, k + 1)
                    pe.wait_ge(l1_acc[G - 1], k + 1)
                    for u in range(G):
                        last = t_.matmul(bank[SUM + 2 * (g % 2) + u // 2][:, (u % 2) * AW:(u % 2 + 1) * AW],
                                         hotf[:, g, u, :], wide[:, g, u, :], start=True, stop=True)
                    last.then_inc(l1_sum, 1)

                def step(i, g, past, left):
                    k = i * RING + g
                    if past >= 2:
                        summed(*later(i, g, -2))
                    if left:
                        query(*later(i, g, 1))
                    pe.wait_ge(l1_gm, k + 1)
                    t_.transpose(MB[0:1, 0:P], small[:, g, 0:1], ident[:, :]).then_inc(l1_gmT, 1)
                    if left > 1:
                        turn(*later(i, g, 2))
                    pe.wait_ge(l1_top, k + 1)
                    t_.matmul(MB[:, P:P + 1], ones[0:1, :], top[:, 0:1], start=True, stop=True).then_inc(l1_topB, 1)

                turn(0, 0)
                query(0, 0)
                turn(0, 1)
                edge_rounds(pe, step)
                summed(ITERS - 1, RING - 2)
                summed(ITERS - 1, RING - 1)

            @block.vector
            def _(dve):
                regs = node_regs(dve, "l1_node")
                L1 = 5

                def add(i, g, u, nodes):
                    k = i * RING + g
                    here = flat(acc[:, bass.ds(nodes[u], 1), :])
                    new = bank[SUM + 2 * (g % 2) + u // 2][:, (u % 2) * AW:(u % 2 + 1) * AW]
                    if u:
                        dve.wait_ge(l1_acc[u - 1], k + 1)
                        v.tensor_add(here, here, new).then_inc(l1_acc[u], 1)
                    else:
                        dve.wait_ge(l1_sum, k + 1)
                        dve.wait_ge(l1_acc[G - 1], k + 2)
                        v.tensor_copy(neg_max[:, bass.ds(nodes[0], G)], small[:, g, 1:2].to_broadcast([P, G]))
                        v.scalar_tensor_tensor(out=here, in0=here, scalar=small[:, g, 2:3], in1=new,
                                               op0=ALU.mult, op1=ALU.add).then_inc(l1_acc[0], 1)

                def widen(i, g):
                    dve.wait_ge(l1_p, i * RING + g + 1)
                    v.tensor_tensor(out=wide[:, g, :, 0:D].rearrange("p u (h d) -> p u h d", h=H),
                                    in0=ring[:, g * G:(g + 1) * G, D:2 * D].rearrange("p u (h d) -> p u h d", h=H),
                                    in1=wide[:, g, :, D:AW].unsqueeze(3).to_broadcast([P, G, H, HD]), op=ALU.mult).then_inc(l1_wide, 1)

                def negate(i, g):
                    dve.wait_ge(l1_topB, i * RING + g + 1)
                    v.tensor_scalar(out=small[:, g, 1:2], in0=MB[:, P:P + 1], scalar1=-1.0, scalar2=None, op0=ALU.mult).then_inc(l1_neg, 1)

                def back(i, g):
                    nodes = nodes_of(dve, regs, g)
                    return lambda u: add(i, g, u, nodes)

                def step(i, g, past, left):
                    k = i * RING + g
                    ch = Chain(dve, l1_v, L1 * k + 1)
                    add_step = back(*later(i, g, -3)) if past >= 3 else lambda u: None
                    arrived(dve, i, g)
                    dve.wait_ge(l1_q, k + 1)
                    prod = junk[:, 0, :]
                    ch(v.tensor_tensor(out=prod.rearrange("p (u d) -> p u d", u=G), in0=QB[g % 2][:, :].rearrange("p (u d) -> p u d", u=G),
                                       in1=ring[:, g * G:(g + 1) * G, 0:D], op=ALU.mult))
                    if past:
                        negate(*later(i, g, -1))
                    add_step(0)
                    ch.wait()
                    ch(v.tensor_reduce(out=lg[:, g, 0, :], in_=prod.rearrange("p (a d) -> p a d", d=HD), axis=AX.X, op=ALU.add))
                    add_step(1)
                    ch.wait()
                    ch(v.tensor_add(lg[:, g, 0, :], lg[:, g, 0, :], bias_now[:, g, :]))
                    ch.wait()
                    ch(v.scalar_tensor_tensor(out=lg[:, g, 1, :], in0=lg[:, g, 0, :], scalar=0.2, in1=lg[:, g, 0, :],
                                              op0=ALU.mult, op1=ALU.max))
                    ch.wait()
                    v.reduce_max(small[:, g, 0:1], lg[:, g, 1, :], axis=AX.X).then_inc(l1_gm, 1)
                    if past:
                        widen(*later(i, g, -1))
                    add_step(2)
                    add_step(3)
                    if past >= 2:
                        load_nodes(dve, regs, k - 2, g - 2)
                    dve.wait_ge(l1_gmT, k + 1)
                    ch(v.reduce_max(top[:, 1:2], MB[0:1, 0:P], axis=AX.X))
                    ch.wait()
                    v.tensor_max(top[:, 0:1], top[:, 0:1], top[:, 1:2]).then_inc(l1_top, 1)
                    assert ch.n == L1

                dve.sem_inc(l1_acc[G - 1], 2)
                v.memset(small[:, RING - 1, 1:2], BIG).then_inc(l1_v, 1)
                edge_rounds(dve, step)
                negate(ITERS - 1, RING - 1)
                widen(ITERS - 1, RING - 1)
                for g in range(1, RING):
                    load_nodes(dve, regs, (ITERS - 1) * RING + g, g)
                    add_step = back(ITERS - 1, g)
                    for u in range(G):
                        add_step(u)
        gcount[0] += ITERS

        with nc.Block() as block:
            @block.sync
            def _(sp):
                for used in early_sems[0::4]:
                    sp.sem_clear(used)

            @block.scalar
            def _(act):
                for used in early_sems[1::4]:
                    act.sem_clear(used)

            @block.vector
            def _(dve):
                for used in early_sems[2::4]:
                    dve.sem_clear(used)

            @block.tensor
            def _(pe):
                for used in early_sems[3::4]:
                    pe.sem_clear(used)
        early.close()
        early_sems = None

        (n2_staged, n2_agg, n2_aggT, n2_aggT_kept, n2_o_mm, n2_o_kept, n2_xT, n2_xT_kept, n2_mm, n2_var, n2_std, n2_xn, n2_xnT,
         n2_xnT_kept, n2_e_mm, n2_e_kept, n2_e0, n2_e_rest, n2_e1, n2_split, t2_out, t2_free, n2_copied, n2_v, n2_factor) = (
            sem(f"n2_{n}") for n in (
             "staged", "agg", "aggT", "aggT_kept", "o_mm", "o_kept", "xT", "xT_kept", "mm", "var", "std", "xn", "xnT", "xnT_kept",
             "e_mm", "e_kept", "e0", "e_rest", "e1", "split", "t2_out", "t2_free", "copied", "vector", "factor"))
        N2 = 2 + NORM
        halves = bank[5][:, :].rearrange("p (t c) -> p t c", t=BT)
        with nc.Block() as block:
            @block.vector
            def _(dve):
                def front(b):
                    v.tensor_tensor(out=tB.rearrange("p t (h d) -> p t h d", h=H),
                                    in0=acc[:, tiles(b), 0:D].rearrange("p t (h d) -> p t h d", h=H),
                                    in1=rs[:, tiles(b), 0:H].unsqueeze(3).to_broadcast([P, BT, H, HD]), op=ALU.mult).then_inc(n2_agg, 1)

                def rest(b):
                    dve.wait_ge(n2_e0, b + 1)
                    dve.wait_ge(t2_free, b + 1)
                    v.tensor_tensor(out=tT2, in0=halves[:, :, 0:EH], in1=be1b[:, :].unsqueeze(1).to_broadcast([P, BT, EH]),
                                    op=ALU.add).then_inc(n2_e_kept, 1)
                    v.tensor_tensor(out=tC[:, :, 0:EH], in0=halves[:, :, EH:2 * EH], in1=look[:, tiles(b), 0:EH],
                                    op=ALU.subtract).then_inc(n2_e_rest, 1)

                def last_part(b):
                    dve.wait_ge(n2_e1, b + 1)
                    v.tensor_sub(look[:, tiles(b), 2 * EH:3 * EH], tC[:, :, 0:EH], look[:, tiles(b), EH:2 * EH]).then_inc(n2_split, 1)

                def batch(b, first, last):
                    ch = Chain(dve, n2_v, N2 * b + 4)
                    if not first:
                        dve.wait_ge(n2_xn, b)
                    dve.wait_ge(n2_mm, b + 1)
                    ch(v.tensor_tensor(out=tA, in0=bank[3][:, :].rearrange("p (t d) -> p t d", t=BT),
                                       in1=bmb[:, :].unsqueeze(1).to_broadcast([P, BT, D]), op=ALU.add))
                    if not last:
                        front(b + 1)
                    ch.wait()
                    ch(v.scalar_tensor_tensor(out=tY, in0=tA, scalar=0.0, in1=xs[:, tiles(b), :], op0=ALU.max, op1=ALU.add))
                    norm_stats(ch, tY, n2_var)
                    if not first:
                        rest(b - 1)
                    dve.wait_ge(n2_copied, b + 1)
                    normalize(ch, b, tY, [tN[:, u, :] for u in range(BT)], n2_std).then_inc(n2_xn, 1)
                    if not first:
                        last_part(b - 1)
                    assert ch.n == N2, ch.n

                ch = Chain(dve, n2_v)
                spread = rs[:, :, H:H + 1].to_broadcast([P, NT, H])
                dve.wait_ge(n2_factor, 1)
                ch(v.tensor_tensor(out=rs[:, :, 0:H], in0=acc[:, :, D:AW], in1=spread, op=ALU.mult))
                ch.wait()
                ch(v.tensor_scalar(out=rs[:, :, 0:H], in0=rs[:, :, 0:H], scalar1=1e-12, scalar2=None, op0=ALU.max))
                ch.wait()
                ch(v.reciprocal(rs[:, :, 0:H], rs[:, :, 0:H]))
                ch.wait()
                ch(v.tensor_tensor(out=rs[:, :, 0:H], in0=rs[:, :, 0:H], in1=spread, op=ALU.mult))
                ch.wait()
                front(0)
                batch_rounds(dve, batch)
                dve.wait_ge(n2_split, NB - 1)
                rest(NB - 1)
                last_part(NB - 1)

            @block.tensor
            def _(pe):
                def project(b):
                    pe.wait_ge(n2_staged, b + 1)
                    for u in range(BT):
                        last = t_.transpose(bank[2][:, u * P:(u + 1) * P], tX[:, u, :], ident[:, :])
                    last.then_inc(n2_xT, 1)
                    pe.wait_ge(n2_agg, b + 1)
                    for u in range(BT):
                        last = t_.transpose(bank[0][:, u * P:(u + 1) * P], tB[:, u, :], ident[:, :])
                    last.then_inc(n2_aggT, 1)
                    pe.wait_ge(n2_aggT_kept, b + 1)
                    t_.matmul(bank[1][:, :], wo[:, :], rT[:, 0, :], start=True, stop=True).then_inc(n2_o_mm, 1)

                def mix(b):
                    pe.wait_ge(n2_xT_kept, b + 1)
                    pe.wait_ge(n2_o_kept, b + 1)
                    for u in range(BT):
                        at = slice(u * P, (u + 1) * P)
                        t_.matmul(bank[3][:, at], rT[:, 1, at], wm[:, 0, :], start=True, stop=False)
                        last = t_.matmul(bank[3][:, at], rT[:, 2, at], wm[:, 1, :], start=False, stop=True)
                    last.then_inc(n2_mm, 1)

                def batch(b, first, last):
                    if not last:
                        project(b + 1)
                    pe.wait_ge(n2_xn, b + 1)
                    for u in range(BT):
                        done = t_.transpose(bank[4][:, u * P:(u + 1) * P], tN[:, u, :], ident[:, :])
                    done.then_inc(n2_xnT, 1)
                    if not last:
                        mix(b + 1)
                    pe.wait_ge(n2_xnT_kept, b + 1)
                    for u in range(BT):
                        for c in range(2):
                            done = t_.matmul(bank[5][:, u * P + c * EH:u * P + (c + 1) * EH], rT[:, 3, u * P:(u + 1) * P], we1[:, c, :],
                                             start=True, stop=True)
                    done.then_inc(n2_e_mm, 1)

                project(0)
                mix(0)
                batch_rounds(pe, batch)

            @block.scalar
            def _(act):
                def turned(b):
                    act.wait_ge(n2_xT, b + 1)
                    s_.copy(rT[:, 1, :], bank[2][:, :]).then_inc(n2_xT_kept, 1)
                    act.wait_ge(n2_aggT, b + 1)
                    s_.copy(rT[:, 0, :], bank[0][:, :]).then_inc(n2_aggT_kept, 1)

                def projected(b):
                    act.wait_ge(n2_o_mm, b + 1)
                    s_.activation(rT[:, 2, :], bank[1][:, :], ACT.Identity, bias=boc[:, 0:1]).then_inc(n2_o_kept, 1)

                def second_part(b):
                    act.wait_ge(n2_e_rest, b + 1)
                    s_.copy(look[:, tiles(b), EH:2 * EH], tC[:, :, 0:EH]).then_inc(n2_e1, 1)

                def batch(b, first, last):
                    if not last:
                        turned(b + 1)
                    root(act, b, n2_var, n2_std)
                    if not first:
                        second_part(b - 1)
                    if not last:
                        projected(b + 1)
                    act.wait_ge(n2_xnT, b + 1)
                    s_.copy(rT[:, 3, :], bank[4][:, :]).then_inc(n2_xnT_kept, 1)
                    act.wait_ge(n2_e_mm, b + 1)
                    s_.copy(look[:, tiles(b), 0:EH], halves[:, :, EH:2 * EH]).then_inc(n2_e0, 1)

                s_.activation(rs[:, :, H], neg_max[:, 0:NT], ACT.Exp, scale=-1.0, bias=small[:, RING - 1, 1:2]).then_inc(n2_factor, 1)
                turned(0)
                projected(0)
                batch_rounds(act, batch)
                second_part(NB - 1)

            @block.gpsimd
            def _(pool):
                def stage(b):
                    q_.tensor_copy(tX, xs[:, tiles(b), :]).then_inc(n2_staged, 1)

                def batch(b, first, last):
                    if not last:
                        pool.wait_ge(n2_xT, b + 1)
                        pool.sem_inc(rounds, 1)
                        stage(b + 1)
                    pool.wait_ge(n2_xn, b + 1)
                    pool.sem_inc(rounds, 1)
                    q_.tensor_copy(xs[:, tiles(b), :], tN).then_inc(n2_copied, 1)

                pool.sem_inc(n2_copied, 1)
                stage(0)
                batch_rounds(pool, batch)
                q_.memset(acc[:, :, :], 0.0)

            @block.sync
            def _(sp):
                sp.sem_inc(t2_free, 1)
                with sp.Fori(0, NB) as b:
                    sp.wait_ge(n2_e_kept, b + 1)
                    sp.dma_start(t2.rearrange("(t p) c -> p t c", p=P)[:, tiles(b), :], tT2).then_inc(t2_out, 16)
                    sp.wait_ge(t2_out, 16 * b + 16)
                    sp.sem_inc(t2_free, 1)

        (l2_placed, l2_hot, l2_hotT, l2_hot_kept, l2_half, l2_pre, l2_s1, l2_s1T, l2_s1T_kept, l2_e, l2_s2, l2_dup, l2_cut, l2_keyB,
         l2_same, l2_v, l2_init) = (sem(f"l2_{n}") for n in (
             "placed", "hot", "hotT", "hot_kept", "half", "pre", "silu1", "silu1T", "silu1T_kept", "e", "silu2", "dup", "cut", "keyB",
             "same", "vector", "init"))
        TR, KB, HB, ST, EB, DB = bank[0:6]
        same_tri = tabf[:, 0:G * P]
        s1T = tabf[0:EH + 1, G * P:2 * G * P]
        W4 = G * EH
        with nc.Block() as block:
            def cut(g):
                return wide[:, g, :, :].rearrange("p u c -> p (u c)")[:, 0:W4]

            def silu2(g):
                return wide[:, g, :, :].rearrange("p u c -> p (u c)")[:, W4:2 * W4]

            @block.gpsimd
            def _(pool):
                def step(i, g, past, left):
                    k = i * RING + g
                    if left == RING:
                        gather(pool, k + RING, g, t2, EH, l2_placed, t2_out)
                    for u in range(G):
                        pool.wait_ge(scattered[u], 16 * k + 16)
                    pool.wait_ge(l2_cut, k + 1)
                    pool.sem_inc(rounds, 1)
                    for u in range(G):
                        q_.indirect_dma_start(mlp_sum[u], bass.IndirectOffsetOnAxis(ap=put_i[:, g, u:u + 1].bitcast(U32), axis=0),
                                              cut(g)[:, u * EH:(u + 1) * EH], None, compute_op=ALU.add).then_inc(scattered[u], 16)

                for k in range(RING):
                    gather(pool, k, k, t2, EH, l2_placed, t2_out)
                edge_rounds(pool, step)
                for u in range(G):
                    pool.wait_ge(scattered[u], 16 * GROUPS + 16)

            @block.scalar
            def _(act):
                columns = ((rel_now, rel), (key_now, key))

                def keep_hot(i, g):
                    act.wait_ge(l2_hotT, i * RING + g + 1)
                    s_.copy(hotT[:, g, :], TR[:, :].bitcast(BF16)[:, 0:G * P]).then_inc(l2_hot_kept, 1)

                def step(i, g, past, left):
                    k = i * RING + g
                    act.wait_ge(l2_pre, k + 1)
                    s_.activation(junk[:, g % 2, 0:W4], junk[:, g % 2, W4:2 * W4], ACT.Silu).then_inc(l2_s1, 1)
                    act.wait_ge(l2_s1T, k + 1)
                    s_.copy(s1T[0:EH, :], ST[0:EH, :]).then_inc(l2_s1T_kept, 1)
                    place(k + RING, g, l2_placed, *columns)
                    if left:
                        keep_hot(*later(i, g, 1))
                    act.wait_ge(l2_e, k + 1)
                    s_.activation(silu2(g), EB[:, 0:W4], ACT.Silu).then_inc(l2_s2, 1)

                for k in range(RING):
                    place(k, k, l2_placed, *columns)
                keep_hot(0, 0)
                edge_rounds(act, step)

            @block.tensor
            def _(pe):
                regs = node_regs(pe, "l2_half")

                def spread_keys(i, g):
                    k = i * RING + g
                    pe.wait_ge(l2_placed, k + 1)
                    for u in range(G):
                        last = t_.matmul(KB[:, u * P:(u + 1) * P], key_now[:, g * G + u:g * G + u + 1].to_broadcast([P, P]),
                                         ident[:, :], start=True, stop=True)
                    last.then_inc(l2_keyB, 1)

                def turn(i, g):
                    pe.wait_ge(l2_hot, i * RING + g + 1)
                    for u in range(G):
                        last = t_.transpose(TR[:, :].bitcast(BF16)[:, u * P:(u + 1) * P], hot[:, g, u, :], ident_b[:, :])
                    last.then_inc(l2_hotT, 1)

                def half(i, g):
                    load_nodes(pe, regs, i * RING + g, g)
                    nodes = nodes_of(pe, regs, g)
                    pe.wait_ge(l2_hot_kept, i * RING + g + 1)
                    for u in range(G):
                        for c in range(3):
                            last = t_.matmul(HB[:, u * EH:(u + 1) * EH], hotT[:, g, u * P:(u + 1) * P],
                                             flat(look[:, bass.ds(nodes[u], 1), c * EH:(c + 1) * EH]), start=(c == 0), stop=(c == 2))
                    last.then_inc(l2_half, 1)

                def same_sums(i, g):
                    pe.wait_ge(l2_s2, i * RING + g + 1)
                    pe.wait_ge(l2_same, i * RING + g + 1)
                    for u in range(G):
                        last = t_.matmul(DB[:, u * EH:(u + 1) * EH], hotf[:, g, u, :], silu2(g)[:, u * EH:(u + 1) * EH], start=True, stop=True)
                    last.then_inc(l2_dup, 1)

                def step(i, g, past, left):
                    k = i * RING + g
                    pe.wait_ge(l2_s1, k + 1)
                    pe.sem_inc(rounds, 1)
                    for u in range(G):
                        last = t_.transpose(ST[0:EH, u * P:(u + 1) * P], junk[:, g % 2, u * EH:(u + 1) * EH], ident[:, :])
                    last.then_inc(l2_s1T, 1)
                    if past:
                        same_sums(*later(i, g, -1))
                    if left:
                        turn(*later(i, g, 1))
                    pe.wait_ge(l2_s1T_kept, k + 1)
                    for u in range(G):
                        last = t_.matmul(EB[:, u * EH:(u + 1) * EH], s1T[:, u * P:(u + 1) * P], we2[:, :], start=True, stop=True)
                    last.then_inc(l2_e, 1)
                    if left:
                        half(*later(i, g, 1))
                    if left > 1:
                        pe.wait_ge(l2_same, k + 2)
                        spread_keys(*later(i, g, 2))

                spread_keys(0, 0)
                turn(0, 0)
                half(0, 0)
                pe.wait_ge(l2_same, 1)
                spread_keys(0, 1)
                edge_rounds(pe, step)
                pe.wait_ge(l2_cut, GROUPS - 1)
                same_sums(ITERS - 1, RING - 1)

            @block.vector
            def _(dve):
                L2 = 7

                def one_hot(i, g):
                    dve.wait_ge(l2_placed, i * RING + g + 1)
                    v.tensor_tensor(out=hot[:, g, :, :], **hots(g)).then_inc(l2_hot, 1)

                def duplicates(i, g):
                    k = i * RING + g
                    ch = Chain(dve, l2_v, L2 * k)
                    keys_g = key_now[:, g * G:(g + 1) * G]
                    dve.wait_ge(l2_keyB, k + 1)
                    v.tensor_tensor(out=hotf[:, g, :, :], in0=KB[:, :].rearrange("p (u e) -> p u e", u=G),
                                    in1=keys_g.unsqueeze(2).to_broadcast([P, G, P]), op=ALU.is_equal).then_inc(l2_same, 1)
                    dve.wait_ge(l2_same, k + 1)
                    ch(v.tensor_tensor(out=same_tri.rearrange("p (u e) -> p u e", u=G), in0=hotf[:, g, :, :],
                                       in1=tri[:, :].unsqueeze(1).to_broadcast([P, G, P]), op=ALU.mult))
                    ch.wait()
                    s = [small[:, g, j * G:(j + 1) * G] for j in range(5)]
                    ch(v.tensor_reduce(out=s[0], in_=same_tri.rearrange("p (u e) -> p u e", u=G), axis=AX.X, op=ALU.add))
                    ch(v.tensor_scalar(out=s[2], in0=keys_g, scalar1=far[:, 1:2], scalar2=None, op0=ALU.subtract))
                    ch.wait()
                    ch(v.tensor_scalar(out=s[1], in0=s[0], scalar1=0.5, scalar2=None, op0=ALU.is_lt))
                    ch.wait()
                    ch(v.scalar_tensor_tensor(out=s[3], in0=keys_g, scalar=float(FAR), in1=s[1], op0=ALU.is_lt, op1=ALU.mult))
                    ch.wait()
                    ch(v.tensor_tensor(out=s[4], in0=s[2], in1=s[3], op=ALU.mult))
                    ch.wait()
                    ch(v.tensor_scalar(out=put_i[:, g, :], in0=s[4], scalar1=far[:, 1:2], scalar2=None, op0=ALU.add))
                    assert ch.n == L2, ch.n

                def keep_cut(i, g):
                    dve.wait_ge(l2_dup, i * RING + g + 1)
                    v.tensor_copy(cut(g), DB[:, 0:W4]).then_inc(l2_cut, 1)

                def step(i, g, past, left):
                    k = i * RING + g
                    if past >= RING - 1:
                        for u in range(G):
                            dve.wait_ge(scattered[u], 16 * k - 16)
                    arrived(dve, i, g)
                    dve.wait_ge(l2_half, k + 1)
                    v.tensor_tensor(out=junk[:, g % 2, W4:2 * W4].rearrange("p (u f) -> p u f", u=G),
                                    in0=HB[:, 0:W4].rearrange("p (u f) -> p u f", u=G), in1=ring[:, g * G:(g + 1) * G, 0:EH],
                                    op=ALU.add).then_inc(l2_pre, 1)
                    if left:
                        one_hot(*later(i, g, 1))
                        duplicates(*later(i, g, 1))
                    if past:
                        keep_cut(*later(i, g, -1))

                v.memset(tabf[EH:EH + 1, G * P:2 * G * P], 1.0).then_inc(l2_init, 1)
                one_hot(0, 0)
                duplicates(0, 0)
                edge_rounds(dve, step)
                keep_cut(ITERS - 1, RING - 1)
        gcount[0] += ITERS

        (n3_staged, n3_in, n3_pair, n3_sum, n3_xT, n3_sumT, n3_xT_kept, n3_sumT_kept, n3_h_mm, n3_h_kept, n3_mm, n3_var, n3_std, n3_xn,
         n3_xnT, n3_xnT_kept, n3_t_mm, n3_t_kept, t3_out, n3_copied, n3_v) = (sem(f"n3_{n}") for n in (
             "staged", "in", "pair", "sum", "xT", "sumT", "xT_kept", "sumT_kept", "h_mm", "h_kept", "mm", "var", "std", "xn", "xnT",
             "xnT_kept", "t_mm", "t_kept", "t3_out", "copied", "vector"))
        N3 = 2 + NORM
        with nc.Block() as block:
            @block.sync
            def _(sp):
                def load(b):
                    for u in range(G):
                        sp.dma_start(tS[:, u, :, :], mlp_sum[u][0:NP, :].rearrange("(t p) f -> p t f", p=P)[:, tiles(b), :]).then_inc(n3_in, 16)

                def store(b):
                    sp.wait_ge(n3_t_kept, b + 1)
                    sp.dma_start(t3.rearrange("(t p) c -> p t c", p=P)[:, tiles(b), :], tab[:, tiles(b), 0:D]).then_inc(t3_out, 16)

                def batch(b, first, last):
                    if not last:
                        sp.wait_ge(n3_sum, b + 1)
                        load(b + 1)
                    if not first:
                        store(b - 1)

                load(0)
                batch_rounds(sp, batch)
                store(NB - 1)
                sp.wait_ge(t3_out, 16 * NB)

            @block.vector
            def _(dve):
                def front(b):
                    dve.wait_ge(n3_in, 16 * G * b + 16 * G)
                    v.tensor_add(tB[:, :, 0:EH], tS[:, 0, :, :], tS[:, 1, :, :])
                    v.tensor_add(tC[:, :, 0:EH], tS[:, 2, :, :], tS[:, 3, :, :]).then_inc(n3_pair, 1)
                    dve.wait_ge(n3_pair, b + 1)
                    v.tensor_add(tB[:, :, 0:EH], tB[:, :, 0:EH], tC[:, :, 0:EH]).then_inc(n3_sum, 1)

                def table(b):
                    dve.wait_ge(n3_t_mm, b + 1)
                    v.tensor_tensor(out=tab[:, tiles(b), 0:D], in0=bank[5][:, :].rearrange("p (t d) -> p t d", t=BT),
                                    in1=dis[:, tiles(b)].unsqueeze(2).to_broadcast([P, BT, D]), op=ALU.mult).then_inc(n3_t_kept, 1)

                def batch(b, first, last):
                    ch = Chain(dve, n3_v, N3 * b)
                    if not first:
                        dve.wait_ge(n3_xn, b)
                    dve.wait_ge(n3_mm, b + 1)
                    ch(v.tensor_tensor(out=tA, in0=bank[3][:, :].rearrange("p (t d) -> p t d", t=BT),
                                       in1=bn2b[:, :].unsqueeze(1).to_broadcast([P, BT, D]), op=ALU.add))
                    if not last:
                        front(b + 1)
                    ch.wait()
                    ch(v.scalar_tensor_tensor(out=tY, in0=xs[:, tiles(b), :], scalar=2.0, in1=tA, op0=ALU.mult, op1=ALU.add))
                    norm_stats(ch, tY, n3_var)
                    if not first:
                        table(b - 1)
                    dve.wait_ge(n3_copied, b + 1)
                    normalize(ch, b, tY, [tN[:, u, :] for u in range(BT)], n3_std).then_inc(n3_xn, 1)
                    assert ch.n == N3

                front(0)
                batch_rounds(dve, batch)
                table(NB - 1)

            @block.tensor
            def _(pe):
                def hidden(b):
                    pe.wait_ge(n3_staged, b + 1)
                    for u in range(BT):
                        last = t_.transpose(bank[1][:, u * P:(u + 1) * P], tX[:, u, :], ident[:, :])
                    last.then_inc(n3_xT, 1)
                    pe.wait_ge(n3_sum, b + 1)
                    pe.sem_inc(rounds, 1)
                    for u in range(BT):
                        last = t_.transpose(bank[0][0:EH, u * P:(u + 1) * P], tB[:, u, 0:EH], ident[:, :])
                    last.then_inc(n3_sumT, 1)
                    pe.wait_ge(n3_xT_kept, b + 1)
                    t_.matmul(bank[2][:, :], wn1[:, 0, :], rT[:, 1, :], start=True, stop=False)
                    pe.wait_ge(n3_sumT_kept, b + 1)
                    t_.matmul(bank[2][:, :], wn1[0:EH, 1, :], rT[0:EH, 0, :], start=False, stop=True).then_inc(n3_h_mm, 1)

                def output(b):
                    pe.wait_ge(n3_h_kept, b + 1)
                    for u in range(BT):
                        last = t_.matmul(bank[3][:, u * P:(u + 1) * P], rT[:, 2, u * P:(u + 1) * P], wn2[:, :], start=True, stop=True)
                    last.then_inc(n3_mm, 1)

                def batch(b, first, last):
                    if not last:
                        hidden(b + 1)
                    pe.wait_ge(n3_xn, b + 1)
                    for u in range(BT):
                        done = t_.transpose(bank[4][:, u * P:(u + 1) * P], tN[:, u, :], ident[:, :])
                    done.then_inc(n3_xnT, 1)
                    if not last:
                        output(b + 1)
                    pe.wait_ge(n3_xnT_kept, b + 1)
                    for u in range(BT):
                        done = t_.matmul(bank[5][:, u * P:(u + 1) * P], rT[:, 3, u * P:(u + 1) * P], wg1[:, :], start=True, stop=True)
                    done.then_inc(n3_t_mm, 1)

                hidden(0)
                output(0)
                batch_rounds(pe, batch)

            @block.scalar
            def _(act):
                def turned(b):
                    act.wait_ge(n3_xT, b + 1)
                    s_.copy(rT[:, 1, :], bank[1][:, :]).then_inc(n3_xT_kept, 1)
                    act.wait_ge(n3_sumT, b + 1)
                    s_.copy(rT[0:EH, 0, :], bank[0][0:EH, :]).then_inc(n3_sumT_kept, 1)

                def hidden(b):
                    act.wait_ge(n3_h_mm, b + 1)
                    s_.activation(rT[:, 2, :], bank[2][:, :], ACT.Silu, bias=bn1c[:, 0:1]).then_inc(n3_h_kept, 1)

                def batch(b, first, last):
                    if not last:
                        turned(b + 1)
                    root(act, b, n3_var, n3_std)
                    if not last:
                        hidden(b + 1)
                    act.wait_ge(n3_xnT, b + 1)
                    s_.copy(rT[:, 3, :], bank[4][:, :]).then_inc(n3_xnT_kept, 1)

                turned(0)
                hidden(0)
                batch_rounds(act, batch)

            @block.gpsimd
            def _(pool):
                def stage(b):
                    q_.tensor_copy(tX, xs[:, tiles(b), :]).then_inc(n3_staged, 1)

                def batch(b, first, last):
                    if not last:
                        pool.wait_ge(n3_xT, b + 1)
                        pool.sem_inc(rounds, 1)
                        stage(b + 1)
                    pool.wait_ge(n3_xn, b + 1)
                    pool.sem_inc(rounds, 1)
                    q_.tensor_copy(xs[:, tiles(b), :], tN).then_inc(n3_copied, 1)

                pool.sem_inc(n3_copied, 1)
                stage(0)
                batch_rounds(pool, batch)

        def convolution(name, table, table_out):
            placed, hot_made, summed, added = (sem(f"{name}_{n}") for n in ("placed", "hot", "sum", "acc"))
            with nc.Block() as block:
                @block.gpsimd
                def _(pool):
                    with pool.Fori(0, ITERS) as i:
                        for g in range(RING):
                            gather(pool, i * RING + g, g, table, D, placed, table_out)

                @block.scalar
                def _(act):
                    for k in range(RING):
                        place(k, k, placed, (rel_now, rel), (ew_now, ew))
                    with act.Fori(0, ITERS) as i:
                        for g in range(RING):
                            k = i * RING + g
                            act.wait_ge(summed, k + 1)
                            place(k + RING, g, placed, (rel_now, rel), (ew_now, ew))

                @block.tensor
                def _(pe):
                    with pe.Fori(0, ITERS) as i:
                        for g in range(RING):
                            k = i * RING + g
                            pe.wait_ge(hot_made, k + 1)
                            pe.wait_ge(added, k * G + G)
                            arrived(pe, i, g)
                            for u in range(G):
                                last = t_.matmul(bank[g][:, u * P:(u + 1) * P], hotf[:, g, u, :], ring[:, g * G + u, 0:D],
                                                 start=True, stop=True)
                            last.then_inc(summed, 1)

                @block.vector
                def _(dve):
                    regs = node_regs(dve, f"{name}_node")

                    def front(i, g):
                        dve.wait_ge(placed, i * RING + g + 1)
                        for u in range(G):
                            at = slice(g * G + u, g * G + u + 1)
                            last = v.tensor_scalar(out=hotf[:, g, u, :], in0=iota[:, :], scalar1=rel_now[:, at], scalar2=ew_now[:, at],
                                                   op0=ALU.is_equal, op1=ALU.mult)
                        last.then_inc(hot_made, 1)

                    def back(i, g):
                        k = i * RING + g
                        load_nodes(dve, regs, k, g)
                        nodes = nodes_of(dve, regs, g)
                        dve.wait_ge(summed, k + 1)
                        for u in range(G):
                            here = flat(acc[:, bass.ds(nodes[u], 1), 0:D])
                            dve.wait_ge(added, k * G + RING * G + u)
                            v.tensor_add(here, here, bank[g][:, u * P:(u + 1) * P]).then_inc(added, 1)

                    def both(i, g, past, left):
                        if left:
                            front(*later(i, g, 1))
                        back(i, g)

                    dve.sem_inc(added, RING * G)
                    front(0, 0)
                    edge_rounds(dve, both)
            gcount[0] += ITERS

        convolution("c1", t3, t3_out)

        n4_own, n4_r, n4_rT, n4_rT_kept, n4_mm, n4_kept, t4_out = (
            sem(f"n4_{n}") for n in ("own", "sum", "sumT", "reluT_kept", "mm", "kept", "t4_out"))
        with nc.Block() as block:
            @block.vector
            def _(dve):
                def spread(b):
                    return dis[:, tiles(b)].unsqueeze(2).to_broadcast([P, BT, D])

                def front(b):
                    v.tensor_add(tA, acc[:, tiles(b), 0:D], tab[:, tiles(b), 0:D]).then_inc(n4_own, 1)
                    dve.wait_ge(n4_own, b + 1)
                    v.tensor_tensor(out=tB, in0=tA, in1=spread(b), op=ALU.mult).then_inc(n4_r, 1)

                def batch(b, first, last):
                    if not last:
                        dve.wait_ge(n4_rT, b + 1)
                        front(b + 1)
                    dve.wait_ge(n4_mm, b + 1)
                    v.tensor_tensor(out=tab[:, tiles(b), 0:D], in0=bank[1][:, :].rearrange("p (t d) -> p t d", t=BT),
                                    in1=spread(b), op=ALU.mult).then_inc(n4_kept, 1)

                front(0)
                batch_rounds(dve, batch)

            @block.tensor
            def _(pe):
                with pe.Fori(0, NB) as b:
                    pe.wait_ge(n4_r, b + 1)
                    for u in range(BT):
                        last = t_.transpose(bank[0][:, u * P:(u + 1) * P], tB[:, u, :], ident[:, :])
                    last.then_inc(n4_rT, 1)
                    pe.wait_ge(n4_rT_kept, b + 1)
                    pe.wait_ge(n4_kept, b + 1)
                    for u in range(BT):
                        last = t_.matmul(bank[1][:, u * P:(u + 1) * P], rT[:, 0, u * P:(u + 1) * P], wg2[:, :], start=True, stop=True)
                    last.then_inc(n4_mm, 1)

            @block.scalar
            def _(act):
                with act.Fori(0, NB) as b:
                    act.wait_ge(n4_rT, b + 1)
                    s_.activation(rT[:, 0, :], bank[0][:, :], ACT.Relu, bias=bg1c[:, 0:1]).then_inc(n4_rT_kept, 1)

            @block.gpsimd
            def _(pool):
                pool.wait_ge(n4_own, NB)
                q_.memset(acc[:, :, :], 0.0)

            @block.sync
            def _(sp):
                sp.sem_inc(n4_kept, 1)
                with sp.Fori(0, NB) as b:
                    sp.wait_ge(n4_kept, b + 2)
                    sp.dma_start(t4.rearrange("(t p) c -> p t c", p=P)[:, tiles(b), :], tab[:, tiles(b), 0:D]).then_inc(t4_out, 16)
                sp.wait_ge(t4_out, 16 * NB)

        convolution("c2", t4, t4_out)

        n5_c, n5_own, n5_var, n5_std, n5_done, n5_out, n5_v = (sem(f"n5_{n}") for n in ("c", "own", "var", "std", "done", "out", "vector"))
        N5 = 2 + NORM
        with nc.Block() as block:
            @block.vector
            def _(dve):
                def front(b):
                    v.tensor_add(tA, acc[:, tiles(b), 0:D], tab[:, tiles(b), 0:D]).then_inc(n5_own, 1)

                def batch(b, first, last):
                    ch = Chain(dve, n5_v, N5 * b)
                    dve.wait_ge(n5_own, b + 1)
                    ch(v.tensor_tensor(out=tB, in0=tA, in1=dis[:, tiles(b)].unsqueeze(2).to_broadcast([P, BT, D]), op=ALU.mult))
                    dve.wait_ge(n5_c, b + 1)
                    if not first:
                        dve.wait_ge(n5_done, b)
                    ch.wait()
                    ch(v.tensor_add(tY, tB, tC))
                    norm_stats(ch, tY, n5_var)
                    if not last:
                        front(b + 1)
                    normalize(ch, b, tY, [flat(tab[:, bass.ds(b * BT + u, 1), 0:D]) for u in range(BT)], n5_std).then_inc(n5_done, 1)
                    assert ch.n == N5

                front(0)
                batch_rounds(dve, batch)

            @block.scalar
            def _(act):
                with act.Fori(0, NB) as b:
                    root(act, b, n5_var, n5_std)

            @block.gpsimd
            def _(pool):
                def front(b):
                    q_.tensor_tensor(out=tC, in0=xs[:, tiles(b), :], in1=bg2[:, :].unsqueeze(1).to_broadcast([P, BT, D]),
                                     op=ALU.add).then_inc(n5_c, 1)

                def batch(b, first, last):
                    if not last:
                        pool.wait_ge(n5_var, b + 1)
                        pool.sem_inc(rounds, 1)
                        front(b + 1)

                front(0)
                batch_rounds(pool, batch)

            @block.sync
            def _(sp):
                with sp.Fori(0, NB) as b:
                    sp.wait_ge(n5_done, b + 1)
                    sp.dma_start(out.rearrange("(t p) c -> p t c", p=P)[:, tiles(b), :], tab[:, tiles(b), 0:D]).then_inc(n5_out, 16)
                sp.wait_ge(n5_out, 16 * NB)


_WEIGHTS = ["L0_gnn_W_att_w", "L0_gnn_W_att_b", "L0_gnn_W1_w", "L0_gnn_W1_b", "L0_gnn_W2_w", "L0_gnn_W2_b", "L0_gnn_a",
            "L1_gnn_Wq", "L1_gnn_Wk", "L1_gnn_Wv", "L1_gnn_We", "L1_gnn_Wo", "L1_gnn_bo", "L1_gnn_Wm", "L1_gnn_bm",
            "L2_gnn_We1", "L2_gnn_be1", "L2_gnn_We2", "L2_gnn_be2", "L2_gnn_Wn1", "L2_gnn_bn1", "L2_gnn_Wn2", "L2_gnn_bn2",
            "L3_gnn_W1", "L3_gnn_b1", "L3_gnn_W2", "L3_gnn_b2"]


def kernel(**inputs):
    import numpy as _np
    import concourse.bacc as _bacc
    from concourse import mybir as _mybir
    from concourse.bass_utils import run_bass_kernel_spmd as _run

    a = {k: _np.asarray(v) for k, v in inputs.items()}

    def tiled(v, fill):
        padded = _np.full(ET * P, fill, v.dtype)
        padded[:E] = v
        return padded.reshape(ET, P)

    arrays = {"x": _np.concatenate([a["x"], _np.zeros((NP - N, D), a["x"].dtype)]),
              "edge_i": _np.concatenate([tiled(a["src"], 0), tiled(a["dst"], PAD_DST)], axis=1),
              "edge_f": _np.concatenate([tiled(a["edge_weight"], 0)] + [tiled(a["edge_attr_3"][:, c], 0) for c in range(3)], axis=1)}
    arrays.update({w: a[w] for w in _WEIGHTS})
    arrays = {f"in_{k}": _np.ascontiguousarray(v) for k, v in arrays.items()}
    nc = _bacc.Bacc("TRN2", target_bir_lowering=False, num_devices=1)
    args = [nc.dram_tensor(k, v.shape, _mybir.dt.from_np(v.dtype), kind="ExternalInput").ap() for k, v in arrays.items()]
    out = nc.dram_tensor("out_nodes", (NP, D), F32, kind="ExternalOutput").ap()
    build(nc, *args, out)
    r = _run(nc, [arrays], core_ids=[0])
    return r.results[0]["out_nodes"][:N]
```

```python
import concourse.bass as bass
from concourse import mybir
from contextlib import ExitStack

F32 = mybir.dt.float32
BF16 = mybir.dt.bfloat16
I32 = mybir.dt.int32
U32 = mybir.dt.uint32
ALU = mybir.AluOpType
ACT = mybir.ActivationFunctionType
AX = mybir.AxisListType

P = 128
D = 128
N, E = 6250, 100000
ET = -(-E // P)
BT = 4
NT = -(-N // (P * BT)) * BT
NB = NT // BT
NP = NT * P
G = 4
RING = 4
USED = -(-N // P)
STEPS = -(-(ET + USED - 1) // (G * RING)) * G * RING
GROUPS = STEPS // G
ITERS = GROUPS // RING
SB = -(-STEPS // P)
COLS = SB * P
AW = 132
H, HD = 4, 32
EH = 64
PAD_DST = 1 << 20
FAR = 8192
SCALE = float(HD) ** -0.5
EPS = 1e-5
BIG = 1e30


class Chain:

    def __init__(self, eng, sem, base=0):
        self.eng, self.sem, self.base, self.n = eng, sem, base, 0

    def __call__(self, instruction):
        self.n += 1
        return instruction.then_inc(self.sem, 1)

    def wait(self):
        self.eng.wait_ge(self.sem, self.base + self.n)


def edge_rounds(eng, body):
    for g in range(RING):
        body(0, g, g, RING)
    with eng.Fori(1, ITERS - 1) as i:
        for g in range(RING):
            body(i, g, RING, RING)
    for g in range(RING):
        body(ITERS - 1, g, RING, RING - 1 - g)


def later(i, g, by):
    return i + (g + by) // RING, (g + by) % RING


def build(nc, x, edge_i, edge_f, W_att_w, W_att_b, W1_w, W1_b, W2_w, W2_b, a_vec,
          Wq, Wk, Wv, We, Wo, bo, Wm, bm, We1, be1, We2, be2, Wn1, bn1, Wn2, bn2,
          G1, g1b, G2, g2b, out):
    ctx = ExitStack()
    with ctx:
        def sb(name, shape, dt=F32):
            return ctx.enter_context(nc.sbuf_tensor(name, shape, dt))

        early, early_sems = ExitStack(), []

        def sem(name, early_only=True):
            if early_only and early_sems is not None:
                early_sems.append(early.enter_context(nc.semaphore(name)))
                return early_sems[-1]
            return ctx.enter_context(nc.semaphore(name))

        def dram(name, shape):
            return nc.dram_tensor(name, shape, F32, kind="Internal").ap()

        t0 = dram("table_attention", [NP, AW])
        t1 = dram("table_key_value", [NP, 2 * D])
        t2 = dram("table_edge_mlp", [NP, EH])
        t3 = dram("table_gcn1", [NP, D])
        t4 = dram("table_gcn2", [NP, D])
        mlp_sum = [dram(f"mlp_sum{u}", [NP + P, EH]) for u in range(G)]
        step_node_dram = nc.dram_tensor("step_node_dram", [COLS], I32, kind="Internal").ap()

        xs = sb("x_nodes", [P, NT, D])
        acc = sb("acc", [P, NT, AW])
        tab = sb("tab", [P, NT, AW])
        look = sb("look", [P, NT, 3 * D], BF16)
        dst_score = look[:, 0:NT, :].rearrange("p t c -> p (t c)").bitcast(F32)[:, 0:NP]
        dis = sb("dis", [P, NT])
        neg_max = sb("neg_max", [P, NT + G - 1])
        src_i = sb("src_i", [P, COLS], I32)
        rel = sb("rel", [P, COLS])
        ew = sb("ew", [P, COLS])
        key = sb("key", [P, COLS])
        step_node = sb("step_node", [1, COLS], I32)
        ring = sb("ring", [P, RING * G, 2 * D])
        idx_now = sb("idx_now", [P, RING * G], I32)
        rel_now = sb("rel_now", [P, RING * G])
        ew_now = sb("ew_now", [P, RING * G])
        key_now = sb("key_now", [P, RING * G])
        bias_now = sb("bias_now", [P, RING, G * H])
        hot = sb("hot", [P, RING, G, P], BF16)
        hotf = sb("hotf", [P, RING, G, P])
        hotT = sb("hotT", [P, RING, G * P], BF16)
        wide = sb("wide", [P, RING, G, AW])
        lg = sb("lg", [P, RING, 2, G * H])
        small = sb("small", [P, RING, 8 * G])
        junk = sb("junk", [P, 2, G * D])
        put_i = sb("put_i", [P, RING, G], I32)
        iota_i = sb("iota_i", [P, P], I32)
        iota = sb("iota", [P, P])
        iota_b = sb("iota_b", [P, P], BF16)
        ident = sb("ident", [P, P])
        ident_b = sb("ident_b", [P, P], BF16)
        tri = sb("tri", [P, P])
        part_i = sb("part_i", [P, SB], I32)
        part = sb("part", [P, SB])
        far = sb("far", [P, 2])
        ones = sb("ones", [P, P])
        eps = sb("eps", [P, 1])
        w_in = sb("w_in", [P, 3, D])
        a2 = sb("a2", [P, 2])
        ab = sb("ab", [P, 1])
        w0 = sb("w0", [P, AW])
        wad = sb("wad", [P, 4])
        b0 = sb("b0", [P, AW])
        w2T = sb("w2T", [P, D])
        b2 = sb("b2", [P, D])
        wkv = sb("wkv", [P, 2 * D])
        wq = sb("wq", [P, D])
        web = sb("web", [P, 3 * H])
        wo = sb("wo", [P, D])
        boc = sb("boc", [P, 1])
        wm = sb("wm", [P, 2, D])
        bmb = sb("bmb", [P, D])
        we1 = sb("we1", [P, 2, EH])
        be1b = sb("be1b", [P, EH])
        we2 = sb("we2", [EH + 1, EH])
        wn1 = sb("wn1", [P, 2, D])
        bn1c = sb("bn1c", [P, 1])
        wn2 = sb("wn2", [P, D])
        bn2b = sb("bn2b", [P, D])
        wg1 = sb("wg1", [P, D])
        wg2 = sb("wg2", [P, D])
        bg1c = sb("bg1c", [P, 1])
        bg2 = sb("bg2", [P, D])
        ringf = ring[:, :, :].rearrange("p a b -> p (a b)")
        tA, tB, tC, tX, tN, tY = (ringf[:, n * BT * D:(n + 1) * BT * D].rearrange("p (t d) -> p t d", t=BT) for n in range(6))
        tT0 = ringf[:, 6 * BT * D:6 * BT * D + BT * AW].rearrange("p (t c) -> p t c", t=BT)
        tT2 = ringf[:, 6 * BT * D:6 * BT * D + BT * EH].rearrange("p (t c) -> p t c", t=BT)
        tS = ringf[:, 6 * BT * D:6 * BT * D + G * BT * EH].rearrange("p (u t f) -> p u t f", u=G, t=BT)
        tKV = ringf[:, 6 * BT * D:8 * BT * D].rearrange("p (t d) -> p t d", t=BT)
        rT = hotf[:, :, :, :].rearrange("p a b c -> p a (b c)")
        stat = sb("stat", [P, BT, 8])
        mv = sb("mv", [P, BT, 2])
        rs = sb("rs", [P, NT, 2 * H])
        top = sb("top", [1, 4])
        kv_row = ew[0:1, 0:ET]
        last_i = key[0:1, 0:ET].bitcast(I32)
        tabf = tab[:, :, :].rearrange("p t c -> p (t c)")
        got_f = tabf[:, 0:SB * 4 * P].rearrange("p (b c) -> p b c", b=SB)
        lookf = look[:, :, :].rearrange("p t c -> p (t c)").bitcast(F32)
        got_if = lookf[:, COLS:COLS + SB * 2 * P].rearrange("p (b c) -> p b c", b=SB)
        got_i = tabf[:, SB * 4 * P:SB * 6 * P].bitcast(I32).rearrange("p (b c) -> p b c", b=SB)
        bias = tabf[:, 0:COLS * H].rearrange("p (s h) -> p s h", h=H)
        accf = acc[:, :, :].rearrange("p t c -> p (t c)")
        keys = accf[:, 0:ET]
        one_row = accf[:, ET:2 * ET]
        src_f = accf[:, 2 * ET:2 * ET + COLS]
        attr = [hot[:, :, :, :].rearrange("p a b c -> p (a b c)").bitcast(F32)[:, 0:COLS],
                hotT[:, :, :].rearrange("p a b -> p (a b)").bitcast(F32)[:, 0:COLS],
                wide[:, :, :, :].rearrange("p a b c -> p (a b c)")[:, 0:COLS]]
        ok_row = wide[:, :, :, :].rearrange("p a b c -> p (a b c)")[:, COLS:2 * COLS]
        row_f = tabf[:, COLS * H:COLS * (H + 1)]
        tile_i = tabf[:, COLS * (H + 1):COLS * (H + 2)].bitcast(I32)
        batch_i = tabf[:, COLS * (H + 2):COLS * (H + 3)].bitcast(I32)

        bank = [ctx.enter_context(nc.psum_tensor(f"bank{n}", [P, 512], F32)) for n in range(8)]

        rounds = sem("gather_rounds", False)
        gathered = [sem(f"gathered{g}", False) for g in range(RING)]
        scattered = [sem(f"scattered{u}", False) for u in range(G)]
        sums_zeroed = sem("sums_zeroed", False)
        gcount = [0]

        v, s_, t_, q_ = nc.vector, nc.scalar, nc.tensor, nc.gpsimd

        loaded_dst, loaded_w, loaded_x = sem("loaded_dst"), sem("loaded_w"), sem("loaded_x")
        iota_made, const_made = sem("iota_made"), sem("const_made")
        prep_v = sem("prep_vector")
        node_out, steps_got, keys_done, tiles_done = sem("node_out"), sem("steps_got"), sem("keys_done"), sem("tiles_done")
        rows_ready, rows_T, rows_kept = sem("rows_ready"), sem("rows_T"), sem("rows_kept")
        w_T, scratch_used, node_in = sem("w_T"), sem("scratch_used"), sem("node_in")
        tile_row_done, keys_T = sem("tile_row_done"), sem("keys_T")

        NW = [0]
        with nc.Block() as block:
            @block.sync
            def _(sp):
                with nc.allow_non_contiguous_dma(reason="last dst of each tile, columns of biases"):
                    sp.dma_start(last_i[:, :], edge_i[:, 2 * P - 1:2 * P].rearrange("t one -> one t")).then_inc(loaded_dst, 16)

                    def w(dst, src):
                        NW[0] += 16
                        sp.dma_start(dst, src).then_inc(loaded_w, 16)

                    def row(dst, vec):
                        w(dst, vec.partition_broadcast(P))

                    w(w_in[:, 0, :], W_att_w)
                    w(w_in[:, 1, :], W1_w)
                    w(w_in[:, 2, :], W2_w)
                    w(a2[:, :], a_vec.rearrange("(c o) one -> o (c one)", c=2))
                    w(ab[:, :], W_att_b.rearrange("(o one) -> o one", one=1))
                    row(b0[:, 0:D], W1_b)
                    row(b2[:, :], W2_b)
                    w(wkv[:, 0:D], Wk)
                    w(wkv[:, D:2 * D], Wv)
                    w(wq[:, :], Wq)
                    row(web[:, :], We.rearrange("c h -> (c h)"))
                    w(wo[:, :], Wo)
                    w(boc[:, :], bo.rearrange("(o one) -> o one", one=1))
                    w(wm[:, :, :], Wm.rearrange("(c p) o -> p c o", p=P))
                    row(bmb[:, :], bm)
                    w(we1[:, :, :], We1.rearrange("(c p) o -> p c o", p=P))
                    row(be1b[:, :], be1)
                    w(we2[0:EH, :], We2)
                    w(we2[EH:EH + 1, :], be2.rearrange("(one o) -> one o", one=1))
                    w(wn1[:, 0, :], Wn1[0:D, :])
                    w(wn1[0:EH, 1, :], Wn1[D:D + EH, :])
                    w(bn1c[:, :], bn1.rearrange("(o one) -> o one", one=1))
                    w(wn2[:, :], Wn2)
                    row(bn2b[:, :], bn2)
                    w(wg1[:, :], G1)
                    w(wg2[:, :], G2)
                    w(bg1c[:, :], g1b.rearrange("(o one) -> o one", one=1))
                    row(bg2[:, :], g2b)
                    sp.dma_start(xs[:, :, :], x.rearrange("(t p) d -> p t d", p=P)).then_inc(loaded_x, 16)
                    sp.wait_ge(tiles_done, 1)
                    sp.dma_start(step_node_dram.rearrange("(b p) -> p b", p=P), part_i[:, :]).then_inc(node_out, 16)
                    sp.wait_ge(node_out, 16)
                    sp.dma_start(step_node[:, :], step_node_dram.rearrange("(one s) -> one s", one=1)).then_inc(node_in, 16)
                sp.wait_ge(loaded_x, 16)
                sp.wait_ge(loaded_w, NW[0])
                sp.wait_ge(node_in, 16)

            @block.gpsimd
            def _(pool):
                q_.iota(iota_i[:, :], pattern=[[1, P]], base=0, channel_multiplier=0).then_inc(iota_made, 1)
                q_.iota(part_i[:, :], pattern=[[P, SB]], base=0, channel_multiplier=1).then_inc(iota_made, 1)
                q_.iota(src_i[0:1, 0:ET], pattern=[[1, ET]], base=0, channel_multiplier=0).then_inc(iota_made, 1)
                q_.memset(ident[:, :], 0.0).then_inc(iota_made, 1)
                pool.wait_ge(iota_made, 4)
                q_.affine_select(out=ident[:, :], in_=ident[:, :], compare_op=ALU.not_equal, fill=1.0,
                                 base=0, pattern=[[-1, P]], channel_multiplier=1).then_inc(const_made, 1)
                pool.wait_ge(keys_done, 1)
                for b in range(SB):
                    at = bass.IndirectOffsetOnAxis(ap=put_i[:, :, :].rearrange("p a b -> p (a b)")[:, b:b + 1].bitcast(U32), axis=0)
                    q_.indirect_dma_start(got_i[:, b, :], None, edge_i, at).then_inc(steps_got, 16)
                    q_.indirect_dma_start(got_f[:, b, :], None, edge_f, at).then_inc(steps_got, 16)
                pool.wait_ge(scratch_used, 1)
                q_.memset(acc[:, :, :], 0.0)

            @block.vector
            def _(dve):
                ch = Chain(dve, prep_v)
                dve.wait_ge(iota_made, 3)
                ch(v.tensor_copy(iota[:, :], iota_i[:, :]))
                ch(v.tensor_copy(part[:, :], part_i[:, :]))
                ch(v.memset(ones[:, :], 1.0))
                ch(v.memset(eps[:, :], EPS))
                ch(v.memset(one_row[:, :], 1.0))
                ch(v.tensor_copy(kv_row[:, :], src_i[0:1, 0:ET]))
                dve.wait_ge(loaded_dst, 16)
                ch(v.tensor_scalar(out=last_i[:, :], in0=last_i[:, :], scalar1=7, scalar2=None, op0=ALU.logical_shift_right))
                ch.wait()
                ch(v.tensor_copy(junk[0:1, :, :].rearrange("p a b -> p (a b)")[:, 0:ET], last_i[:, :]))
                ch(v.tensor_copy(iota_b[:, :], iota[:, :]))
                ch.wait()
                ch(v.tensor_scalar(out=tri[:, :], in0=iota[:, :], scalar1=part[:, 0:1], scalar2=None, op0=ALU.is_lt))
                ch(v.tensor_scalar(out=far[:, 0:1], in0=part[:, 0:1], scalar1=float(FAR), scalar2=None, op0=ALU.add))
                ch(v.tensor_scalar(out=far[:, 1:2], in0=part[:, 0:1], scalar1=float(NP), scalar2=None, op0=ALU.add))
                v.tensor_add(kv_row[:, :], kv_row[:, :], junk[0:1, :, :].rearrange("p a b -> p (a b)")[:, 0:ET]).then_inc(tile_row_done, 1)
                dve.wait_ge(const_made, 1)
                ch(v.tensor_copy(ident_b[:, :], ident[:, :]))
                dve.wait_ge(keys_T, 1)
                ch(v.tensor_copy(keys[:, 0:512], bank[0][:, 0:512]))
                ch(v.tensor_copy(keys[:, 512:ET], bank[1][:, 0:ET - 512]))
                ch.wait()
                for b in range(SB):
                    ch(v.scalar_tensor_tensor(out=tabf[:, b * ET:(b + 1) * ET], in0=keys[:, :], scalar=part[:, b:b + 1],
                                              in1=one_row[:, :], op0=ALU.is_lt, op1=ALU.mult,
                                              accum_out=small[:, 0, b:b + 1]))
                ch.wait()
                ch(v.tensor_scalar(out=small[:, 1, 0:SB], in0=small[:, 0, 0:SB], scalar1=float(ET - 1), scalar2=None, op0=ALU.min))
                ch.wait()
                v.tensor_copy(put_i[:, :, :].rearrange("p a b -> p (a b)")[:, 0:SB], small[:, 1, 0:SB]).then_inc(keys_done, 1)
                ch(v.tensor_sub(small[:, 2, 0:SB], part[:, :], small[:, 1, 0:SB]))
                ch.wait()
                ch(v.tensor_scalar(out=small[:, 0, 0:SB], in0=small[:, 2, 0:SB], scalar1=float(NT - 1), scalar2=None, op0=ALU.min))
                ch.wait()
                v.tensor_copy(part_i[:, :], small[:, 0, 0:SB]).then_inc(tiles_done, 1)
                ch(v.tensor_scalar(out=small[:, 3, 0:SB], in0=small[:, 2, 0:SB], scalar1=float(P), scalar2=None, op0=ALU.mult))
                dve.wait_ge(steps_got, 32 * SB)
                ch(v.tensor_copy(got_if, got_i))
                ch.wait()
                for b in range(SB):
                    last = v.tensor_scalar(out=got_if[:, b, P:2 * P], in0=got_if[:, b, P:2 * P],
                                           scalar1=small[:, 3, b:b + 1], scalar2=None, op0=ALU.subtract)
                last.then_inc(rows_ready, 1)
                for b in range(SB):
                    at = slice(b * P, (b + 1) * P)
                    dve.wait_ge(rows_T, b + 1)
                    c0, c1 = bank[2 * (b % 2)], bank[2 * (b % 2) + 1]
                    ch(v.tensor_copy(src_f[:, at], c0[:, 0:P]))
                    ch(v.tensor_copy(rel[:, at], c0[:, P:2 * P]))
                    ch(v.tensor_copy(ew[:, at], c0[:, 2 * P:3 * P]))
                    ch(v.tensor_copy(attr[0][:, at], c0[:, 3 * P:4 * P]))
                    ch(v.tensor_copy(attr[1][:, at], c1[:, 0:P]))
                    v.tensor_copy(attr[2][:, at], c1[:, P:2 * P]).then_inc(rows_kept, 1)
                dve.wait_ge(rows_kept, SB)
                ch.wait()
                ch(v.tensor_copy(src_i[:, :], src_f))
                ch.wait()
                ch(v.tensor_scalar(out=tile_i, in0=src_i[:, :], scalar1=P.bit_length() - 1, scalar2=None, op0=ALU.logical_shift_right))
                ch(v.tensor_scalar(out=batch_i, in0=src_i[:, :], scalar1=(BT * P).bit_length() - 1, scalar2=None, op0=ALU.logical_shift_right))
                ch(v.tensor_scalar(out=row_f, in0=src_f, scalar1=float(BT), scalar2=None, op0=ALU.mult))
                ch.wait()
                ch(v.tensor_copy(src_f, tile_i))
                ch.wait()
                ch(v.scalar_tensor_tensor(out=row_f, in0=src_f, scalar=float(1 - BT * P), in1=row_f, op0=ALU.mult, op1=ALU.add))
                ch.wait()
                ch(v.tensor_copy(src_f, batch_i))
                ch.wait()
                ch(v.scalar_tensor_tensor(out=row_f, in0=src_f, scalar=float(BT * P - BT), in1=row_f, op0=ALU.mult, op1=ALU.add))
                ch(v.tensor_scalar(out=ok_row, in0=rel[:, :], scalar1=0.0, scalar2=None, op0=ALU.is_ge))
                ch.wait()
                ch(v.scalar_tensor_tensor(out=ok_row, in0=rel[:, :], scalar=float(P), in1=ok_row, op0=ALU.is_lt, op1=ALU.mult))
                ch.wait()
                ch(v.scalar_tensor_tensor(out=key[:, :], in0=row_f, scalar=far[:, 0:1], in1=ok_row, op0=ALU.subtract, op1=ALU.mult))
                ch.wait()
                ch(v.tensor_scalar(out=key[:, :], in0=key[:, :], scalar1=far[:, 0:1], scalar2=None, op0=ALU.add))
                ch(v.tensor_scalar(out=ok_row, in0=ok_row, scalar1=-1.0, scalar2=BIG, op0=ALU.add, op1=ALU.mult))
                ch(v.memset(neg_max[:, :], BIG))
                v.memset(top[:, :], -BIG).then_inc(scratch_used, 1)
                ch(v.memset(b0[:, D:D + 1], 1.0))
                ch(v.memset(b0[:, D + 2:AW], 0.0))
                ch(v.memset(w0[:, D:AW], 0.0))
                ch.wait()
                dve.wait_ge(w_T, 1)
                ch(v.tensor_copy(w0[:, 0:D], bank[4][:, 0:D]))
                ch(v.tensor_copy(w2T[:, :], bank[4][:, D:2 * D]))
                ch(v.tensor_copy(w0[:, D + 1:D + 2], bank[5][:, 0:1]))
                ch(v.tensor_copy(wad[:, 0:1], bank[5][:, 1:2]))
                ch(v.tensor_copy(b0[:, D + 1:D + 2], bank[5][:, 2:3]))
                ch(v.tensor_copy(wad[:, 1:2], bank[5][:, 3:4]))
                ch.wait()

            @block.tensor
            def _(pe):
                pe.wait_ge(tile_row_done, 1)
                t_.matmul(bank[0][:, 0:512], ones[0:1, :], kv_row[:, 0:512], start=True, stop=True)
                t_.matmul(bank[1][:, 0:ET - 512], ones[0:1, :], kv_row[:, 512:ET], start=True, stop=True).then_inc(keys_T, 1)
                pe.wait_ge(const_made, 1)
                pe.wait_ge(loaded_w, NW[0])
                t_.transpose(bank[4][:, 0:D], w_in[:, 1, :], ident[:, :])
                t_.transpose(bank[4][:, D:2 * D], w_in[:, 2, :], ident[:, :])
                t_.matmul(bank[5][:, 0:2], w_in[:, 0, :], a2[:, :], start=True, stop=True)
                t_.matmul(bank[5][:, 2:4], ab[:, 0:1].to_broadcast([P, P]), a2[:, :], start=True, stop=True).then_inc(w_T, 1)
                pe.wait_ge(rows_ready, 1)
                for b in range(SB):
                    if b >= 2:
                        pe.wait_ge(rows_kept, b - 1)
                    c0, c1 = bank[2 * (b % 2)], bank[2 * (b % 2) + 1]
                    t_.transpose(c0[:, 0:P], got_if[:, b, 0:P], ident[:, :])
                    t_.transpose(c0[:, P:2 * P], got_if[:, b, P:2 * P], ident[:, :])
                    t_.transpose(c0[:, 2 * P:3 * P], got_f[:, b, 0:P], ident[:, :])
                    t_.transpose(c0[:, 3 * P:4 * P], got_f[:, b, P:2 * P], ident[:, :])
                    t_.transpose(c1[:, 0:P], got_f[:, b, 2 * P:3 * P], ident[:, :])
                    t_.transpose(c1[:, P:2 * P], got_f[:, b, 3 * P:4 * P], ident[:, :]).then_inc(rows_T, 1)

        def tiles(b):
            return bass.ds(b * BT, BT)

        def flat(a):
            return a.rearrange("p a b -> p (a b)")

        def arrived(eng, i, g):
            eng.wait_ge(gathered[g], 16 * G * (gcount[0] + i + 1))

        def place(k, g, placed, *columns):
            for now, every in columns + ((idx_now, src_i),):
                last = s_.copy(now[:, g * G:(g + 1) * G], every[:, bass.ds(k * G, G)])
            last.then_inc(placed, 1)

        def gather(pool, k, g, table, width, placed, table_out):
            pool.wait_ge(table_out, 16 * NB)
            pool.wait_ge(placed, k + 1)
            pool.sem_inc(rounds, 1)
            for u in range(G):
                slot = g * G + u
                q_.indirect_dma_start(ring[:, slot, 0:width], None, table, bass.IndirectOffsetOnAxis(
                    ap=idx_now[:, slot:slot + 1].bitcast(U32), axis=0)).then_inc(gathered[g], 16)

        def node_regs(eng, name, sets=2):
            return [[eng.alloc_register(f"{name}{j}{u}") for u in range(G)] for j in range(sets)]

        def load_nodes(eng, regs, k, g):
            eng.reg_load(regs[g % len(regs)], step_node[0:1, bass.ds(k * G, G)])

        def nodes_of(eng, regs, g):
            return [eng.snap(r, min_val=0, max_val=NT - 1) for r in regs[g % len(regs)]]

        def hots(g):
            return dict(in0=iota[:, :].unsqueeze(1).to_broadcast([P, G, P]),
                        in1=rel_now[:, g * G:(g + 1) * G].unsqueeze(2).to_broadcast([P, G, P]), op=ALU.is_equal)

        def batch_rounds(eng, batch):
            batch(0, 0, 2)
            batch(1, 1, 2)
            with eng.Fori(2, NB - 2) as b:
                batch(b, 2, 2)
            batch(NB - 2, 2, 1)
            batch(NB - 1, 2, 0)

        NORM = BT + 1

        def norm_stats(ch, y, var):
            for u in range(BT):
                ch(v.bn_stats(out=stat[:, u, 0:6], in_=y[:, u, :]))
            ch.wait()
            ch.eng.sem_inc(rounds, 1)
            for u in range(BT):
                last = v.bn_aggr(out=mv[:, u, :], in_=stat[:, u, 0:6])
            last.then_inc(var, 1)

        def normalize(ch, b, y, outs, std):
            ch.eng.wait_ge(std, b + 1)
            ch(v.reciprocal(stat[:, :, 6], stat[:, :, 6]))
            ch.wait()
            for u in range(BT):
                last = v.tensor_scalar(out=outs[u], in0=y[:, u, :], scalar1=mv[:, u, 0:1], scalar2=stat[:, u, 6:7],
                                       op0=ALU.subtract, op1=ALU.mult)
            return last

        def root(act, b, var, std):
            act.wait_ge(var, b + 1)
            s_.activation(stat[:, :, 6], mv[:, :, 1], ACT.Sqrt, bias=eps[:, 0:1]).then_inc(std, 1)

        x_staged, x_T, xT_kept, t0_mm, t0_kept, score_mm, t0_out, t0_free, n0_v = (
            sem(f"n0_{n}") for n in ("x_staged", "x_T", "xT_kept", "t0_mm", "t0_kept", "score_mm", "t0_out", "t0_free", "vector"))
        SHARE = -(-STEPS // NB)
        assert SHARE * NB <= COLS
        with nc.Block() as block:
            @block.gpsimd
            def _(pool):
                pool.sem_inc(x_T, 1)
                with pool.Fori(0, NB) as b:
                    pool.wait_ge(x_T, b + 1)
                    pool.sem_inc(rounds, 1)
                    q_.tensor_copy(tX[:, :, :], xs[:, tiles(b), :]).then_inc(x_staged, 1)

            @block.tensor
            def _(pe):
                with pe.Fori(0, NB) as b:
                    pe.wait_ge(x_staged, b + 1)
                    for u in range(BT):
                        last = t_.transpose(bank[0][:, u * P:(u + 1) * P], tX[:, u, :], ident[:, :])
                    last.then_inc(x_T, 1)
                    pe.wait_ge(xT_kept, b + 1)
                    pe.wait_ge(t0_kept, b + 1)
                    for u in range(BT):
                        last = t_.matmul(bank[1 + u // 2][:, (u % 2) * AW:(u % 2 + 1) * AW],
                                         rT[:, 0, u * P:(u + 1) * P], w0[:, :], start=True, stop=True)
                    last.then_inc(t0_mm, 1)
                    t_.matmul(bank[3][:, :], wad[:, 0:1].to_broadcast([P, P]), rT[:, 0, :], start=True, stop=True).then_inc(score_mm, 1)

            @block.scalar
            def _(act):
                with act.Fori(0, NB) as b:
                    act.wait_ge(x_T, b + 2)
                    s_.copy(rT[:, 0, :], bank[0][:, :]).then_inc(xT_kept, 1)
                    act.wait_ge(score_mm, b + 1)
                    s_.activation(dst_score[:, bass.ds(b * BT * P, BT * P)], bank[3][:, :], ACT.Identity, bias=wad[:, 1:2])

            @block.vector
            def _(dve):
                def biases(b):
                    ch = Chain(dve, n0_v, 3 * H * b)
                    cols = bass.ds(b * SHARE, SHARE)
                    for h in range(H):
                        ch(v.scalar_tensor_tensor(out=bias[:, cols, h], in0=attr[0][:, cols], scalar=web[:, h:h + 1],
                                                  in1=ok_row[:, cols], op0=ALU.mult, op1=ALU.add))
                    for c in (1, 2):
                        ch.wait()
                        for h in range(H):
                            ch(v.scalar_tensor_tensor(out=bias[:, cols, h], in0=attr[c][:, cols],
                                                      scalar=web[:, c * H + h:c * H + h + 1],
                                                      in1=bias[:, cols, h], op0=ALU.mult, op1=ALU.add))

                dve.sem_inc(t0_kept, 1)
                with dve.Fori(0, NB) as b:
                    dve.wait_ge(t0_mm, b + 1)
                    dve.wait_ge(t0_free, b + 1)
                    for j in range(2):
                        last = v.tensor_add(tT0[:, 2 * j:2 * j + 2, :],
                                            bank[1 + j][:, 0:2 * AW].rearrange("p (t c) -> p t c", t=2),
                                            b0[:, :].unsqueeze(1).to_broadcast([P, 2, AW]))
                    last.then_inc(t0_kept, 1)
                    biases(b)

            @block.sync
            def _(sp):
                for u in range(G):
                    sp.dma_start(mlp_sum[u].rearrange("(p r) f -> p (r f)", p=P),
                                 acc[:, :, :].rearrange("p t c -> p (t c)")[:, 0:(NT + 1) * EH]).then_inc(sums_zeroed, 16)
                sp.sem_inc(t0_free, 1)
                with sp.Fori(0, NB) as b:
                    sp.wait_ge(t0_kept, b + 2)
                    sp.dma_start(t0.rearrange("(t p) c -> p t c", p=P)[:, tiles(b), :], tT0[:, :, :]).then_inc(t0_out, 16)
                    sp.wait_ge(t0_out, 16 * b + 16)
                    sp.sem_inc(t0_free, 1)
                sp.wait_ge(sums_zeroed, 16 * G)

        l0_placed, l0_logit, l0_wide, l0_sum, l0_v, l0_p = (
            sem(f"l0_{n}") for n in ("placed", "logit", "wide", "sum", "vector", "prob"))
        l0_acc = [sem(f"l0_acc{u}") for u in range(G)]
        with nc.Block() as block:
            @block.gpsimd
            def _(pool):
                with pool.Fori(0, ITERS) as i:
                    for g in range(RING):
                        gather(pool, i * RING + g, g, t0, AW, l0_placed, t0_out)

            @block.scalar
            def _(act):
                for k in range(RING):
                    place(k, k, l0_placed, (rel_now, rel), (ew_now, ew))
                with act.Fori(0, ITERS) as i:
                    for g in range(RING):
                        k = i * RING + g
                        act.wait_ge(l0_logit, k + 1)
                        s_.activation(small[:, g, 0:G], lg[:, g, 1, 0:G], ACT.Exp).then_inc(l0_p, 1)
                        s_.copy(wide[:, g, :, D + 1], ew_now[:, g * G:(g + 1) * G])
                        act.wait_ge(l0_p, k + 1)
                        for u in range(G):
                            last = s_.activation(wide[:, g, u, 0:D + 1], ring[:, g * G + u, 0:D + 1], ACT.Identity,
                                                 scale=small[:, g, u:u + 1])
                        last.then_inc(l0_wide, 1)
                        act.wait_ge(l0_wide, k + 1)
                        place(k + RING, g, l0_placed, (rel_now, rel), (ew_now, ew))

            @block.tensor
            def _(pe):
                with pe.Fori(0, ITERS) as i:
                    for g in range(RING):
                        k = i * RING + g
                        pe.wait_ge(l0_wide, k + 1)
                        pe.wait_ge(l0_acc[G - 1], k + 1)
                        for u in range(G):
                            last = t_.matmul(bank[2 * (g % 2) + u // 2][:, (u % 2) * AW:(u % 2) * AW + D + 2],
                                             hotf[:, g, u, :], wide[:, g, u, 0:D + 2], start=True, stop=True)
                        last.then_inc(l0_sum, 1)

            @block.vector
            def _(dve):
                regs = node_regs(dve, "l0_node", RING)

                def step(i, g, past):
                    k = i * RING + g
                    ch = Chain(dve, l0_v, 2 * k)
                    add = back(*later(i, g, -2)) if past >= 2 else lambda u: None
                    nodes = nodes_of(dve, regs, g)
                    dve.wait_ge(l0_placed, k + 1)
                    v.tensor_tensor(out=hotf[:, g, :, :], **hots(g))
                    add(0)
                    for u in range(G):
                        last = v.scalar_tensor_tensor(out=junk[:, 0, u * P:(u + 1) * P], in0=iota[:, :],
                                                      scalar=rel_now[:, g * G + u:g * G + u + 1],
                                                      in1=dst_score[:, bass.ds(nodes[u] * P, P)],
                                                      op0=ALU.is_equal, op1=ALU.mult, accum_out=small[:, g, G + u:G + u + 1])
                        if u == 1:
                            add(1)
                    ch(last)
                    add(2)
                    arrived(dve, i, g)
                    ch.wait()
                    ch(v.tensor_add(lg[:, g, 0, 0:G], ring[:, g * G:(g + 1) * G, D + 1], small[:, g, G:2 * G]))
                    add(3)
                    ch.wait()
                    v.scalar_tensor_tensor(out=lg[:, g, 1, 0:G], in0=lg[:, g, 0, 0:G], scalar=0.01, in1=lg[:, g, 0, 0:G],
                                           op0=ALU.mult, op1=ALU.max).then_inc(l0_logit, 1)

                def back(i, g):
                    k = i * RING + g
                    nodes = nodes_of(dve, regs, g)

                    def add(u):
                        here = flat(acc[:, bass.ds(nodes[u], 1), 0:D + 2])
                        if u:
                            dve.wait_ge(l0_acc[u - 1], k + 1)
                        else:
                            dve.wait_ge(l0_sum, k + 1)
                            dve.wait_ge(l0_acc[G - 1], k + 2)
                        v.tensor_add(here, here, bank[2 * (g % 2) + u // 2][:, (u % 2) * AW:(u % 2) * AW + D + 2]).then_inc(l0_acc[u], 1)
                    return add

                def step_and_load(i, g, past, left):
                    step(i, g, past)
                    if left:
                        j, h = later(i, g, 1)
                        load_nodes(dve, regs, j * RING + h, h)

                dve.sem_inc(l0_acc[G - 1], 2)
                load_nodes(dve, regs, 0, 0)
                edge_rounds(dve, step_and_load)
                for g in range(RING - 2, RING):
                    add = back(ITERS - 1, g)
                    for u in range(G):
                        add(u)
        gcount[0] += ITERS


        (n1_hn, n1_c, n1_mixed, n1_prod, n1_prodT, n1_prodT_kept, n1_mm, n1_xn, n1_xnT, n1_xnT_kept, n1_kv_mm, n1_q_mm, n1_kv_kept, n1_q0,
         n1_cx, n1_q_rest, n1_q1, n1_split, t1_out, t1_free, n1_copied, n1_v, n1_deg, n1_dis, n1_var, n1_std) = (sem(f"n1_{n}") for n in (
             "hn", "c", "mixed", "prod", "prodT", "prodT_kept", "mm", "xn", "xnT", "xnT_kept", "kv_mm", "q_mm", "kv_kept", "q0",
             "c_x", "q_rest", "q1", "split", "t1_out", "t1_free", "copied", "vector", "deg", "dis", "var", "std"))
        N1 = 2 + NORM
        with nc.Block() as block:
            @block.vector
            def _(dve):
                def front(b, before=True):
                    x_b = xs[:, tiles(b), :]
                    if before:
                        dve.wait_ge(n1_cx, b)
                        dve.wait_ge(n1_prodT, b)
                    v.tensor_tensor(out=tA, in0=acc[:, tiles(b), 0:D], in1=rs[:, tiles(b), 0:1].to_broadcast([P, BT, D]),
                                    op=ALU.mult).then_inc(n1_hn, 1)
                    dve.wait_ge(n1_hn, b + 1)
                    v.tensor_tensor(out=tB, in0=tA, in1=x_b, op=ALU.mult).then_inc(n1_prod, 1)

                def rest(b):
                    dve.wait_ge(n1_q0, b + 1)
                    v.scalar_tensor_tensor(out=tX, in0=bank[5][:, :].rearrange("p (t d) -> p t d", t=BT), scalar=SCALE,
                                           in1=look[:, tiles(b), 0:D], op0=ALU.mult, op1=ALU.subtract).then_inc(n1_q_rest, 1)

                def last_part(b):
                    dve.wait_ge(n1_q1, b + 1)
                    v.tensor_sub(look[:, tiles(b), 2 * D:3 * D], tX, look[:, tiles(b), D:2 * D]).then_inc(n1_split, 1)

                def batch(b, past, left):
                    ch = Chain(dve, n1_v, N1 * b + 6)
                    if past:
                        dve.wait_ge(n1_xn, b)
                    dve.wait_ge(n1_mm, b + 1)
                    dve.wait_ge(n1_c, b + 1)
                    v.tensor_tensor(out=flat(tY), in0=bank[1][:, :], in1=flat(tC), op=ALU.add).then_inc(n1_mixed, 1)
                    dve.wait_ge(n1_mixed, b + 1)
                    ch(v.scalar_tensor_tensor(out=flat(tY), in0=flat(tY), scalar=0.01, in1=flat(tY), op0=ALU.mult, op1=ALU.max))
                    ch.wait()
                    ch(v.tensor_tensor(out=tY, in0=tY, in1=xs[:, tiles(b), :], op=ALU.add))
                    ch.wait()
                    norm_stats(ch, tY, n1_var)
                    if past > 1:
                        last_part(b - 2)
                    dve.wait_ge(n1_copied, b + 1)
                    if past:
                        dve.wait_ge(n1_xnT, b)
                    normalize(ch, b, tY, [tN[:, u, :] for u in range(BT)], n1_std).then_inc(n1_xn, 1)
                    if past:
                        rest(b - 1)
                    if left > 1:
                        front(b + 2)
                    assert ch.n == N1

                ch = Chain(dve, n1_v)
                deg = neg_max[:, 0:NT]
                ch(v.tensor_scalar(out=deg, in0=acc[:, :, D + 1], scalar1=1.0, scalar2=None, op0=ALU.add))
                ch(v.tensor_scalar(out=rs[:, :, 0], in0=acc[:, :, D], scalar1=1e-9, scalar2=None, op0=ALU.add))
                ch.wait()
                v.tensor_scalar(out=dis[:, :], in0=deg, scalar1=1e-12, scalar2=None, op0=ALU.max).then_inc(n1_deg, 1)
                ch(v.reciprocal(rs[:, :, 0], rs[:, :, 0]))
                ch.wait()
                front(0, False)
                front(1)
                dve.wait_ge(n1_dis, 1)
                ch(v.reciprocal(dis[:, :], dis[:, :]))
                ch.wait()
                ch(v.scalar_tensor_tensor(out=dis[:, :], in0=deg, scalar=0.0, in1=dis[:, :], op0=ALU.is_gt, op1=ALU.mult))
                ch.wait()
                ch(v.memset(neg_max[:, :], BIG))
                assert ch.n == 6
                batch_rounds(dve, batch)
                last_part(NB - 2)
                dve.wait_ge(n1_split, NB - 1)
                rest(NB - 1)
                last_part(NB - 1)

            @block.tensor
            def _(pe):
                def front(b, before=True):
                    pe.wait_ge(n1_prod, b + 1)
                    for u in range(BT):
                        last = t_.transpose(bank[0][:, u * P:(u + 1) * P], tB[:, u, :], ident[:, :])
                    last.then_inc(n1_prodT, 1)
                    pe.wait_ge(n1_prodT_kept, b + 1)
                    if before:
                        pe.wait_ge(n1_mixed, b)
                    for u in range(BT):
                        last = t_.matmul(bank[1][:, u * P:(u + 1) * P], rT[:, 0, u * P:(u + 1) * P], w2T[:, :], start=True, stop=True)
                    last.then_inc(n1_mm, 1)

                def batch(b, past, left):
                    pe.wait_ge(n1_xn, b + 1)
                    for u in range(BT):
                        done = t_.transpose(bank[2][:, u * P:(u + 1) * P], tN[:, u, :], ident[:, :])
                    done.then_inc(n1_xnT, 1)
                    pe.wait_ge(n1_xnT_kept, b + 1)
                    if past:
                        pe.wait_ge(n1_q_rest, b)
                    for u in range(BT):
                        done = t_.matmul(bank[5][:, u * P:(u + 1) * P], rT[:, 1, u * P:(u + 1) * P], wq[:, :], start=True, stop=True)
                    done.then_inc(n1_q_mm, 1)
                    pe.wait_ge(n1_kv_kept, b + 1)
                    for u in range(BT):
                        done = t_.matmul(bank[3 + u // 2][:, (u % 2) * 2 * D:(u % 2 + 1) * 2 * D],
                                         rT[:, 1, u * P:(u + 1) * P], wkv[:, :], start=True, stop=True)
                    done.then_inc(n1_kv_mm, 1)
                    if left > 1:
                        front(b + 2)

                front(0, False)
                front(1)
                batch_rounds(pe, batch)

            @block.scalar
            def _(act):
                def front(b):
                    act.wait_ge(n1_prodT, b + 1)
                    s_.copy(rT[:, 0, :], bank[0][:, :]).then_inc(n1_prodT_kept, 1)

                def second_part(b):
                    act.wait_ge(n1_q_rest, b + 1)
                    s_.copy(look[:, tiles(b), D:2 * D], tX).then_inc(n1_q1, 1)

                def batch(b, past, left):
                    root(act, b, n1_var, n1_std)
                    act.wait_ge(n1_xnT, b + 1)
                    s_.copy(rT[:, 1, :], bank[2][:, :]).then_inc(n1_xnT_kept, 1)
                    if past:
                        second_part(b - 1)
                    act.wait_ge(n1_q_mm, b + 1)
                    s_.activation(look[:, tiles(b), 0:D], bank[5][:, :].rearrange("p (t d) -> p t d", t=BT), ACT.Copy,
                                  scale=SCALE).then_inc(n1_q0, 1)
                    act.wait_ge(n1_kv_mm, b + 1)
                    act.wait_ge(t1_free, b + 1)
                    s_.copy(flat(tKV[:, 0:2, :]), bank[3][:, :])
                    s_.copy(flat(tKV[:, 2:4, :]), bank[4][:, :]).then_inc(n1_kv_kept, 1)
                    if left > 1:
                        front(b + 2)

                act.sem_inc(n1_kv_kept, 1)
                act.wait_ge(n1_deg, 1)
                s_.activation(dis[:, :], dis[:, :], ACT.Sqrt).then_inc(n1_dis, 1)
                front(0)
                front(1)
                batch_rounds(act, batch)
                second_part(NB - 1)

            @block.gpsimd
            def _(pool):
                def front(b, before=True):
                    if before:
                        pool.wait_ge(n1_mixed, b)
                    pool.wait_ge(n1_hn, b + 1)
                    pool.sem_inc(rounds, 1)
                    q_.tensor_tensor(out=tC, in0=tA, in1=xs[:, tiles(b), :], op=ALU.add).then_inc(n1_cx, 1)
                    pool.wait_ge(n1_cx, b + 1)
                    q_.tensor_tensor(out=tC, in0=tC, in1=b2[:, :].unsqueeze(1).to_broadcast([P, BT, D]), op=ALU.add).then_inc(n1_c, 1)

                def batch(b, past, left):
                    if left:
                        front(b + 1)
                    pool.wait_ge(n1_xn, b + 1)
                    pool.sem_inc(rounds, 1)
                    q_.tensor_copy(xs[:, tiles(b), :], tN).then_inc(n1_copied, 1)

                pool.sem_inc(n1_copied, 1)
                front(0, False)
                batch_rounds(pool, batch)
                q_.memset(acc[:, :, :], 0.0)

            @block.sync
            def _(sp):
                sp.sem_inc(t1_free, 1)
                with sp.Fori(0, NB) as b:
                    sp.wait_ge(n1_kv_kept, b + 2)
                    sp.dma_start(t1.rearrange("(t p) c -> p t c", p=P)[:, tiles(b), :], tKV).then_inc(t1_out, 16)
                    sp.wait_ge(t1_out, 16 * b + 16)
                    sp.sem_inc(t1_free, 1)

        (l1_placed, l1_away, l1_hot, l1_hotT, l1_hot_kept, l1_q, l1_gm, l1_gmT, l1_top, l1_topB, l1_neg, l1_p, l1_wide, l1_sum,
         l1_v) = (sem(f"l1_{n}") for n in (
             "placed", "away", "hot", "hotT", "hot_kept", "query", "group_max", "group_max_T", "top", "top_spread", "neg_top", "prob",
             "wide", "sum", "vector"))
        l1_acc = [sem(f"l1_acc{u}") for u in range(G)]
        TR, QB, MB, SUM = bank[0], (bank[1], bank[2]), bank[3], 4
        with nc.Block() as block:
            @block.gpsimd
            def _(pool):
                with pool.Fori(0, ITERS) as i:
                    for g in range(RING):
                        gather(pool, i * RING + g, g, t1, 2 * D, l1_placed, t1_out)

            @block.scalar
            def _(act):
                away = junk[:, 1, :]

                def place1(k, g):
                    s_.copy(rel_now[:, g * G:(g + 1) * G], rel[:, bass.ds(k * G, G)])
                    s_.copy(bias_now[:, g, :], tabf[:, bass.ds(k * G * H, G * H)])
                    place(k, g, l1_placed)

                def far_away(i, g, past):
                    k = i * RING + g
                    act.wait_ge(l1_placed, k + 1)
                    if past:
                        act.wait_ge(l1_hot, k)
                    for u in range(G):
                        last = s_.activation(away[:, u * P:(u + 1) * P], iota[:, :], ACT.Abs, scale=-1.0,
                                             bias=rel_now[:, g * G + u:g * G + u + 1])
                    last.then_inc(l1_away, 1)

                def one_hot(i, g, past):
                    k = i * RING + g
                    if past >= RING:
                        act.wait_ge(l1_sum, k - RING + 1)
                    act.wait_ge(l1_away, k + 1)
                    s_.activation(flat(hotf[:, g, :, :]), away, ACT.Relu, scale=-1.0, bias=1.0)
                    s_.activation(flat(hot[:, g, :, :]), away, ACT.Relu, scale=-1.0, bias=1.0).then_inc(l1_hot, 1)

                def keep_hot(i, g):
                    act.wait_ge(l1_hotT, i * RING + g + 1)
                    s_.copy(hotT[:, g, :], TR[:, :].bitcast(BF16)[:, 0:G * P]).then_inc(l1_hot_kept, 1)

                def weights(i, g):
                    act.wait_ge(l1_neg, i * RING + g + 1)
                    s_.activation(wide[:, g, :, D:AW], lg[:, g, 1, :].rearrange("p (u h) -> p u h", u=G), ACT.Exp,
                                  bias=small[:, g, 1:2])
                    s_.activation(small[:, g, 2:3], small[:, (g - 1) % RING, 1:2], ACT.Exp, scale=-1.0,
                                  bias=small[:, g, 1:2]).then_inc(l1_p, 1)

                def step(i, g, past, left):
                    k = i * RING + g
                    if left > 1:
                        far_away(*later(i, g, 2), past + 2)
                    if past:
                        weights(*later(i, g, -1))
                    if left > 1:
                        one_hot(*later(i, g, 2), past + 2)
                        keep_hot(*later(i, g, 2))
                    if past:
                        act.wait_ge(l1_wide, k)
                        place1(k + RING - 1, (g + RING - 1) % RING)

                for k in range(RING):
                    place1(k, k)
                for g in range(2):
                    far_away(0, g, g)
                    one_hot(0, g, g)
                    keep_hot(0, g)
                edge_rounds(act, step)
                weights(ITERS - 1, RING - 1)

            @block.tensor
            def _(pe):
                regs = node_regs(pe, "l1_q")

                def turn(i, g):
                    pe.wait_ge(l1_hot, i * RING + g + 1)
                    for u in range(G):
                        last = t_.transpose(TR[:, :].bitcast(BF16)[:, u * P:(u + 1) * P], hot[:, g, u, :], ident_b[:, :])
                    last.then_inc(l1_hotT, 1)

                def query(i, g):
                    load_nodes(pe, regs, i * RING + g, g)
                    nodes = nodes_of(pe, regs, g)
                    pe.wait_ge(l1_hot_kept, i * RING + g + 1)
                    for u in range(G):
                        for c in range(3):
                            last = t_.matmul(QB[g % 2][:, u * P:(u + 1) * P], hotT[:, g, u * P:(u + 1) * P],
                                             flat(look[:, bass.ds(nodes[u], 1), c * D:(c + 1) * D]), start=(c == 0), stop=(c == 2))
                    last.then_inc(l1_q, 1)

                def summed(i, g):
                    k = i * RING + g
                    pe.wait_ge(l1_wide, k + 1)
                    pe.wait_ge(l1_acc[G - 1], k + 1)
                    for u in range(G):
                        last = t_.matmul(bank[SUM + 2 * (g % 2) + u // 2][:, (u % 2) * AW:(u % 2 + 1) * AW],
                                         hotf[:, g, u, :], wide[:, g, u, :], start=True, stop=True)
                    last.then_inc(l1_sum, 1)

                def step(i, g, past, left):
                    k = i * RING + g
                    if past >= 2:
                        summed(*later(i, g, -2))
                    if left:
                        query(*later(i, g, 1))
                    pe.wait_ge(l1_gm, k + 1)
                    t_.transpose(MB[0:1, 0:P], small[:, g, 0:1], ident[:, :]).then_inc(l1_gmT, 1)
                    if left > 1:
                        turn(*later(i, g, 2))
                    pe.wait_ge(l1_top, k + 1)
                    t_.matmul(MB[:, P:P + 1], ones[0:1, :], top[:, 0:1], start=True, stop=True).then_inc(l1_topB, 1)

                turn(0, 0)
                query(0, 0)
                turn(0, 1)
                edge_rounds(pe, step)
                summed(ITERS - 1, RING - 2)
                summed(ITERS - 1, RING - 1)

            @block.vector
            def _(dve):
                regs = node_regs(dve, "l1_node")
                L1 = 5

                def add(i, g, u, nodes):
                    k = i * RING + g
                    here = flat(acc[:, bass.ds(nodes[u], 1), :])
                    new = bank[SUM + 2 * (g % 2) + u // 2][:, (u % 2) * AW:(u % 2 + 1) * AW]
                    if u:
                        dve.wait_ge(l1_acc[u - 1], k + 1)
                        v.tensor_add(here, here, new).then_inc(l1_acc[u], 1)
                    else:
                        dve.wait_ge(l1_sum, k + 1)
                        dve.wait_ge(l1_acc[G - 1], k + 2)
                        v.tensor_copy(neg_max[:, bass.ds(nodes[0], G)], small[:, g, 1:2].to_broadcast([P, G]))
                        v.scalar_tensor_tensor(out=here, in0=here, scalar=small[:, g, 2:3], in1=new,
                                               op0=ALU.mult, op1=ALU.add).then_inc(l1_acc[0], 1)

                def widen(i, g):
                    dve.wait_ge(l1_p, i * RING + g + 1)
                    v.tensor_tensor(out=wide[:, g, :, 0:D].rearrange("p u (h d) -> p u h d", h=H),
                                    in0=ring[:, g * G:(g + 1) * G, D:2 * D].rearrange("p u (h d) -> p u h d", h=H),
                                    in1=wide[:, g, :, D:AW].unsqueeze(3).to_broadcast([P, G, H, HD]), op=ALU.mult).then_inc(l1_wide, 1)

                def negate(i, g):
                    dve.wait_ge(l1_topB, i * RING + g + 1)
                    v.tensor_scalar(out=small[:, g, 1:2], in0=MB[:, P:P + 1], scalar1=-1.0, scalar2=None, op0=ALU.mult).then_inc(l1_neg, 1)

                def back(i, g):
                    nodes = nodes_of(dve, regs, g)
                    return lambda u: add(i, g, u, nodes)

                def step(i, g, past, left):
                    k = i * RING + g
                    ch = Chain(dve, l1_v, L1 * k + 1)
                    add_step = back(*later(i, g, -3)) if past >= 3 else lambda u: None
                    arrived(dve, i, g)
                    dve.wait_ge(l1_q, k + 1)
                    prod = junk[:, 0, :]
                    ch(v.tensor_tensor(out=prod.rearrange("p (u d) -> p u d", u=G), in0=QB[g % 2][:, :].rearrange("p (u d) -> p u d", u=G),
                                       in1=ring[:, g * G:(g + 1) * G, 0:D], op=ALU.mult))
                    if past:
                        negate(*later(i, g, -1))
                    add_step(0)
                    ch.wait()
                    ch(v.tensor_reduce(out=lg[:, g, 0, :], in_=prod.rearrange("p (a d) -> p a d", d=HD), axis=AX.X, op=ALU.add))
                    add_step(1)
                    ch.wait()
                    ch(v.tensor_add(lg[:, g, 0, :], lg[:, g, 0, :], bias_now[:, g, :]))
                    ch.wait()
                    ch(v.scalar_tensor_tensor(out=lg[:, g, 1, :], in0=lg[:, g, 0, :], scalar=0.2, in1=lg[:, g, 0, :],
                                              op0=ALU.mult, op1=ALU.max))
                    ch.wait()
                    v.reduce_max(small[:, g, 0:1], lg[:, g, 1, :], axis=AX.X).then_inc(l1_gm, 1)
                    if past:
                        widen(*later(i, g, -1))
                    if past >= 2:
                        load_nodes(dve, regs, k - 2, g - 2)
                    add_step(2)
                    dve.wait_ge(l1_gmT, k + 1)
                    ch(v.reduce_max(top[:, 1:2], MB[0:1, 0:P], axis=AX.X))
                    add_step(3)
                    ch.wait()
                    v.tensor_max(top[:, 0:1], top[:, 0:1], top[:, 1:2]).then_inc(l1_top, 1)
                    assert ch.n == L1

                dve.sem_inc(l1_acc[G - 1], 2)
                v.memset(small[:, RING - 1, 1:2], BIG).then_inc(l1_v, 1)
                edge_rounds(dve, step)
                negate(ITERS - 1, RING - 1)
                widen(ITERS - 1, RING - 1)
                for g in range(1, RING):
                    load_nodes(dve, regs, (ITERS - 1) * RING + g, g)
                    add_step = back(ITERS - 1, g)
                    for u in range(G):
                        add_step(u)
        gcount[0] += ITERS

        with nc.Block() as block:
            @block.sync
            def _(sp):
                for used in early_sems[0::4]:
                    sp.sem_clear(used)

            @block.scalar
            def _(act):
                for used in early_sems[1::4]:
                    act.sem_clear(used)

            @block.vector
            def _(dve):
                for used in early_sems[2::4]:
                    dve.sem_clear(used)

            @block.tensor
            def _(pe):
                for used in early_sems[3::4]:
                    pe.sem_clear(used)
        early.close()
        early_sems = None

        (n2_staged, n2_agg, n2_aggT, n2_aggT_kept, n2_o_mm, n2_o_kept, n2_xT, n2_xT_kept, n2_mm, n2_mixed, n2_var, n2_std, n2_xn, n2_xnT,
         n2_xnT_kept, n2_e_mm, n2_e_kept, n2_e0, n2_e_rest, n2_e1, n2_split, t2_out, t2_free, n2_copied, n2_v, n2_factor) = (
            sem(f"n2_{n}") for n in (
             "staged", "agg", "aggT", "aggT_kept", "o_mm", "o_kept", "xT", "xT_kept", "mm", "mixed", "var", "std", "xn", "xnT", "xnT_kept",
             "e_mm", "e_kept", "e0", "e_rest", "e1", "split", "t2_out", "t2_free", "copied", "vector", "factor"))
        N2 = 1 + NORM
        halves = bank[5][:, :].rearrange("p (t c) -> p t c", t=BT)
        with nc.Block() as block:
            @block.vector
            def _(dve):
                def front(b, before=True):
                    if before:
                        dve.wait_ge(n2_aggT, b)
                    v.tensor_tensor(out=tB.rearrange("p t (h d) -> p t h d", h=H),
                                    in0=acc[:, tiles(b), 0:D].rearrange("p t (h d) -> p t h d", h=H),
                                    in1=rs[:, tiles(b), 0:H].unsqueeze(3).to_broadcast([P, BT, H, HD]), op=ALU.mult).then_inc(n2_agg, 1)

                def rest(b):
                    dve.wait_ge(n2_e0, b + 1)
                    dve.wait_ge(t2_free, b + 1)
                    v.tensor_tensor(out=tT2, in0=halves[:, :, 0:EH], in1=be1b[:, :].unsqueeze(1).to_broadcast([P, BT, EH]),
                                    op=ALU.add).then_inc(n2_e_kept, 1)
                    v.tensor_tensor(out=tC[:, :, 0:EH], in0=halves[:, :, EH:2 * EH], in1=look[:, tiles(b), 0:EH],
                                    op=ALU.subtract).then_inc(n2_e_rest, 1)

                def last_part(b):
                    dve.wait_ge(n2_e1, b + 1)
                    v.tensor_sub(look[:, tiles(b), 2 * EH:3 * EH], tC[:, :, 0:EH], look[:, tiles(b), EH:2 * EH]).then_inc(n2_split, 1)

                def batch(b, past, left):
                    ch = Chain(dve, n2_v, N2 * b + 4)
                    if past:
                        dve.wait_ge(n2_xn, b)
                    dve.wait_ge(n2_mm, b + 1)
                    v.tensor_tensor(out=tA, in0=bank[3][:, :].rearrange("p (t d) -> p t d", t=BT),
                                    in1=bmb[:, :].unsqueeze(1).to_broadcast([P, BT, D]), op=ALU.add).then_inc(n2_mixed, 1)
                    dve.wait_ge(n2_mixed, b + 1)
                    ch(v.scalar_tensor_tensor(out=tY, in0=tA, scalar=0.0, in1=xs[:, tiles(b), :], op0=ALU.max, op1=ALU.add))
                    ch.wait()
                    norm_stats(ch, tY, n2_var)
                    if past > 1:
                        last_part(b - 2)
                    dve.wait_ge(n2_copied, b + 1)
                    if past:
                        dve.wait_ge(n2_xnT, b)
                    normalize(ch, b, tY, [tN[:, u, :] for u in range(BT)], n2_std).then_inc(n2_xn, 1)
                    if past:
                        rest(b - 1)
                    if left > 1:
                        front(b + 2)
                    assert ch.n == N2, ch.n

                ch = Chain(dve, n2_v)
                spread = rs[:, :, H:H + 1].to_broadcast([P, NT, H])
                dve.wait_ge(n2_factor, 1)
                ch(v.tensor_tensor(out=rs[:, :, 0:H], in0=acc[:, :, D:AW], in1=spread, op=ALU.mult))
                ch.wait()
                ch(v.tensor_scalar(out=rs[:, :, 0:H], in0=rs[:, :, 0:H], scalar1=1e-12, scalar2=None, op0=ALU.max))
                ch.wait()
                ch(v.reciprocal(rs[:, :, 0:H], rs[:, :, 0:H]))
                ch.wait()
                ch(v.tensor_tensor(out=rs[:, :, 0:H], in0=rs[:, :, 0:H], in1=spread, op=ALU.mult))
                ch.wait()
                front(0, False)
                front(1)
                batch_rounds(dve, batch)
                last_part(NB - 2)
                dve.wait_ge(n2_split, NB - 1)
                rest(NB - 1)
                last_part(NB - 1)

            @block.tensor
            def _(pe):
                def project(b):
                    pe.wait_ge(n2_staged, b + 1)
                    for u in range(BT):
                        last = t_.transpose(bank[2][:, u * P:(u + 1) * P], tX[:, u, :], ident[:, :])
                    last.then_inc(n2_xT, 1)
                    pe.wait_ge(n2_agg, b + 1)
                    for u in range(BT):
                        last = t_.transpose(bank[0][:, u * P:(u + 1) * P], tB[:, u, :], ident[:, :])
                    last.then_inc(n2_aggT, 1)
                    pe.wait_ge(n2_aggT_kept, b + 1)
                    t_.matmul(bank[1][:, :], wo[:, :], rT[:, 0, :], start=True, stop=True).then_inc(n2_o_mm, 1)

                def mix(b):
                    pe.wait_ge(n2_xT_kept, b + 1)
                    pe.wait_ge(n2_o_kept, b + 1)
                    for u in range(BT):
                        at = slice(u * P, (u + 1) * P)
                        t_.matmul(bank[3][:, at], rT[:, 1, at], wm[:, 0, :], start=True, stop=False)
                        last = t_.matmul(bank[3][:, at], rT[:, 2, at], wm[:, 1, :], start=False, stop=True)
                    last.then_inc(n2_mm, 1)

                def batch(b, past, left):
                    if left:
                        pe.wait_ge(n2_mixed, b + 1)
                        mix(b + 1)
                    pe.wait_ge(n2_xn, b + 1)
                    for u in range(BT):
                        done = t_.transpose(bank[4][:, u * P:(u + 1) * P], tN[:, u, :], ident[:, :])
                    done.then_inc(n2_xnT, 1)
                    pe.wait_ge(n2_xnT_kept, b + 1)
                    if past:
                        pe.wait_ge(n2_e_rest, b)
                    for u in range(BT):
                        done = t_.matmul(bank[5][:, u * P:(u + 1) * P], rT[:, 3, u * P:(u + 1) * P], flat(we1[:, :, :]),
                                         start=True, stop=True)
                    done.then_inc(n2_e_mm, 1)
                    if left > 1:
                        project(b + 2)

                project(0)
                mix(0)
                project(1)
                batch_rounds(pe, batch)

            @block.scalar
            def _(act):
                def turned(b):
                    act.wait_ge(n2_xT, b + 1)
                    s_.copy(rT[:, 1, :], bank[2][:, :]).then_inc(n2_xT_kept, 1)
                    act.wait_ge(n2_aggT, b + 1)
                    s_.copy(rT[:, 0, :], bank[0][:, :]).then_inc(n2_aggT_kept, 1)

                def projected(b):
                    act.wait_ge(n2_o_mm, b + 1)
                    s_.activation(rT[:, 2, :], bank[1][:, :], ACT.Identity, bias=boc[:, 0:1]).then_inc(n2_o_kept, 1)

                def second_part(b):
                    act.wait_ge(n2_e_rest, b + 1)
                    s_.copy(look[:, tiles(b), EH:2 * EH], tC[:, :, 0:EH]).then_inc(n2_e1, 1)

                def batch(b, past, left):
                    root(act, b, n2_var, n2_std)
                    if left:
                        projected(b + 1)
                    act.wait_ge(n2_xnT, b + 1)
                    s_.copy(rT[:, 3, :], bank[4][:, :]).then_inc(n2_xnT_kept, 1)
                    if past:
                        second_part(b - 1)
                    act.wait_ge(n2_e_mm, b + 1)
                    s_.copy(look[:, tiles(b), 0:EH], halves[:, :, EH:2 * EH]).then_inc(n2_e0, 1)
                    if left > 1:
                        turned(b + 2)

                s_.activation(rs[:, :, H], neg_max[:, 0:NT], ACT.Exp, scale=-1.0, bias=small[:, RING - 1, 1:2]).then_inc(n2_factor, 1)
                turned(0)
                projected(0)
                turned(1)
                batch_rounds(act, batch)
                second_part(NB - 1)

            @block.gpsimd
            def _(pool):
                def stage(b):
                    pool.wait_ge(n2_xT, b)
                    pool.sem_inc(rounds, 1)
                    q_.tensor_copy(tX, xs[:, tiles(b), :]).then_inc(n2_staged, 1)

                def batch(b, past, left):
                    if left > 1:
                        stage(b + 2)
                    pool.wait_ge(n2_xn, b + 1)
                    pool.sem_inc(rounds, 1)
                    q_.tensor_copy(xs[:, tiles(b), :], tN).then_inc(n2_copied, 1)

                pool.sem_inc(n2_copied, 1)
                q_.tensor_copy(tX, xs[:, tiles(0), :]).then_inc(n2_staged, 1)
                stage(1)
                batch_rounds(pool, batch)
                q_.memset(acc[:, :, :], 0.0)

            @block.sync
            def _(sp):
                sp.sem_inc(t2_free, 1)
                with sp.Fori(0, NB) as b:
                    sp.wait_ge(n2_e_kept, b + 1)
                    sp.dma_start(t2.rearrange("(t p) c -> p t c", p=P)[:, tiles(b), :], tT2).then_inc(t2_out, 16)
                    sp.wait_ge(t2_out, 16 * b + 16)
                    sp.sem_inc(t2_free, 1)

        (l2_placed, l2_hot, l2_hotT, l2_hot_kept, l2_half, l2_pre, l2_s1, l2_s1T, l2_s1T_kept, l2_e, l2_s2, l2_dup, l2_cut, l2_keyB,
         l2_same, l2_v, l2_init) = (sem(f"l2_{n}") for n in (
             "placed", "hot", "hotT", "hot_kept", "half", "pre", "silu1", "silu1T", "silu1T_kept", "e", "silu2", "dup", "cut", "keyB",
             "same", "vector", "init"))
        TR, KB, HB, ST, EB, DB = bank[0:6]
        same_tri = tabf[:, 0:G * P]
        s1T = tabf[0:EH + 1, G * P:2 * G * P]
        W4 = G * EH
        with nc.Block() as block:
            def cut(g):
                return wide[:, g, :, :].rearrange("p u c -> p (u c)")[:, 0:W4]

            def silu2(g):
                return wide[:, g, :, :].rearrange("p u c -> p (u c)")[:, W4:2 * W4]

            @block.gpsimd
            def _(pool):
                def step(i, g, past, left):
                    k = i * RING + g
                    if left == RING:
                        gather(pool, k + RING, g, t2, EH, l2_placed, t2_out)
                    for u in range(G if past else 0):
                        pool.wait_ge(scattered[u], 16 * k)
                    pool.wait_ge(l2_cut, k + 1)
                    pool.sem_inc(rounds, 1)
                    for u in range(G):
                        q_.indirect_dma_start(mlp_sum[u], bass.IndirectOffsetOnAxis(ap=put_i[:, g, u:u + 1].bitcast(U32), axis=0),
                                              cut(g)[:, u * EH:(u + 1) * EH], None, compute_op=ALU.add).then_inc(scattered[u], 16)

                pool.wait_ge(sums_zeroed, 16 * G)
                for k in range(RING):
                    gather(pool, k, k, t2, EH, l2_placed, t2_out)
                edge_rounds(pool, step)
                for u in range(G):
                    pool.wait_ge(scattered[u], 16 * GROUPS)

            @block.scalar
            def _(act):
                columns = ((rel_now, rel), (key_now, key))

                def keep_hot(i, g):
                    act.wait_ge(l2_hotT, i * RING + g + 1)
                    s_.copy(hotT[:, g, :], TR[:, :].bitcast(BF16)[:, 0:G * P]).then_inc(l2_hot_kept, 1)

                def step(i, g, past, left):
                    k = i * RING + g
                    act.wait_ge(l2_pre, k + 1)
                    s_.activation(junk[:, g % 2, 0:W4], junk[:, g % 2, W4:2 * W4], ACT.Silu).then_inc(l2_s1, 1)
                    act.wait_ge(l2_s1T, k + 1)
                    s_.copy(s1T[0:EH, :], ST[0:EH, :]).then_inc(l2_s1T_kept, 1)
                    place(k + RING, g, l2_placed, *columns)
                    if left:
                        keep_hot(*later(i, g, 1))
                    act.wait_ge(l2_e, k + 1)
                    s_.activation(silu2(g), EB[:, 0:W4], ACT.Silu).then_inc(l2_s2, 1)

                for k in range(RING):
                    place(k, k, l2_placed, *columns)
                keep_hot(0, 0)
                edge_rounds(act, step)

            @block.tensor
            def _(pe):
                regs = node_regs(pe, "l2_half")

                def spread_keys(i, g):
                    k = i * RING + g
                    pe.wait_ge(l2_placed, k + 1)
                    for u in range(G):
                        last = t_.matmul(KB[:, u * P:(u + 1) * P], key_now[:, g * G + u:g * G + u + 1].to_broadcast([P, P]),
                                         ident[:, :], start=True, stop=True)
                    last.then_inc(l2_keyB, 1)

                def turn(i, g):
                    pe.wait_ge(l2_hot, i * RING + g + 1)
                    for u in range(G):
                        last = t_.transpose(TR[:, :].bitcast(BF16)[:, u * P:(u + 1) * P], hot[:, g, u, :], ident_b[:, :])
                    last.then_inc(l2_hotT, 1)

                def half(i, g):
                    load_nodes(pe, regs, i * RING + g, g)
                    nodes = nodes_of(pe, regs, g)
                    pe.wait_ge(l2_hot_kept, i * RING + g + 1)
                    for u in range(G):
                        for c in range(3):
                            last = t_.matmul(HB[:, u * EH:(u + 1) * EH], hotT[:, g, u * P:(u + 1) * P],
                                             flat(look[:, bass.ds(nodes[u], 1), c * EH:(c + 1) * EH]), start=(c == 0), stop=(c == 2))
                    last.then_inc(l2_half, 1)

                def same_sums(i, g):
                    pe.wait_ge(l2_s2, i * RING + g + 1)
                    pe.wait_ge(l2_same, i * RING + g + 1)
                    for u in range(G):
                        last = t_.matmul(DB[:, u * EH:(u + 1) * EH], hotf[:, g, u, :], silu2(g)[:, u * EH:(u + 1) * EH], start=True, stop=True)
                    last.then_inc(l2_dup, 1)

                def step(i, g, past, left):
                    k = i * RING + g
                    pe.wait_ge(l2_s1, k + 1)
                    pe.sem_inc(rounds, 1)
                    for u in range(G):
                        last = t_.transpose(ST[0:EH, u * P:(u + 1) * P], junk[:, g % 2, u * EH:(u + 1) * EH], ident[:, :])
                    last.then_inc(l2_s1T, 1)
                    if past:
                        same_sums(*later(i, g, -1))
                    if left:
                        turn(*later(i, g, 1))
                    pe.wait_ge(l2_s1T_kept, k + 1)
                    for u in range(G):
                        last = t_.matmul(EB[:, u * EH:(u + 1) * EH], s1T[:, u * P:(u + 1) * P], we2[:, :], start=True, stop=True)
                    last.then_inc(l2_e, 1)
                    if left:
                        half(*later(i, g, 1))
                    if left > 1:
                        pe.wait_ge(l2_same, k + 2)
                        spread_keys(*later(i, g, 2))

                spread_keys(0, 0)
                turn(0, 0)
                half(0, 0)
                pe.wait_ge(l2_same, 1)
                spread_keys(0, 1)
                edge_rounds(pe, step)
                pe.wait_ge(l2_cut, GROUPS - 1)
                same_sums(ITERS - 1, RING - 1)

            @block.vector
            def _(dve):
                L2 = 7

                def one_hot(i, g):
                    dve.wait_ge(l2_placed, i * RING + g + 1)
                    v.tensor_tensor(out=hot[:, g, :, :], **hots(g)).then_inc(l2_hot, 1)

                def duplicates(i, g):
                    k = i * RING + g
                    ch = Chain(dve, l2_v, L2 * k)
                    keys_g = key_now[:, g * G:(g + 1) * G]
                    dve.wait_ge(l2_keyB, k + 1)
                    v.tensor_tensor(out=hotf[:, g, :, :], in0=KB[:, :].rearrange("p (u e) -> p u e", u=G),
                                    in1=keys_g.unsqueeze(2).to_broadcast([P, G, P]), op=ALU.is_equal).then_inc(l2_same, 1)
                    dve.wait_ge(l2_same, k + 1)
                    ch(v.tensor_tensor(out=same_tri.rearrange("p (u e) -> p u e", u=G), in0=hotf[:, g, :, :],
                                       in1=tri[:, :].unsqueeze(1).to_broadcast([P, G, P]), op=ALU.mult))
                    ch.wait()
                    s = [small[:, g, j * G:(j + 1) * G] for j in range(5)]
                    ch(v.tensor_reduce(out=s[0], in_=same_tri.rearrange("p (u e) -> p u e", u=G), axis=AX.X, op=ALU.add))
                    ch(v.tensor_scalar(out=s[2], in0=keys_g, scalar1=far[:, 1:2], scalar2=None, op0=ALU.subtract))
                    ch.wait()
                    ch(v.tensor_scalar(out=s[1], in0=s[0], scalar1=0.5, scalar2=None, op0=ALU.is_lt))
                    ch.wait()
                    ch(v.scalar_tensor_tensor(out=s[3], in0=keys_g, scalar=float(FAR), in1=s[1], op0=ALU.is_lt, op1=ALU.mult))
                    ch.wait()
                    ch(v.tensor_tensor(out=s[4], in0=s[2], in1=s[3], op=ALU.mult))
                    ch.wait()
                    ch(v.tensor_scalar(out=put_i[:, g, :], in0=s[4], scalar1=far[:, 1:2], scalar2=None, op0=ALU.add))
                    assert ch.n == L2, ch.n

                def keep_cut(i, g):
                    dve.wait_ge(l2_dup, i * RING + g + 1)
                    v.tensor_copy(cut(g), DB[:, 0:W4]).then_inc(l2_cut, 1)

                def step(i, g, past, left):
                    k = i * RING + g
                    if past >= RING - 1:
                        for u in range(G):
                            dve.wait_ge(scattered[u], 16 * k - 32)
                    arrived(dve, i, g)
                    dve.wait_ge(l2_half, k + 1)
                    v.tensor_tensor(out=junk[:, g % 2, W4:2 * W4].rearrange("p (u f) -> p u f", u=G),
                                    in0=HB[:, 0:W4].rearrange("p (u f) -> p u f", u=G), in1=ring[:, g * G:(g + 1) * G, 0:EH],
                                    op=ALU.add).then_inc(l2_pre, 1)
                    if left:
                        one_hot(*later(i, g, 1))
                        duplicates(*later(i, g, 1))
                    if past:
                        keep_cut(*later(i, g, -1))

                v.memset(tabf[EH:EH + 1, G * P:2 * G * P], 1.0).then_inc(l2_init, 1)
                one_hot(0, 0)
                duplicates(0, 0)
                edge_rounds(dve, step)
                keep_cut(ITERS - 1, RING - 1)
        gcount[0] += ITERS

        (n3_staged, n3_in, n3_pair, n3_sum, n3_xT, n3_sumT, n3_xT_kept, n3_sumT_kept, n3_h_mm, n3_h_kept, n3_mm, n3_mixed, n3_y,
         n3_y_kept, n3_var, n3_stats, n3_std, n3_centred, n3_xn, n3_xnT, n3_xnT_kept, n3_t_mm, n3_t_kept, t3_out, n3_copied, n3_v) = (
            sem(f"n3_{n}") for n in (
             "staged", "in", "pair", "sum", "xT", "sumT", "xT_kept", "sumT_kept", "h_mm", "h_kept", "mm", "mixed", "y",
             "y_kept", "var", "stats", "std", "centred", "xn", "xnT", "xnT_kept", "t_mm", "t_kept", "t3_out", "copied", "vector"))
        mean, std = rs[:, :, 0:1], rs[:, :, 2:3]
        with nc.Block() as block:
            @block.sync
            def _(sp):
                def load(b):
                    for u in range(G):
                        by_partition = mlp_sum[u][0:NP, :].rearrange("(r t) f -> r (t f)", t=BT)
                        sp.dma_start(flat(tS[:, u, :, :]), by_partition[bass.ds(b * P, P), :]).then_inc(n3_in, 16)

                load(0)
                with sp.Fori(1, NB) as b:
                    sp.wait_ge(n3_sum, b)
                    load(b)
                with sp.Fori(0, NB) as b:
                    sp.wait_ge(n3_t_kept, b + 1)
                    sp.dma_start(t3.rearrange("(t p) c -> p t c", p=P)[:, tiles(b), :], tab[:, tiles(b), 0:D]).then_inc(t3_out, 16)
                sp.wait_ge(t3_out, 16 * NB)

            @block.vector
            def _(dve):
                def front(b, before=True):
                    if before:
                        dve.wait_ge(n3_sumT, b)
                    dve.wait_ge(n3_in, 16 * G * b + 16 * G)
                    v.tensor_add(tB[:, :, 0:EH], tS[:, 0, :, :], tS[:, 1, :, :])
                    v.tensor_add(tC[:, :, 0:EH], tS[:, 2, :, :], tS[:, 3, :, :]).then_inc(n3_pair, 1)
                    dve.wait_ge(n3_pair, b + 1)
                    v.tensor_add(tB[:, :, 0:EH], tB[:, :, 0:EH], tC[:, :, 0:EH]).then_inc(n3_sum, 1)

                def mlp(b, past, left):
                    ch = Chain(dve, n3_v, BT * b)
                    if left > 1:
                        front(b + 2)
                    dve.wait_ge(n3_mm, b + 1)
                    v.tensor_tensor(out=tA, in0=bank[3][:, :].rearrange("p (t d) -> p t d", t=BT),
                                    in1=bn2b[:, :].unsqueeze(1).to_broadcast([P, BT, D]), op=ALU.add).then_inc(n3_mixed, 1)
                    if past:
                        dve.wait_ge(n3_y_kept, b)
                    dve.wait_ge(n3_mixed, b + 1)
                    v.scalar_tensor_tensor(out=tY, in0=xs[:, tiles(b), :], scalar=2.0, in1=tA, op0=ALU.mult, op1=ALU.add).then_inc(n3_y, 1)
                    dve.wait_ge(n3_y, b + 1)
                    norm_stats(ch, tY, n3_var)
                    dve.wait_ge(n3_var, b + 1)
                    v.tensor_copy(rs[:, tiles(b), 0:2], mv[:, :, :]).then_inc(n3_stats, 1)

                def normalized(b, past=True):
                    dve.wait_ge(n3_y_kept, b + 1)
                    if past:
                        dve.wait_ge(n3_xn, b)
                    v.tensor_tensor(out=tA, in0=tab[:, tiles(b), 0:D], in1=mean[:, tiles(b), :].to_broadcast([P, BT, D]),
                                    op=ALU.subtract).then_inc(n3_centred, 1)
                    if past:
                        dve.wait_ge(n3_copied, b)
                        dve.wait_ge(n3_xnT, b)
                    dve.wait_ge(n3_centred, b + 1)
                    v.tensor_tensor(out=tN, in0=tA, in1=std[:, tiles(b), :].to_broadcast([P, BT, D]), op=ALU.mult).then_inc(n3_xn, 1)

                def table(b, past, left):
                    if left:
                        normalized(b + 1)
                    dve.wait_ge(n3_t_mm, b + 1)
                    v.tensor_tensor(out=tab[:, tiles(b), 0:D], in0=bank[5][:, :].rearrange("p (t d) -> p t d", t=BT),
                                    in1=dis[:, tiles(b)].unsqueeze(2).to_broadcast([P, BT, D]), op=ALU.mult).then_inc(n3_t_kept, 1)

                front(0, False)
                front(1)
                batch_rounds(dve, mlp)
                dve.wait_ge(n3_std, 1)
                v.reciprocal(rs[:, :, 2], rs[:, :, 2]).then_inc(n3_std, 1)
                dve.wait_ge(n3_std, 2)
                normalized(0, False)
                batch_rounds(dve, table)

            @block.tensor
            def _(pe):
                def hidden(b, before=True):
                    pe.wait_ge(n3_staged, b + 1)
                    for u in range(BT):
                        last = t_.transpose(bank[1][:, u * P:(u + 1) * P], tX[:, u, :], ident[:, :])
                    last.then_inc(n3_xT, 1)
                    pe.wait_ge(n3_sum, b + 1)
                    pe.sem_inc(rounds, 1)
                    for u in range(BT):
                        last = t_.transpose(bank[0][0:EH, u * P:(u + 1) * P], tB[:, u, 0:EH], ident[:, :])
                    last.then_inc(n3_sumT, 1)
                    if before:
                        pe.wait_ge(n3_h_kept, b)
                    pe.wait_ge(n3_xT_kept, b + 1)
                    t_.matmul(bank[2][:, :], wn1[:, 0, :], rT[:, 1, :], start=True, stop=False)
                    pe.wait_ge(n3_sumT_kept, b + 1)
                    t_.matmul(bank[2][:, :], wn1[0:EH, 1, :], rT[0:EH, 0, :], start=False, stop=True).then_inc(n3_h_mm, 1)

                def mlp(b, past, left):
                    if left:
                        hidden(b + 1)
                    pe.wait_ge(n3_h_kept, b + 1)
                    if past:
                        pe.wait_ge(n3_mixed, b)
                    for u in range(BT):
                        last = t_.matmul(bank[3][:, u * P:(u + 1) * P], rT[:, 2, u * P:(u + 1) * P], wn2[:, :], start=True, stop=True)
                    last.then_inc(n3_mm, 1)

                def table(b, past, left):
                    pe.wait_ge(n3_xn, b + 1)
                    for u in range(BT):
                        done = t_.transpose(bank[4][:, u * P:(u + 1) * P], tN[:, u, :], ident[:, :])
                    done.then_inc(n3_xnT, 1)
                    pe.wait_ge(n3_xnT_kept, b + 1)
                    if past:
                        pe.wait_ge(n3_t_kept, b)
                    for u in range(BT):
                        done = t_.matmul(bank[5][:, u * P:(u + 1) * P], rT[:, 3, u * P:(u + 1) * P], wg1[:, :], start=True, stop=True)
                    done.then_inc(n3_t_mm, 1)

                hidden(0, False)
                batch_rounds(pe, mlp)
                batch_rounds(pe, table)

            @block.scalar
            def _(act):
                def mlp(b, past, left):
                    act.wait_ge(n3_xT, b + 1)
                    s_.copy(rT[:, 1, :], bank[1][:, :]).then_inc(n3_xT_kept, 1)
                    act.wait_ge(n3_sumT, b + 1)
                    s_.copy(rT[0:EH, 0, :], bank[0][0:EH, :]).then_inc(n3_sumT_kept, 1)
                    if past:
                        act.wait_ge(n3_mm, b)
                    act.wait_ge(n3_h_mm, b + 1)
                    s_.activation(rT[:, 2, :], bank[2][:, :], ACT.Silu, bias=bn1c[:, 0:1]).then_inc(n3_h_kept, 1)

                batch_rounds(act, mlp)
                act.wait_ge(n3_stats, NB)
                s_.activation(rs[:, :, 2], rs[:, :, 1], ACT.Sqrt, bias=eps[:, 0:1]).then_inc(n3_std, 1)
                with act.Fori(0, NB) as b:
                    act.wait_ge(n3_xnT, b + 1)
                    s_.copy(rT[:, 3, :], bank[4][:, :]).then_inc(n3_xnT_kept, 1)

            @block.gpsimd
            def _(pool):
                def stage(b):
                    pool.wait_ge(n3_xT, b)
                    pool.sem_inc(rounds, 1)
                    q_.tensor_copy(tX, xs[:, tiles(b), :]).then_inc(n3_staged, 1)

                def mlp(b, past, left):
                    if left > 1:
                        stage(b + 2)
                    pool.wait_ge(n3_y, b + 1)
                    pool.sem_inc(rounds, 1)
                    q_.tensor_copy(tab[:, tiles(b), 0:D], tY).then_inc(n3_y_kept, 1)

                q_.tensor_copy(tX, xs[:, tiles(0), :]).then_inc(n3_staged, 1)
                stage(1)
                batch_rounds(pool, mlp)
                with pool.Fori(0, NB) as b:
                    pool.wait_ge(n3_xn, b + 1)
                    pool.sem_inc(rounds, 1)
                    q_.tensor_copy(xs[:, tiles(b), :], tN).then_inc(n3_copied, 1)

        def convolution(name, table, table_out):
            placed, hot_made, summed, added = (sem(f"{name}_{n}") for n in ("placed", "hot", "sum", "acc"))
            with nc.Block() as block:
                @block.gpsimd
                def _(pool):
                    with pool.Fori(0, ITERS) as i:
                        for g in range(RING):
                            gather(pool, i * RING + g, g, table, D, placed, table_out)

                @block.scalar
                def _(act):
                    for k in range(RING):
                        place(k, k, placed, (rel_now, rel), (ew_now, ew))
                    with act.Fori(0, ITERS) as i:
                        for g in range(RING):
                            k = i * RING + g
                            act.wait_ge(summed, k + 1)
                            place(k + RING, g, placed, (rel_now, rel), (ew_now, ew))

                @block.tensor
                def _(pe):
                    with pe.Fori(0, ITERS) as i:
                        for g in range(RING):
                            k = i * RING + g
                            pe.wait_ge(hot_made, k + 1)
                            pe.wait_ge(added, k * G + G)
                            arrived(pe, i, g)
                            for u in range(G):
                                last = t_.matmul(bank[g][:, u * P:(u + 1) * P], hotf[:, g, u, :], ring[:, g * G + u, 0:D],
                                                 start=True, stop=True)
                            last.then_inc(summed, 1)

                @block.vector
                def _(dve):
                    regs = node_regs(dve, f"{name}_node")

                    def front(i, g):
                        dve.wait_ge(placed, i * RING + g + 1)
                        for u in range(G):
                            at = slice(g * G + u, g * G + u + 1)
                            last = v.tensor_scalar(out=hotf[:, g, u, :], in0=iota[:, :], scalar1=rel_now[:, at], scalar2=ew_now[:, at],
                                                   op0=ALU.is_equal, op1=ALU.mult)
                        last.then_inc(hot_made, 1)

                    def back(i, g):
                        k = i * RING + g
                        load_nodes(dve, regs, k, g)
                        nodes = nodes_of(dve, regs, g)
                        dve.wait_ge(summed, k + 1)
                        for u in range(G):
                            here = flat(acc[:, bass.ds(nodes[u], 1), 0:D])
                            dve.wait_ge(added, k * G + RING * G + u)
                            v.tensor_add(here, here, bank[g][:, u * P:(u + 1) * P]).then_inc(added, 1)

                    def both(i, g, past, left):
                        if left:
                            front(*later(i, g, 1))
                        back(i, g)

                    dve.sem_inc(added, RING * G)
                    front(0, 0)
                    edge_rounds(dve, both)
            gcount[0] += ITERS

        convolution("c1", t3, t3_out)

        n4_own, n4_r, n4_rT, n4_rT_kept, n4_mm, n4_kept, t4_out = (
            sem(f"n4_{n}") for n in ("own", "sum", "sumT", "reluT_kept", "mm", "kept", "t4_out"))
        with nc.Block() as block:
            @block.vector
            def _(dve):
                def spread(b):
                    return dis[:, tiles(b)].unsqueeze(2).to_broadcast([P, BT, D])

                def front(b):
                    v.tensor_add(tA, acc[:, tiles(b), 0:D], tab[:, tiles(b), 0:D]).then_inc(n4_own, 1)
                    dve.wait_ge(n4_own, b + 1)
                    v.tensor_tensor(out=tB, in0=tA, in1=spread(b), op=ALU.mult).then_inc(n4_r, 1)

                def batch(b, past, left):
                    if left:
                        dve.wait_ge(n4_rT, b + 1)
                        front(b + 1)
                    dve.wait_ge(n4_mm, b + 1)
                    v.tensor_tensor(out=tab[:, tiles(b), 0:D], in0=bank[1][:, :].rearrange("p (t d) -> p t d", t=BT),
                                    in1=spread(b), op=ALU.mult).then_inc(n4_kept, 1)

                front(0)
                batch_rounds(dve, batch)

            @block.tensor
            def _(pe):
                with pe.Fori(0, NB) as b:
                    pe.wait_ge(n4_r, b + 1)
                    for u in range(BT):
                        last = t_.transpose(bank[0][:, u * P:(u + 1) * P], tB[:, u, :], ident[:, :])
                    last.then_inc(n4_rT, 1)
                    pe.wait_ge(n4_rT_kept, b + 1)
                    pe.wait_ge(n4_kept, b + 1)
                    for u in range(BT):
                        last = t_.matmul(bank[1][:, u * P:(u + 1) * P], rT[:, 0, u * P:(u + 1) * P], wg2[:, :], start=True, stop=True)
                    last.then_inc(n4_mm, 1)

            @block.scalar
            def _(act):
                with act.Fori(0, NB) as b:
                    act.wait_ge(n4_rT, b + 1)
                    s_.activation(rT[:, 0, :], bank[0][:, :], ACT.Relu, bias=bg1c[:, 0:1]).then_inc(n4_rT_kept, 1)

            @block.gpsimd
            def _(pool):
                pool.wait_ge(n4_own, NB)
                q_.memset(acc[:, :, :], 0.0)

            @block.sync
            def _(sp):
                sp.sem_inc(n4_kept, 1)
                with sp.Fori(0, NB) as b:
                    sp.wait_ge(n4_kept, b + 2)
                    sp.dma_start(t4.rearrange("(t p) c -> p t c", p=P)[:, tiles(b), :], tab[:, tiles(b), 0:D]).then_inc(t4_out, 16)
                sp.wait_ge(t4_out, 16 * NB)

        convolution("c2", t4, t4_out)

        n5_c, n5_own, n5_var, n5_std, n5_done, n5_out, n5_v = (sem(f"n5_{n}") for n in ("c", "own", "var", "std", "done", "out", "vector"))
        N5 = 2 + NORM
        with nc.Block() as block:
            @block.vector
            def _(dve):
                def front(b):
                    v.tensor_add(tA, acc[:, tiles(b), 0:D], tab[:, tiles(b), 0:D]).then_inc(n5_own, 1)

                def batch(b, past, left):
                    ch = Chain(dve, n5_v, N5 * b)
                    dve.wait_ge(n5_own, b + 1)
                    ch(v.tensor_tensor(out=tB, in0=tA, in1=dis[:, tiles(b)].unsqueeze(2).to_broadcast([P, BT, D]), op=ALU.mult))
                    dve.wait_ge(n5_c, b + 1)
                    if past:
                        dve.wait_ge(n5_done, b)
                    ch.wait()
                    ch(v.tensor_add(tY, tB, tC))
                    ch.wait()
                    norm_stats(ch, tY, n5_var)
                    if left:
                        front(b + 1)
                    normalize(ch, b, tY, [flat(tab[:, bass.ds(b * BT + u, 1), 0:D]) for u in range(BT)], n5_std).then_inc(n5_done, 1)
                    assert ch.n == N5

                front(0)
                batch_rounds(dve, batch)

            @block.scalar
            def _(act):
                with act.Fori(0, NB) as b:
                    root(act, b, n5_var, n5_std)

            @block.gpsimd
            def _(pool):
                def front(b):
                    q_.tensor_tensor(out=tC, in0=xs[:, tiles(b), :], in1=bg2[:, :].unsqueeze(1).to_broadcast([P, BT, D]),
                                     op=ALU.add).then_inc(n5_c, 1)

                def batch(b, past, left):
                    if left:
                        pool.wait_ge(n5_var, b + 1)
                        pool.sem_inc(rounds, 1)
                        front(b + 1)

                front(0)
                batch_rounds(pool, batch)

            @block.sync
            def _(sp):
                with sp.Fori(0, NB) as b:
                    sp.wait_ge(n5_done, b + 1)
                    sp.dma_start(out.rearrange("(t p) c -> p t c", p=P)[:, tiles(b), :], tab[:, tiles(b), 0:D]).then_inc(n5_out, 16)
                sp.wait_ge(n5_out, 16 * NB)


_WEIGHTS = ["L0_gnn_W_att_w", "L0_gnn_W_att_b", "L0_gnn_W1_w", "L0_gnn_W1_b", "L0_gnn_W2_w", "L0_gnn_W2_b", "L0_gnn_a",
            "L1_gnn_Wq", "L1_gnn_Wk", "L1_gnn_Wv", "L1_gnn_We", "L1_gnn_Wo", "L1_gnn_bo", "L1_gnn_Wm", "L1_gnn_bm",
            "L2_gnn_We1", "L2_gnn_be1", "L2_gnn_We2", "L2_gnn_be2", "L2_gnn_Wn1", "L2_gnn_bn1", "L2_gnn_Wn2", "L2_gnn_bn2",
            "L3_gnn_W1", "L3_gnn_b1", "L3_gnn_W2", "L3_gnn_b2"]


def kernel(**inputs):
    import numpy as _np
    import concourse.bacc as _bacc
    from concourse import mybir as _mybir
    from concourse.bass_utils import run_bass_kernel_spmd as _run

    a = {k: _np.asarray(v) for k, v in inputs.items()}

    def tiled(v, fill):
        padded = _np.full(ET * P, fill, v.dtype)
        padded[:E] = v
        return padded.reshape(ET, P)

    arrays = {"x": _np.concatenate([a["x"], _np.zeros((NP - N, D), a["x"].dtype)]),
              "edge_i": _np.concatenate([tiled(a["src"], 0), tiled(a["dst"], PAD_DST)], axis=1),
              "edge_f": _np.concatenate([tiled(a["edge_weight"], 0)] + [tiled(a["edge_attr_3"][:, c], 0) for c in range(3)], axis=1)}
    arrays.update({w: a[w] for w in _WEIGHTS})
    arrays = {f"in_{k}": _np.ascontiguousarray(v) for k, v in arrays.items()}
    nc = _bacc.Bacc("TRN2", target_bir_lowering=False, num_devices=1)
    args = [nc.dram_tensor(k, v.shape, _mybir.dt.from_np(v.dtype), kind="ExternalInput").ap() for k, v in arrays.items()]
    out = nc.dram_tensor("out_nodes", (NP, D), F32, kind="ExternalOutput").ap()
    build(nc, *args, out)
    r = _run(nc, [arrays], core_ids=[0])
    return r.results[0]["out_nodes"][:N]
```
